# Optimizing a Trainium2 kernel written in Bass

```python
import numpy as np
import jax
import jax.numpy as jnp

def _softmax(x, axis=-1):
    return jax.nn.softmax(x, axis=axis)

def _gelu(x):
    return jax.nn.gelu(x, approximate=True)

def _silu(x):
    return jax.nn.silu(x)

def _sigmoid(x):
    return jax.nn.sigmoid(x)

def _layernorm(x, axis=-1, eps=1e-05):
    m = jnp.mean(x, axis=axis, keepdims=True)
    v = jnp.var(x, axis=axis, keepdims=True)
    return (x - m) / jnp.sqrt(v + eps)

def _scatter_add(tgt, idx, src, axis=0):
    return tgt.at[idx].add(src)

def _segment_sum(src, seg, n):
    return jax.ops.segment_sum(src, seg, n)
kernel_name = 'mk_gnn_preln_d2_gnn_r32_3608f6'

def setup_inputs(seed: int=0):
    np.random.seed(seed)
    _w = jnp.asarray

    def _rec_inputs():
        import jax
        import jax.numpy as jnp
        _gk = jax.random.key(seed)
        x = -0.000202 + 1 * jax.random.normal(jax.random.fold_in(_gk, 1), (3125, 128), jnp.float32)
        _s = jax.random.randint(jax.random.fold_in(_gk, 2), (25000,), 0, 3125, jnp.int32)
        _d = jax.random.randint(jax.random.fold_in(_gk, 3), (25000,), 0, 3125, jnp.int32)
        _loop = jnp.arange(3125, dtype=jnp.int32)
        src = jnp.concatenate([_s, _d, _loop])
        dst = jnp.concatenate([_d, _s, _loop])
        _o = jnp.argsort(dst, stable=True)
        src = src[_o]
        dst = dst[_o]
        edge_type_8 = jax.random.randint(jax.random.fold_in(_gk, 12), (53125,), 0, 8, jnp.int32)
        edge_weight = jax.random.uniform(jax.random.fold_in(_gk, 13), (53125,), jnp.float32, 0.0, 1)
        node_type_4 = jax.random.randint(jax.random.fold_in(_gk, 14), (3125,), 0, 4, jnp.int32)
        return (x, src, dst, edge_type_8, edge_weight, node_type_4)
    x, src, dst, edge_type_8, edge_weight, node_type_4 = _rec_inputs()

    def _L0_gnn_setup():
        import jax, jax.numpy as jnp
        import numpy as np
        import math
        HIDDEN = 128
        N_NODES = 50000
        N_EDGES = 25000
        N_NTYPES = 4
        N_ETYPES = 8

        def _type_matmul(h, W, types):
            out = jnp.zeros_like(h)
            for t in range(W.shape[0]):
                out = out + jnp.where((types == t)[:, None], h @ W[t], 0.0)
            return out

        def _sparse_softmax(scores, indices, n_segments):
            seg_max = jnp.maximum(jax.ops.segment_max(scores, indices, num_segments=n_segments), -1000000000.0)
            exp_s = jnp.exp(scores - seg_max[indices])
            seg_sum = jax.ops.segment_sum(exp_s, indices, num_segments=n_segments)
            return exp_s / (seg_sum[indices] + 1e-10)
        key = jax.random.key(seed)
        ks = jax.random.split(key, 10)
        x = jax.random.normal(ks[0], (N_NODES, HIDDEN), dtype=jnp.float32)
        edge_index = jax.random.randint(ks[1], (2, N_EDGES), 0, N_NODES, dtype=jnp.int64 if jax.config.read('jax_enable_x64') else jnp.int32)
        edge_type = jax.random.randint(ks[2], (N_EDGES,), 0, N_ETYPES, dtype=jnp.int32)
        node_type = jax.random.randint(ks[3], (N_NODES,), 0, N_NTYPES, dtype=jnp.int32)
        W_Q = jax.random.normal(ks[4], (N_NTYPES, HIDDEN, HIDDEN), dtype=jnp.float32) * 0.02
        W_K = jax.random.normal(ks[5], (N_NTYPES, HIDDEN, HIDDEN), dtype=jnp.float32) * 0.02
        W_V = jax.random.normal(ks[6], (N_NTYPES, HIDDEN, HIDDEN), dtype=jnp.float32) * 0.02
        W_edge = jax.random.normal(ks[7], (N_ETYPES, HIDDEN, HIDDEN), dtype=jnp.float32) * 0.02
        mu = jnp.ones((N_ETYPES,), dtype=jnp.float32)
        return {'x': x, 'edge_index': edge_index, 'edge_type': edge_type, 'node_type': node_type, 'W_Q': W_Q, 'W_K': W_K, 'W_V': W_V, 'W_edge': W_edge, 'mu': mu}
    _L0_gnn_all = _L0_gnn_setup()
    _L0_gnn_in = {k: v for k, v in _L0_gnn_all.items() if k in ('W_Q', 'W_K', 'W_V', 'W_edge', 'mu')}
    del _L0_gnn_all

    def _L1_gnn_setup():
        import jax, jax.numpy as jnp
        import numpy as np
        N, F_IN, H, HEADS = (50000, 128, 128, 4)
        C = H // HEADS
        E = 25000

        def layer_norm(x, w, b, eps=1e-05):
            mu = x.mean(-1, keepdims=True)
            var = ((x - mu) ** 2).mean(-1, keepdims=True)
            return (x - mu) * jax.lax.rsqrt(var + eps) * w + b

        def gat_conv(x, src, dst, edge_attr, W, att_src, att_dst, W_edge, att_edge, bias):
            n = x.shape[0]
            ones = jnp.ones((src.shape[0],), dtype=edge_attr.dtype)
            deg = jax.ops.segment_sum(ones, dst, n)
            loop_attr = jax.ops.segment_sum(edge_attr, dst, n) / jnp.maximum(deg, 1.0)[:, None]
            loop = jnp.arange(n, dtype=src.dtype)
            src = jnp.concatenate([src, loop])
            dst = jnp.concatenate([dst, loop])
            ea = jnp.concatenate([edge_attr, loop_attr], axis=0)
            h = (x @ W).reshape(n, HEADS, C)
            a_src = (h * att_src).sum(-1)
            a_dst = (h * att_dst).sum(-1)
            e = (ea @ W_edge).reshape(-1, HEADS, C)
            a_edge = (e * att_edge).sum(-1)
            alpha = jax.nn.leaky_relu(a_src[src] + a_dst[dst] + a_edge, 0.2)
            m = jax.lax.stop_gradient(jax.ops.segment_max(alpha, dst, n))
            alpha = jnp.exp(alpha - m[dst])
            s = jax.ops.segment_sum(alpha, dst, n)
            alpha = alpha / (s[dst] + 1e-16)
            out = jax.ops.segment_sum(alpha[:, :, None] * h[src], dst, n)
            return out.reshape(n, H) + bias
        key = jax.random.key(seed)
        ks = iter(jax.random.split(key, 40))

        def lin(k, i, o, s=0.05):
            return jax.random.normal(k, (i, o), jnp.float32) * s
        d = {}
        d['x'] = jax.random.normal(next(ks), (N, F_IN), jnp.float32)
        d['edge_time'] = jax.random.uniform(next(ks), (E,), jnp.float32)
        d['ip_w1'] = lin(next(ks), F_IN, 2 * H)
        d['ip_b1'] = jnp.zeros((2 * H,), jnp.float32)
        d['ip_ln_w'] = jnp.ones((2 * H,), jnp.float32)
        d['ip_ln_b'] = jnp.zeros((2 * H,), jnp.float32)
        d['ip_w2'] = lin(next(ks), 2 * H, H)
        d['ip_b2'] = jnp.zeros((H,), jnp.float32)
        d['pn_w'] = jnp.ones((H,), jnp.float32)
        d['pn_b'] = jnp.zeros((H,), jnp.float32)
        d['ta_w1'] = lin(next(ks), 1, H)
        d['ta_b1'] = jnp.zeros((H,), jnp.float32)
        d['ta_ln_w'] = jnp.ones((H,), jnp.float32)
        d['ta_ln_b'] = jnp.zeros((H,), jnp.float32)
        d['ta_w2'] = lin(next(ks), H, H)
        d['ta_b2'] = jnp.zeros((H,), jnp.float32)
        for p in ('g1', 'g2'):
            d[p + '_w'] = lin(next(ks), H, H)
            d[p + '_att_src'] = jax.random.normal(next(ks), (HEADS, C), jnp.float32) * 0.05
            d[p + '_att_dst'] = jax.random.normal(next(ks), (HEADS, C), jnp.float32) * 0.05
            d[p + '_ew'] = lin(next(ks), H, H)
            d[p + '_att_edge'] = jax.random.normal(next(ks), (HEADS, C), jnp.float32) * 0.05
            d[p + '_b'] = jnp.zeros((H,), jnp.float32)
        d['n1_w'] = jnp.ones((H,), jnp.float32)
        d['n1_b'] = jnp.zeros((H,), jnp.float32)
        d['n2_w'] = jnp.ones((H,), jnp.float32)
        d['n2_b'] = jnp.zeros((H,), jnp.float32)
        d['edge_index'] = jax.random.randint(next(ks), (2, E), 0, N, jnp.int32)
        return d
    _L1_gnn_all = _L1_gnn_setup()
    _L1_gnn_in = {k: v for k, v in _L1_gnn_all.items() if k in ('ip_w1', 'ip_b1', 'ip_ln_w', 'ip_ln_b', 'ip_w2', 'ip_b2', 'pn_w', 'pn_b', 'ta_w1', 'ta_b1', 'ta_ln_w', 'ta_ln_b', 'ta_w2', 'ta_b2', 'g1_w', 'g1_att_src', 'g1_att_dst', 'g1_ew', 'g1_att_edge', 'g1_b', 'g2_w', 'g2_att_src', 'g2_att_dst', 'g2_ew', 'g2_att_edge', 'g2_b', 'n1_w', 'n1_b', 'n2_w', 'n2_b')}
    del _L1_gnn_all
    return {'x': x, 'src': src, 'dst': dst, 'edge_type_8': edge_type_8, 'edge_weight': edge_weight, 'node_type_4': node_type_4, 'L0_gnn_W_Q': _L0_gnn_in['W_Q'], 'L0_gnn_W_K': _L0_gnn_in['W_K'], 'L0_gnn_W_V': _L0_gnn_in['W_V'], 'L0_gnn_W_edge': _L0_gnn_in['W_edge'], 'L0_gnn_mu': _L0_gnn_in['mu'], 'L1_gnn_ip_w1': _L1_gnn_in['ip_w1'], 'L1_gnn_ip_b1': _L1_gnn_in['ip_b1'], 'L1_gnn_ip_ln_w': _L1_gnn_in['ip_ln_w'], 'L1_gnn_ip_ln_b': _L1_gnn_in['ip_ln_b'], 'L1_gnn_ip_w2': _L1_gnn_in['ip_w2'], 'L1_gnn_ip_b2': _L1_gnn_in['ip_b2'], 'L1_gnn_pn_w': _L1_gnn_in['pn_w'], 'L1_gnn_pn_b': _L1_gnn_in['pn_b'], 'L1_gnn_ta_w1': _L1_gnn_in['ta_w1'], 'L1_gnn_ta_b1': _L1_gnn_in['ta_b1'], 'L1_gnn_ta_ln_w': _L1_gnn_in['ta_ln_w'], 'L1_gnn_ta_ln_b': _L1_gnn_in['ta_ln_b'], 'L1_gnn_ta_w2': _L1_gnn_in['ta_w2'], 'L1_gnn_ta_b2': _L1_gnn_in['ta_b2'], 'L1_gnn_g1_w': _L1_gnn_in['g1_w'], 'L1_gnn_g1_att_src': _L1_gnn_in['g1_att_src'], 'L1_gnn_g1_att_dst': _L1_gnn_in['g1_att_dst'], 'L1_gnn_g1_ew': _L1_gnn_in['g1_ew'], 'L1_gnn_g1_att_edge': _L1_gnn_in['g1_att_edge'], 'L1_gnn_g1_b': _L1_gnn_in['g1_b'], 'L1_gnn_g2_w': _L1_gnn_in['g2_w'], 'L1_gnn_g2_att_src': _L1_gnn_in['g2_att_src'], 'L1_gnn_g2_att_dst': _L1_gnn_in['g2_att_dst'], 'L1_gnn_g2_ew': _L1_gnn_in['g2_ew'], 'L1_gnn_g2_att_edge': _L1_gnn_in['g2_att_edge'], 'L1_gnn_g2_b': _L1_gnn_in['g2_b'], 'L1_gnn_n1_w': _L1_gnn_in['n1_w'], 'L1_gnn_n1_b': _L1_gnn_in['n1_b'], 'L1_gnn_n2_w': _L1_gnn_in['n2_w'], 'L1_gnn_n2_b': _L1_gnn_in['n2_b']}

def reference(x, src, dst, edge_type_8, edge_weight, node_type_4, L0_gnn_W_Q, L0_gnn_W_K, L0_gnn_W_V, L0_gnn_W_edge, L0_gnn_mu, L1_gnn_ip_w1, L1_gnn_ip_b1, L1_gnn_ip_ln_w, L1_gnn_ip_ln_b, L1_gnn_ip_w2, L1_gnn_ip_b2, L1_gnn_pn_w, L1_gnn_pn_b, L1_gnn_ta_w1, L1_gnn_ta_b1, L1_gnn_ta_ln_w, L1_gnn_ta_ln_b, L1_gnn_ta_w2, L1_gnn_ta_b2, L1_gnn_g1_w, L1_gnn_g1_att_src, L1_gnn_g1_att_dst, L1_gnn_g1_ew, L1_gnn_g1_att_edge, L1_gnn_g1_b, L1_gnn_g2_w, L1_gnn_g2_att_src, L1_gnn_g2_att_dst, L1_gnn_g2_ew, L1_gnn_g2_att_edge, L1_gnn_g2_b, L1_gnn_n1_w, L1_gnn_n1_b, L1_gnn_n2_w, L1_gnn_n2_b):
    import jax
    import jax.numpy as jnp

    def _L0_gnn_ref(x, edge_index, edge_type, node_type, W_Q, W_K, W_V, W_edge, mu):
        import jax, jax.numpy as jnp
        import numpy as np
        import math
        HIDDEN = 128
        N_NODES = 50000
        N_EDGES = 25000
        N_NTYPES = 4
        N_ETYPES = 8

        def _type_matmul(h, W, types):
            out = jnp.zeros_like(h)
            for t in range(W.shape[0]):
                out = out + jnp.where((types == t)[:, None], h @ W[t], 0.0)
            return out

        def _sparse_softmax(scores, indices, n_segments):
            seg_max = jnp.maximum(jax.ops.segment_max(scores, indices, num_segments=n_segments), -1000000000.0)
            exp_s = jnp.exp(scores - seg_max[indices])
            seg_sum = jax.ops.segment_sum(exp_s, indices, num_segments=n_segments)
            return exp_s / (seg_sum[indices] + 1e-10)
        N, d = x.shape
        scale = math.sqrt(d)
        src, dst = (edge_index[0], edge_index[1])
        Q = _type_matmul(x, W_Q, node_type)
        K = _type_matmul(x, W_K, node_type)
        V = _type_matmul(x, W_V, node_type)
        q_dst = Q[dst]
        k_src = K[src]
        k_t = _type_matmul(k_src, W_edge, edge_type)
        scores = jnp.sum(q_dst * k_t, axis=-1) / scale
        scores = scores * mu[edge_type]
        attn = _sparse_softmax(scores, dst, N)
        weighted_v = V[src] * attn[:, None]
        out = jax.ops.segment_sum(weighted_v, dst, num_segments=N)
        return out

    def _L1_gnn_ref(x, edge_time, ip_w1, ip_b1, ip_ln_w, ip_ln_b, ip_w2, ip_b2, pn_w, pn_b, ta_w1, ta_b1, ta_ln_w, ta_ln_b, ta_w2, ta_b2, g1_w, g1_att_src, g1_att_dst, g1_ew, g1_att_edge, g1_b, g2_w, g2_att_src, g2_att_dst, g2_ew, g2_att_edge, g2_b, n1_w, n1_b, n2_w, n2_b, edge_index):
        import jax, jax.numpy as jnp
        import numpy as np
        N, F_IN, H, HEADS = (50000, 128, 128, 4)
        C = H // HEADS
        E = 25000

        def layer_norm(x, w, b, eps=1e-05):
            mu = x.mean(-1, keepdims=True)
            var = ((x - mu) ** 2).mean(-1, keepdims=True)
            return (x - mu) * jax.lax.rsqrt(var + eps) * w + b

        def gat_conv(x, src, dst, edge_attr, W, att_src, att_dst, W_edge, att_edge, bias):
            n = x.shape[0]
            ones = jnp.ones((src.shape[0],), dtype=edge_attr.dtype)
            deg = jax.ops.segment_sum(ones, dst, n)
            loop_attr = jax.ops.segment_sum(edge_attr, dst, n) / jnp.maximum(deg, 1.0)[:, None]
            loop = jnp.arange(n, dtype=src.dtype)
            src = jnp.concatenate([src, loop])
            dst = jnp.concatenate([dst, loop])
            ea = jnp.concatenate([edge_attr, loop_attr], axis=0)
            h = (x @ W).reshape(n, HEADS, C)
            a_src = (h * att_src).sum(-1)
            a_dst = (h * att_dst).sum(-1)
            e = (ea @ W_edge).reshape(-1, HEADS, C)
            a_edge = (e * att_edge).sum(-1)
            alpha = jax.nn.leaky_relu(a_src[src] + a_dst[dst] + a_edge, 0.2)
            m = jax.lax.stop_gradient(jax.ops.segment_max(alpha, dst, n))
            alpha = jnp.exp(alpha - m[dst])
            s = jax.ops.segment_sum(alpha, dst, n)
            alpha = alpha / (s[dst] + 1e-16)
            out = jax.ops.segment_sum(alpha[:, :, None] * h[src], dst, n)
            return out.reshape(n, H) + bias
        src, dst = (edge_index[0], edge_index[1])
        h = jax.nn.relu(x @ ip_w1 + ip_b1)
        h = layer_norm(h, ip_ln_w, ip_ln_b)
        h = h @ ip_w2 + ip_b2
        h = jnp.clip(jax.nn.relu(layer_norm(h, pn_w, pn_b)), -10.0, 10.0)
        tw = edge_time[:, None] @ ta_w1 + ta_b1
        tw = jax.nn.relu(layer_norm(tw, ta_ln_w, ta_ln_b))
        tw = jnp.clip(jnp.tanh(tw @ ta_w2 + ta_b2), -3.0, 3.0)
        g = gat_conv(h, src, dst, tw, g1_w, g1_att_src, g1_att_dst, g1_ew, g1_att_edge, g1_b) + h
        g = jax.nn.elu(layer_norm(jnp.clip(g, -10.0, 10.0), n1_w, n1_b))
        g2 = gat_conv(g, src, dst, tw, g2_w, g2_att_src, g2_att_dst, g2_ew, g2_att_edge, g2_b) + g
        return jax.nn.elu(layer_norm(jnp.clip(g2, -10.0, 10.0), n2_w, n2_b))
    edge_index = jnp.stack([src, dst])
    h = jnp.maximum(_layernorm(x, axis=-1), 0.0)
    x = x + _L0_gnn_ref(h, edge_index, edge_type_8, node_type_4, L0_gnn_W_Q, L0_gnn_W_K, L0_gnn_W_V, L0_gnn_W_edge, L0_gnn_mu)
    h = jnp.maximum(_layernorm(x, axis=-1), 0.0)
    x = x + _L1_gnn_ref(h, edge_weight, L1_gnn_ip_w1, L1_gnn_ip_b1, L1_gnn_ip_ln_w, L1_gnn_ip_ln_b, L1_gnn_ip_w2, L1_gnn_ip_b2, L1_gnn_pn_w, L1_gnn_pn_b, L1_gnn_ta_w1, L1_gnn_ta_b1, L1_gnn_ta_ln_w, L1_gnn_ta_ln_b, L1_gnn_ta_w2, L1_gnn_ta_b2, L1_gnn_g1_w, L1_gnn_g1_att_src, L1_gnn_g1_att_dst, L1_gnn_g1_ew, L1_gnn_g1_att_edge, L1_gnn_g1_b, L1_gnn_g2_w, L1_gnn_g2_att_src, L1_gnn_g2_att_dst, L1_gnn_g2_ew, L1_gnn_g2_att_edge, L1_gnn_g2_b, L1_gnn_n1_w, L1_gnn_n1_b, L1_gnn_n2_w, L1_gnn_n2_b, edge_index)
    return x

_drawn_inputs = setup_inputs


def setup_inputs(seed=0):
    import zlib

    import numpy as np

    out = dict(_drawn_inputs(seed))
    spreads = {'L0_gnn_mu': (1.0, 0.6),
     'L1_gnn_ip_b1': (0.0, 0.1),
     'L1_gnn_ip_ln_w': (1.0, 0.2),
     'L1_gnn_ip_ln_b': (0.0, 0.1),
     'L1_gnn_ip_b2': (0.0, 0.1),
     'L1_gnn_pn_w': (1.0, 0.2),
     'L1_gnn_pn_b': (0.0, 0.1),
     'L1_gnn_ta_b1': (0.0, 0.8),
     'L1_gnn_ta_ln_w': (1.0, 0.6),
     'L1_gnn_ta_ln_b': (0.0, 0.8),
     'L1_gnn_ta_b2': (0.0, 0.8),
     'L1_gnn_g1_b': (0.0, 0.1),
     'L1_gnn_g2_b': (0.0, 0.1),
     'L1_gnn_n1_w': (1.0, 0.2),
     'L1_gnn_n1_b': (0.0, 0.1),
     'L1_gnn_n2_w': (1.0, 0.2),
     'L1_gnn_n2_b': (0.0, 0.1)}
    factors = {'edge_weight': 8.0,
     'L0_gnn_W_Q': 8.0,
     'L0_gnn_W_K': 8.0,
     'L0_gnn_W_edge': 8.0,
     'L1_gnn_ta_w1': 8.0,
     'L1_gnn_ta_w2': 8.0,
     'L1_gnn_g1_att_src': 8.0,
     'L1_gnn_g1_att_dst': 64.0,
     'L1_gnn_g1_ew': 8.0,
     'L1_gnn_g1_att_edge': 8.0,
     'L1_gnn_g2_att_src': 7.854,
     'L1_gnn_g2_att_dst': 61.69,
     'L1_gnn_g2_ew': 8.0,
     'L1_gnn_g2_att_edge': 8.0}
    for name, (base, spread) in spreads.items():
        noise = np.random.default_rng([zlib.crc32(name.encode()), seed]).standard_normal(out[name].shape)
        drawn = base * np.exp(spread * noise) if base else spread * noise
        out[name] = jnp.asarray(drawn.astype(out[name].dtype))
    for name, factor in factors.items():
        out[name] = (out[name] * factor).astype(out[name].dtype)
    return out
```

```python
import concourse.bass as bass
from concourse import mybir
from contextlib import ExitStack

F32 = mybir.dt.float32
BF16 = mybir.dt.bfloat16
I32 = mybir.dt.int32
ALU = mybir.AluOpType
ACT = mybir.ActivationFunctionType
AX = mybir.AxisListType
ds = bass.ds

P = 128
BIG = 1e30
NOWHERE = 8000


class Chain:

    def __init__(self, eng, sem):
        self.eng, self.sem, self.n = eng, sem, 0

    def did(self, instruction):
        instruction.then_inc(self.sem, 1)
        self.n += 1

    def wait(self):
        self.eng.wait_ge(self.sem, self.n)


def build(nc, A, out):
    N = A["x"].shape[0]
    E = A["src"].shape[0]
    NB = -(-N // P)
    LAST = N - (NB - 1) * P
    ROW = 512
    Q = -(-E // ROW)
    TPR = ROW // P
    T = Q * TPR
    EP = Q * ROW
    LROW = E - (Q - 1) * ROW
    NT = A["L0_gnn_W_Q"].shape[0]
    ET = A["L0_gnn_W_edge"].shape[0]
    H = A["L1_gnn_g1_att_src"].shape[0]
    C = P // H
    H2 = 2 * H
    NW = NB * P
    NWP = NW + P
    KV = 2 * P
    SUP = 16
    GPS = SUP // TPR
    NSUP = T // SUP
    RS = NSUP // 2
    NG = -(-NB // 4)
    EPS = 1e-5
    NGG = -(-NB // 3)
    NCONST, N_E_IN = 13, 13
    assert EP == T * P and T % (2 * SUP) == 0 and RS * 2 == NSUP and NWP <= NOWHERE

    def dram(name, shape, dt=F32):
        return nc.dram_tensor(name, shape, dt).ap()

    kv_table = dram("kv_table", (N * ET, KV))
    v_spill = dram("v_spill", (NSUP, P, SUP * P))
    row_table = [dram(f"row_table{l}", (N, P)) for l in range(2)]
    rate_d = dram("rate_d", (2, EP))
    aedge_d = dram("aedge_d", (H2, EP))
    ends_d = dram("ends_d", (EP, H2))
    starts_d = [dram(f"starts_d{l}", (EP, H2)) for l in range(2)]
    loops_d = [dram(f"loops_d{l}", (EP, H)) for l in range(2)]
    lo_d = dram("lo_d", (1, EP), BF16)
    x1_d = dram("x1_d", (P, NW))
    res_d = dram("res_d", (P, NW))
    hw_d = dram("hw_d", (P, NW))

    ctx = ExitStack()
    with ctx:
        def sb(name, shape, dt=F32):
            return ctx.enter_context(nc.sbuf_tensor(name, shape, dt))

        sems = {}

        def S(name):
            if name not in sems:
                sems[name] = ctx.enter_context(nc.semaphore(name))
            return sems[name]

        ps = ctx.enter_context(nc.psum_tensor("ps", [P, 8, 512], F32))

        def bank(i):
            return ps[:, i, :]

        ring = sb("ring", [P, RS * SUP * P])
        acc = sb("acc", [P, NWP])
        node = sb("node", [P, 3 * NW])
        nodes = [node[:, i * NW:(i + 1) * NW].rearrange("p (b f) -> p b f", f=P) for i in range(3)]

        def scan_tile(i, n=1):
            return node[0:Q, i * H * ROW:(i + n) * H * ROW].rearrange("p (h c) -> p h c", c=ROW)

        def cut(at, n):
            return ring[:, at:at + n]

        hTt = [cut(i * NW, NW) for i in range(NT)]
        KT = cut(NT * NW, NW)
        QT = cut((NT + 1) * NW, NWP)
        free0 = (NT + 1) * NW + NWP
        stg = [cut(free0 + i * ET * KV, ET * KV).rearrange("p (t f) -> p t f", f=KV) for i in range(2)]
        eraw = ring[0:Q, free0:free0 + 6 * ROW].rearrange("p (a c) -> p a c", c=ROW)
        ef = ring[0:Q, 0:10 * ROW].rearrange("p (a c) -> p a c", c=ROW)
        zero_rows = ring[0:Q, 10 * ROW:10 * ROW + H2 * ROW]
        tmpw = cut(NT * NW, NW)
        assert free0 + 2 * ET * KV <= RS * SUP * P
        kv_buf = [cut(i * SUP * KV, SUP * KV).rearrange("p (j f) -> p j f", f=KV) for i in range(2)]
        at = 2 * SUP * KV
        kTb = [cut(at + i * ROW, ROW) for i in range(2)]
        hid = [cut(at + (2 + i) * ROW, ROW) for i in range(2)]
        tw = [cut(at + (4 + i) * ROW, ROW) for i in range(2)]
        assert at + 6 * ROW <= (NT + 1) * NW
        aeb = ring[0:H2, free0:free0 + GPS * ROW]
        rateb = [ring[0:2, at + 6 * ROW + i * GPS * ROW:at + 6 * ROW + (i + 1) * GPS * ROW] for i in range(2)]
        assert at + 6 * ROW + 2 * GPS * ROW <= (NT + 1) * NW
        v_buf = [cut(i * SUP * P, SUP * P).rearrange("p (j f) -> p j f", f=P) for i in range(2)]
        zt = cut(0, NB * KV).rearrange("p (b f) -> p b f", f=KV)
        zT = [cut(NB * KV + i * NW, NW) for i in range(2)]
        hT = cut(NB * KV + 2 * NW, NW)
        rows = ring[:, :].rearrange("p (s j f) -> p s j f", s=RS, f=P)
        wqkv = acc[:, 0:3 * NT * P].rearrange("p (m t f) -> p m t f", m=3, t=NT)
        wedge = acc[:, 3 * NT * P:(3 * NT + ET) * P]
        ipw1 = acc[:, 0:KV]
        ipw2 = acc[:, KV:2 * KV].rearrange("p (a f) -> p a f", a=2)
        ipv = acc[:, 2 * KV:2 * KV + 9 * P]

        ident = sb("ident", [P, P])
        iota = sb("iota", [P, P])
        iota16 = sb("iota16", [P, P], BF16)
        ipart = sb("ipart", [P, 1])
        tri = sb("tri", [P, P])
        ones = sb("ones", [P, P])
        eps_t = sb("eps_t", [P, 1])
        cont = sb("cont", [Q, ROW], BF16)
        contn = sb("contn", [Q, ROW], BF16)
        pre = sb("pre", [Q, ROW], BF16)
        post = sb("post", [Q, ROW], BF16)
        pen = sb("pen", [Q, ROW], BF16)
        prepen = sb("prepen", [Q, ROW], BF16)
        rowf = sb("rowf", [H2, 3, Q])
        flags = sb("flags", [Q, 3, H2])
        carry = sb("carry", [H2, Q + 1])
        relT = sb("relT", [P, T])
        kvT = sb("kvT", [P, T], I32)
        srcT = sb("srcT", [P, T], I32)
        loT = sb("loT", [P, T], BF16)
        hiT = sb("hiT", [P, T], BF16)
        shiT = sb("shiT", [P, T], BF16)
        idx = sb("idx", [P, RS * SUP], I32)
        d0 = sb("d0", [1, T], I32)
        aT = sb("aT", [P, T, H])
        endi = sb("endi", [P, NB], I32)
        starti = sb("starti", [P, NB], I32)
        deg = sb("deg", [P, NB])
        mae = sb("mae", [P, NB, H2])
        ncol = sb("ncol", [P, NB, H2])
        nst = sb("nst", [P, NB, H2])
        al = sb("al", [P, NB, H])
        stats = sb("stats", [P, NB, 6])
        mv = sb("mv", [P, NB, 2])
        rstd = sb("rstd", [P, NB])
        vec6 = sb("vec6", [P, 6, P])
        Wx = sb("Wx", [P, P + H2])
        Wm = sb("Wm", [P, 2, H])
        taw2 = sb("taw2", [P, P])
        lhs2 = sb("lhs2", [2, P])
        lnwb = sb("lnwb", [2, P])
        tacol = sb("tacol", [P, 2])
        wk = sb("wk", [P, 2 * ROW])
        wk2 = [wk[:, i * ROW:(i + 1) * ROW] for i in range(2)]
        vst = [wk[:, i * P:(i + 1) * P] for i in range(2)]
        src16 = [sb(f"src16_{i}", [P, 2 * ROW], BF16) for i in range(2)]
        oh16 = [sb(f"oh16_{i}", [P, ROW], BF16) for i in range(2)]
        ohh = [sb(f"ohh{i}", [P, TPR, NB], BF16) for i in range(2)]
        A3 = sb("A3", [P, 3, NB * H], BF16)
        a3r = sb("a3r", [P, NB * H])
        smal = sb("smal", [P, 16])
        nb_ = sb("nb_", [P, NB])
        ticks = sb("ticks", [P, 4])
        lhm = sb("lhm", [2, 1])

        block = ctx.enter_context(nc.Block())

        def row_of(ap):
            return ap.rearrange("(a n) -> a n", a=1)

        def spread(ap, n=P):
            return row_of(ap).to_broadcast([n, ap.shape[0]])

        def node_blocks(table, f=P):
            return (table[0:(NB - 1) * P, :].rearrange("(b p) f -> p b f", p=P), table[(NB - 1) * P:N, :])

        def bc(ap, axis, shape):
            return ap.unsqueeze(axis).to_broadcast(shape)

        @block.sync
        def _(sp):
            D, DP, DN, SR, TY, EW = [eraw[:, i, :] if i == 5 else eraw[:, i, :].bitcast(I32) for i in range(6)]
            sp.wait_ge(S("const"), NCONST)

            def edges(dst, src, shift):
                if shift < 0:
                    sp.dma_start(dst[0:1, 1:ROW], src[0:ROW - 1].unsqueeze(0)).then_inc(S("e_in"), 16)
                    sp.dma_start(dst[1:Q - 1, :], src[ROW - 1:(Q - 1) * ROW - 1].rearrange("(q c) -> q c", c=ROW)).then_inc(S("e_in"), 16)
                else:
                    sp.dma_start(dst[0:Q - 1, :], src[shift:shift + (Q - 1) * ROW].rearrange("(q c) -> q c", c=ROW)).then_inc(S("e_in"), 16)
                n = LROW - shift
                sp.dma_start(dst[Q - 1:Q, 0:n], src[(Q - 1) * ROW + shift:E].unsqueeze(0)).then_inc(S("e_in"), 16)

            edges(D, A["dst"], 0)
            edges(DP, A["dst"], -1)
            edges(DN, A["dst"], 1)
            edges(SR, A["src"], 0)
            edges(TY, A["edge_type_8"], 0)
            edges(EW, A["edge_weight"], 0)
            assert 13 == N_E_IN
            xa, xb = node_blocks(A["x"])
            sp.dma_start(nodes[0][:, 0:NB - 1, :], xa).then_inc(S("x_in"), 16)
            sp.dma_start(nodes[0][0:LAST, NB - 1, :], xb).then_inc(S("x_in"), 16)
            with nc.allow_non_contiguous_dma("one destination per tile"):
                sp.dma_start(d0[0:1, :], A["dst"].unsqueeze(0)[:, 0:E:P]).then_inc(S("d0_in"), 16)
                sp.dma_start(tacol[:, 0:1], A["L1_gnn_ta_ln_b"].unsqueeze(1)).then_inc(S("ta_in"), 16)
                sp.dma_start(tacol[:, 1:2], A["L1_gnn_ta_b2"].unsqueeze(1)).then_inc(S("ta_in"), 16)
            for l in range(2):
                sp.dma_start(starts_d[l].rearrange("(q c) h -> q (c h)", c=ROW), zero_rows).then_inc(S("zero_out"), 16)
            sp.wait_ge(S("lo_ready"), 1)
            sp.dma_start(lo_d.rearrange("a (q c) -> q (a c)", c=ROW), ef[:, 8, 0:ROW // 2].bitcast(BF16)).then_inc(S("lo_out"), 16)
            sp.wait_ge(S("rate_ready"), 1)
            sp.dma_start(rate_d.rearrange("a (q c) -> q a c", c=ROW), ef[:, 0:2, :]).then_inc(S("rate_out"), 16)

            def kv_store(b, h):
                sp.wait_ge(S("kv_dve"), b + 1)
                sp.wait_ge(S("kv_act"), b + 1)
                sp.wait_ge(S("kv_pool"), b + 1)
                if isinstance(b, int) and b == NB - 1:
                    sp.dma_start(kv_table[b * P * ET:N * ET, :].rearrange("(p t) f -> p t f", t=ET),
                                 stg[h][0:LAST, :, :]).then_inc(S(f"kv_out{h}"), 16)
                else:
                    sp.dma_start(kv_table[ds(b * P * ET, P * ET), :].rearrange("(p t) f -> p t f", t=ET),
                                 stg[h][:, :, :]).then_inc(S(f"kv_out{h}"), 16)

            sp.wait_ge(S("rate_out"), 16)
            with sp.Fori(0, (NB - 1) // 2) as i:
                for h in range(2):
                    kv_store(2 * i + h, h)
            kv_store(NB - 1, 0)

            def walk1(i, h, first):
                s = 2 * i + h
                if not first:
                    sp.wait_ge(S("m1"), (s - 1) * GPS)
                sp.dma_start(rateb[h], rate_d[:, ds(s * GPS * ROW, GPS * ROW)]).then_inc(S(f"rate_in{h}"), 16)
                sp.wait_ge(S(f"got{h}"), (i + 1) * 16 * SUP)
                sp.dma_start(v_spill[ds(s, 1), :, :].rearrange("a p (j f) -> p (a j) f", f=P),
                             kv_buf[h][:, :, P:KV]).then_inc(S(f"spill{h}"), 16)
                if not (first and h == 0):
                    ae_store(s - 1)

            def ae_store(s):
                sp.wait_ge(S("ae"), s * GPS + GPS)
                sp.dma_start(aedge_d[:, ds(s * GPS * ROW, GPS * ROW)], aeb).then_inc(S("ae_out"), 16)

            for h in range(2):
                walk1(0, h, True)
            with sp.Fori(1, NSUP // 2) as i:
                for h in range(2):
                    walk1(i, h, False)
            ae_store(NSUP - 1)

            sp.wait_ge(S("ae_out"), 16 * NSUP)
            sp.wait_ge(S("sm0"), 1)
            sp.dma_start(scan_tile(0, 2), aedge_d.rearrange("h (q c) -> q h c", c=ROW)).then_inc(S("ae_in"), 16)
            for h in range(2):
                sp.wait_ge(S(f"spill{h}"), 16 * NSUP // 2)

            def walk2(i, h, first):
                s = 2 * i + h
                if not first:
                    sp.wait_ge(S("sum"), (s - 1) * GPS)
                sp.dma_start(v_buf[h], v_spill[ds(s, 1), :, :].rearrange("a p (j f) -> p (a j) f", f=P)).then_inc(S(f"v_in{h}"), 16)

            for h in range(2):
                walk2(0, h, True)
            sp.wait_ge(S("mae1"), 1)
            sp.dma_start(ends_d.rearrange("(q c) h -> q (c h)", c=ROW),
                         scan_tile(0, 2).rearrange("p h c -> p (h c)")).then_inc(S("ends_out"), 16)
            with sp.Fori(1, NSUP // 2) as i:
                for h in range(2):
                    walk2(i, h, False)

            sp.wait_ge(S("ends_out"), 16)
            sp.dma_start(nodes[0][:, 0:NB - 1, :], xa).then_inc(S("x_in"), 16)
            sp.dma_start(nodes[0][0:LAST, NB - 1, :], xb).then_inc(S("x_in"), 16)
            sp.wait_ge(S("x1"), NG)
            sp.dma_start(x1_d, nodes[0].rearrange("p b f -> p (b f)")).then_inc(S("x1_out"), 16)
            sp.dma_start(ipw1, A["L1_gnn_ip_w1"]).then_inc(S("ip_in"), 16)
            sp.dma_start(ipw2, A["L1_gnn_ip_w2"].rearrange("(a p) f -> p a f", p=P)).then_inc(S("ip_in"), 16)
            at_ = 0
            for name in ("ip_b1", "ip_ln_w", "ip_ln_b", "ip_b2", "pn_w", "pn_b"):
                n = A["L1_gnn_" + name].shape[0]
                sp.dma_start(ipv[:, at_:at_ + n], spread(A["L1_gnn_" + name])).then_inc(S("ip_in"), 16)
                at_ += n

            for l in range(2):
                g = f"L1_gnn_g{l + 1}_"
                sp.wait_ge(S("x1"), (l + 1) * NG)
                sp.dma_start(Wx[:, 0:P], A[g + "w"]).then_inc(S("gw_in"), 16)
                sp.dma_start(wk[:, 0:P], spread(A[g + "att_src"].rearrange("h c -> (h c)"))).then_inc(S("gw_in"), 16)
                sp.dma_start(wk[:, P:2 * P], spread(A[g + "att_dst"].rearrange("h c -> (h c)"))).then_inc(S("gw_in"), 16)
                sp.wait_ge(S("tsrc"), 5 + l)
                sp.dma_start(res_d, nodes[0].rearrange("p b f -> p (b f)")).then_inc(S("res_out"), 16)
                sp.wait_ge(S("hw"), 9 * (l + 1))
                ra, rb = node_blocks(row_table[l])
                sp.dma_start(ra, nodes[1][:, 0:NB - 1, :]).then_inc(S("row_out"), 16)
                sp.dma_start(rb, nodes[1][0:LAST, NB - 1, :]).then_inc(S("row_out"), 16)
                sp.dma_start(hw_d, nodes[1].rearrange("p b f -> p (b f)")).then_inc(S("hw_out"), 16)
                sp.wait_ge(S("row_out"), 32 * (l + 1))
                sp.wait_ge(S("hw_out"), 16 * (l + 1))
                sp.wait_ge(S("res_out"), 16 * (l + 1))
                sp.wait_ge(S("start_out"), 16 * NB * (l + 1))
                sp.dma_start(scan_tile(2, 2).rearrange("p h c -> p (h c)"),
                             starts_d[l].rearrange("(q c) h -> q (c h)", c=ROW)).then_inc(S("start_in"), 16)

                def lo_in(i, h, first):
                    if not first:
                        sp.wait_ge(S("oh"), Q + l * Q + 4 * i + 2 * h - 2)
                    sp.dma_start(src16[h][:, :], lo_d[:, ds((2 * i + h) * 2 * ROW, 2 * ROW)].to_broadcast([P, 2 * ROW])).then_inc(S(f"lo_in{h}"), 16)

                for h in range(2):
                    lo_in(0, h, True)
                with sp.Fori(1, Q // 4) as i:
                    for h in range(2):
                        lo_in(i, h, False)
                sp.wait_ge(S("held"), l + 1)
                sp.dma_start(scan_tile(3), aedge_d[l * H:(l + 1) * H, :].rearrange("h (q c) -> q h c", c=ROW)).then_inc(S("ael_in"), 16)
                sp.wait_ge(S("el"), l + 1)
                sp.dma_start(loops_d[l].rearrange("(q c) h -> q (c h)", c=ROW),
                             scan_tile(0).rearrange("p h c -> p (h c)")).then_inc(S("loop_out"), 16)
                sp.wait_ge(S("loop_out"), 16 * (l + 1))
                sp.wait_ge(S("wT"), H * (l + 1))
                sp.dma_start(nodes[0].rearrange("p b f -> p (b f)"), res_d).then_inc(S("back_in"), 16)
                sp.dma_start(nodes[1].rearrange("p b f -> p (b f)"), hw_d).then_inc(S("back_in"), 16)
            sp.wait_ge(S("mixed"), 2)
            sp.dma_start(nodes[1].rearrange("p b f -> p (b f)"), x1_d).then_inc(S("x1_in"), 16)
            sp.wait_ge(S("final"), 1)
            oa, ob = node_blocks(out)
            sp.dma_start(oa, nodes[0][:, 0:NB - 1, :]).then_inc(S("out"), 16)
            sp.dma_start(ob, nodes[0][0:LAST, NB - 1, :]).then_inc(S("out"), 16)
            sp.wait_ge(S("out"), 32)

        @block.gpsimd
        def _(pool):
            c = Chain(pool, S("const"))
            c.did(pool.memset(eraw[:, 0:3, :].bitcast(I32), NOWHERE))
            c.did(pool.memset(eraw[:, 3:6, :], 0.0))
            c.did(pool.memset(nodes[0][:, NB - 1, :], 0.0))
            c.did(pool.memset(zero_rows, 0.0))
            c.did(pool.memset(ident[:, :], 0.0))
            c.did(pool.memset(ticks[:, :], 0.0))
            c.did(pool.memset(tri[:, :], 1.0))
            c.did(pool.memset(ones[:, :], 1.0))
            c.did(pool.iota(iota[:, :], [[1, P]], base=0, channel_multiplier=0, allow_small_or_imprecise_dtypes=True))
            c.did(pool.iota(iota16[:, :], [[1, P]], base=0, channel_multiplier=0, allow_small_or_imprecise_dtypes=True))
            c.did(pool.iota(ipart[:, :], [[0, 1]], base=0, channel_multiplier=1, allow_small_or_imprecise_dtypes=True))
            c.wait()
            c.did(pool.affine_select(out=ident[:, :], in_=ident[:, :], compare_op=ALU.not_equal, fill=1.0, base=0,
                                     pattern=[[-1, P]], channel_multiplier=1))
            c.did(pool.affine_select(out=tri[:, :], in_=tri[:, :], compare_op=ALU.is_ge, fill=0.0, base=0,
                                     pattern=[[1, P]], channel_multiplier=-1))
            assert c.n == NCONST

            def tick(n):
                if not (isinstance(n, int) and n == 0):
                    pool.wait_ge(S("tick"), n)
                pool.tensor_tensor(ticks[:, 0:1], ticks[:, 1:2], ticks[:, 2:3], ALU.add).then_inc(S("tick"), 1)

            def spread_v(b, h, i):
                pool.wait_ge(S("v_sb"), b + 1)
                if i is not None:
                    pool.wait_ge(S(f"kv_out{h}"), 16 * i)
                tick(b)
                pool.tensor_copy(stg[h][:, :, P:KV], bc(vst[h], 1, [P, ET, P])).then_inc(S("kv_pool"), 1)

            for h in range(2):
                spread_v(h, h, None)
            with pool.Fori(1, (NB - 1) // 2) as i:
                for h in range(2):
                    spread_v(2 * i + h, h, i)
            spread_v(NB - 1, 0, (NB - 1) // 2)
            pool.wait_ge(S("kv_out0"), 16 * (NB // 2 + 1))
            pool.wait_ge(S("kv_out1"), 16 * (NB // 2))
            pool.memset(acc[:, :], 0.0).then_inc(S("acc0"), 1)

            def walk1(i, h, first):
                s = 2 * i + h
                if not first:
                    pool.wait_ge(S(f"got{h}"), i * 16 * SUP)
                    pool.wait_ge(S("kT"), (s - 1) * GPS)
                    pool.wait_ge(S(f"spill{h}"), 16 * i)
                tick(NB + 2 * s)
                pool.tensor_copy(idx[:, h * SUP:(h + 1) * SUP], kvT[:, ds(s * SUP, SUP)]).then_inc(S("idx"), 1)
                pool.wait_ge(S("idx"), s + 1)
                tick(NB + 2 * s + 1)
                for j in range(SUP):
                    pool.indirect_dma_start(kv_buf[h][:, j, :], None, kv_table,
                                            bass.IndirectOffsetOnAxis(ap=idx[:, h * SUP + j:h * SUP + j + 1], axis=0)).then_inc(S(f"got{h}"), 16)

            pool.wait_ge(S("ef_sb"), 2)
            for h in range(2):
                walk1(0, h, True)
            with pool.Fori(1, NSUP // 2) as i:
                for h in range(2):
                    walk1(i, h, False)

            pool.memset(ncol[:, :, :], 0.0).then_inc(S("ncol0"), 1)
            pool.wait_ge(S("ncol0"), 1)
            pool.wait_ge(S("ends_out"), 16)
            pool.wait_ge(S("endi"), 2)
            for b in range(NB):
                n = LAST if b == NB - 1 else P
                pool.indirect_dma_start(ncol[0:n, b, :], None, ends_d,
                                        bass.IndirectOffsetOnAxis(ap=endi[0:n, b:b + 1], axis=0)).then_inc(S("sums_in"), 16)

            for l in range(2):
                pool.wait_ge(S("nst"), 2 * (l + 1))
                pool.wait_ge(S("zero_out"), 32)
                for b in range(NB):
                    n = LAST if b == NB - 1 else P
                    pool.indirect_dma_start(starts_d[l], bass.IndirectOffsetOnAxis(ap=starti[0:n, b:b + 1], axis=0),
                                            nst[0:n, b, :], None).then_inc(S("start_out"), 16)
                pool.memset(al[:, :, :], 0.0).then_inc(S("al0"), 1)
                pool.wait_ge(S("row_out"), 32 * (l + 1))
                for half in range(2):
                    if half:
                        pool.wait_ge(S("loop_out"), 16 * (l + 1))
                        pool.wait_ge(S("al0"), l + 1)
                        for b in range(NB):
                            n = LAST if b == NB - 1 else P
                            pool.indirect_dma_start(al[0:n, b, :], None, loops_d[l],
                                                    bass.IndirectOffsetOnAxis(ap=endi[0:n, b:b + 1], axis=0)).then_inc(S("al_in"), 16)
                    if l + half > 0:
                        for s in range(RS):
                            pool.wait_ge(S(f"row{s}"), (2 * l + half) * 16 * SUP)
                    pool.tensor_copy(idx[:, :], srcT[:, half * RS * SUP:(half + 1) * RS * SUP]).then_inc(S("idx"), 1)
                    pool.wait_ge(S("idx"), NSUP + 2 * l + half + 1)
                    for s in range(RS):
                        if half:
                            pool.wait_ge(S("sum"), Q + l * Q + (s + 1) * GPS)
                        for j in range(SUP):
                            pool.indirect_dma_start(rows[:, s, j, :], None, row_table[l],
                                                    bass.IndirectOffsetOnAxis(ap=idx[:, s * SUP + j:s * SUP + j + 1], axis=0)).then_inc(S(f"row{s}"), 16)

        @block.scalar
        def _(act):
            def root(k):
                act.wait_ge(S("var"), k + 1)
                act.activation(rstd[:, :], rstd[:, :], ACT.Sqrt).then_inc(S("std"), 1)

            def turned(k, dst):
                for g in range(NG):
                    n = min(4, NB - 4 * g) * P
                    act.wait_ge(S("tr"), k * NG + g + 1)
                    act.activation(dst[:, 4 * g * P:4 * g * P + n], bank((k * NG + g) % 2)[:, 0:n], ACT.Copy).then_inc(S("tr_sb"), 1)

            for dst, src in ((tmpw[:, 0:P], A["L1_gnn_g1_ew"]), (tmpw[:, P:2 * P], A["L1_gnn_g2_ew"]),
                             (tmpw[:, 2 * P:3 * P], spread(A["L1_gnn_g1_att_edge"].rearrange("h c -> (h c)"))),
                             (tmpw[:, 3 * P:4 * P], spread(A["L1_gnn_g2_att_edge"].rearrange("h c -> (h c)"))),
                             (wk[:, 0:P], A["L1_gnn_ta_w1"].to_broadcast([P, P])),
                             (wk[:, P:2 * P], spread(A["L1_gnn_ta_b1"])),
                             (lhs2[0:1, :], A["L1_gnn_ta_w1"]), (lhs2[1:2, :], row_of(A["L1_gnn_ta_b1"])),
                             (lnwb[:, :], spread(A["L1_gnn_ta_ln_w"], 2)), (smal[:, 8:8 + ET], spread(A["L0_gnn_mu"])),
                             (taw2[:, :], A["L1_gnn_ta_w2"]),
                             (wqkv[:, 0, :, :], A["L0_gnn_W_K"].rearrange("t i o -> i t o")),
                             (wqkv[:, 1, :, :], A["L0_gnn_W_Q"].rearrange("t i o -> i t o")),
                             (wqkv[:, 2, :, :], A["L0_gnn_W_V"].rearrange("t i o -> i t o")),
                             (wedge.rearrange("p (t o) -> p t o", o=P), A["L0_gnn_W_edge"].rearrange("t i o -> i t o"))):
                act.dma_start(dst, src).then_inc(S("w_in"), 16)
            for i, (g, name) in enumerate((l, n) for l in (1, 2) for n in ("g{}_b", "n{}_w", "n{}_b")):
                act.dma_start(vec6[:, i, :], spread(A["L1_gnn_" + name.format(g)])).then_inc(S("w_in"), 16)
            act.wait_ge(S("const"), NCONST)
            act.dma_start(nodes[2][:, :, :].rearrange("p b f -> p (b f)").bitcast(I32)[:, 0:N], spread(A["node_type_4"])).then_inc(S("nt_in"), 16)

            act.wait_ge(S("rvar"), 1)
            act.activation(ef[:, 1, :], ef[:, 1, :], ACT.Sqrt).then_inc(S("rstd0"), 1)
            root(0)
            turned(0, KT)
            for m, dst in enumerate((KT, QT)):
                for g in range(NG):
                    n = min(512, NW - g * 512)
                    act.wait_ge(S("qk"), m * NG + g + 1)
                    act.activation(dst[:, g * 512:g * 512 + n], bank(2 + (m * NG + g) % 2)[:, 0:n], ACT.Copy).then_inc(S("qk_sb"), 1)

            def kv(b, h, i):
                act.wait_ge(S("kv"), b + 1)
                if i is not None:
                    act.wait_ge(S("kv_pool"), b - 1)
                act.activation(vst[h], bank(4 + h)[:, 0:P], ACT.Copy).then_inc(S("v_sb"), 1)
                if i is not None:
                    act.wait_ge(S(f"kv_out{h}"), 16 * i)
                act.activation(stg[h][:, ET // 2:ET, 0:P], bank(2 * h + 1).rearrange("p (t f) -> p t f", f=P), ACT.Copy).then_inc(S("kv_act"), 1)

            for h in range(2):
                kv(h, h, None)
            with act.Fori(1, (NB - 1) // 2) as i:
                for h in range(2):
                    kv(2 * i + h, h, i)
            kv(NB - 1, 0, (NB - 1) // 2)

            def walk1(i, first):
                for gg in range(2 * GPS):
                    g = 2 * GPS * i + gg
                    f = first and gg < 2
                    act.wait_ge(S("kT"), g + 1)
                    if not f:
                        act.wait_ge(S("kq"), g - 1)
                    act.activation(kTb[gg % 2], bank(gg % 2), ACT.Copy).then_inc(S("kT_sb"), 1)
                    act.wait_ge(S("m1"), g + 1)
                    if not f:
                        act.wait_ge(S("m2"), g - 1)
                    act.activation(hid[gg % 2], bank(4), ACT.Relu, bias=tacol[:, 0:1]).then_inc(S("relu"), 1)
                    act.wait_ge(S("m2"), g + 1)
                    if not f:
                        act.wait_ge(S("m3"), g - 1)
                    act.activation(tw[gg % 2], bank(5), ACT.Tanh, bias=tacol[:, 1:2]).then_inc(S("tanh"), 1)

            act.wait_ge(S("ta_in"), 32)
            walk1(0, True)
            with act.Fori(1, NSUP // 2) as i:
                walk1(i, False)
            act.wait_ge(S("xm"), 1)
            act.activation(scan_tile(0)[:, 0, :], scan_tile(0)[:, 0, :], ACT.Exp).then_inc(S("exp"), 1)

            root(1)
            turned(1, hT)
            root(2)
            turned(2, zT[0])
            turned(3, zT[1])
            root(3)
            for l in range(2):
                turned(4 + l, hT)
                act.wait_ge(S("xm"), 2 + l)
                act.activation(scan_tile(2), scan_tile(2), ACT.Exp).then_inc(S("exp"), 1)
                act.wait_ge(S("elm"), 1 + l)
                act.activation(scan_tile(1), scan_tile(1), ACT.Exp).then_inc(S("exp"), 1)
                root(4 + l)
                act.wait_ge(S("elu"), l + 1)
                act.activation(nodes[2], nodes[2], ACT.Exp).then_inc(S("elu_e"), 1)

        @block.tensor
        def _(pe):
            def turn(k, blocks):
                pe.wait_ge(S("tsrc"), k + 1)
                for g in range(NG):
                    n = k * NG + g
                    if n >= 2:
                        pe.wait_ge(S("tr_sb"), n - 1)
                    nb = min(4, NB - 4 * g)
                    for j in range(nb):
                        t = pe.transpose(bank(n % 2)[:, j * P:(j + 1) * P], blocks(4 * g + j), ident[:, :])
                    t.then_inc(S("tr"), 1)

            def turn_sums(k):
                pe.wait_ge(S("added"), (k + 1) * T)
                for g in range(NG):
                    if k * NG + g >= 2:
                        pe.wait_ge(S("x1"), k * NG + g - 1)
                    for j in range(min(4, NB - 4 * g)):
                        b = 4 * g + j
                        t = pe.transpose(bank((k * NG + g) % 2)[:, j * P:(j + 1) * P], acc[:, b * P:(b + 1) * P], ident[:, :])
                    t.then_inc(S("accT"), 1)

            def carried(k, n, tile, back):
                pe.wait_ge(S("local"), k + 1)
                pe.transpose(bank(7)[0:n, 0:Q], tile[:, :, 0 if back else ROW - 1], ident[0:Q, 0:Q]).then_inc(S("carT"), 1)
                pe.wait_ge(S("carS"), k + 1)
                pe.transpose(bank(7)[0:Q, P:P + n], carry[0:n, 1:Q + 1] if back else carry[0:n, 0:Q],
                             ident[0:n, 0:n]).then_inc(S("carB"), 1)

            pe.wait_ge(S("const"), NCONST)
            pe.wait_ge(S("ef"), 1)
            for a, e in enumerate((4, 1, 7, 5, 2, 3)):
                for k in range(TPR):
                    t = pe.transpose(bank(a)[:, k * Q:(k + 1) * Q], ef[:, e, k * P:(k + 1) * P], ident[0:Q, 0:Q])
                t.then_inc(S("efT"), 1)
            pe.wait_ge(S("flags"), 1)
            for a in range(3):
                t = pe.transpose(bank(6)[0:H2, a * Q:(a + 1) * Q], flags[:, a, :], ident[0:Q, 0:Q])
            t.then_inc(S("flT"), 1)
            pe.wait_ge(S("ef_sb"), 7)
            turn(0, lambda b: nodes[1][:, b, :])

            pe.wait_ge(S("w_in"), 16 * 21)
            pe.wait_ge(S("hTt"), NT)
            for m in range(2):
                for g in range(NG):
                    k = m * NG + g
                    if k >= 2:
                        pe.wait_ge(S("qk_sb"), k - 1)
                    n = min(512, NW - g * 512)
                    for t in range(NT):
                        mm = pe.matmul(bank(2 + k % 2)[:, 0:n], wqkv[:, m, t, :], hTt[t][:, g * 512:g * 512 + n],
                                       start=(t == 0), stop=(t == NT - 1))
                    mm.then_inc(S("qk"), 1)
            pe.wait_ge(S("qk_sb"), 2 * NG)
            pe.wait_ge(S("tr_sb"), NG)
            pe.wait_ge(S("we"), 1)
            for b in range(NB):
                h = b % 2
                if b >= 2:
                    pe.wait_ge(S("kv_dve"), b - 1)
                    pe.wait_ge(S("kv_act"), b - 1)
                for t in range(NT):
                    pe.matmul(bank(4 + h)[:, 0:P], hTt[t][:, b * P:(b + 1) * P], wqkv[:, 2, t, :],
                              start=(t == 0), stop=(t == NT - 1))
                for half in range(2):
                    mm = pe.matmul(bank(2 * h + half), KT[:, b * P:(b + 1) * P], wedge[:, half * 512:(half + 1) * 512],
                                   start=True, stop=True)
                mm.then_inc(S("kv"), 1)

            def edge_terms(g, gg):
                pe.wait_ge(S("tanh"), g + 1)
                pe.matmul(bank(6)[0:H2, :], Wm[:, :, :].rearrange("p l h -> p (l h)"), tw[gg % 2], start=True, stop=True).then_inc(S("m3"), 1)

            def walk1(i, first):
                for gg in range(2 * GPS):
                    h, g = gg // GPS, 2 * GPS * i + gg
                    if gg % GPS == 0:
                        pe.wait_ge(S(f"got{h}"), (i + 1) * 16 * SUP)
                        pe.wait_ge(S(f"rate_in{h}"), 16 * (i + 1))
                    if gg % 2 == 0:
                        _, w = nc.values_load_multi_w_load_instructions(
                            d0[0:1, ds(g * TPR, 2 * TPR)], engines=[mybir.EngineType.PE], min_val=0, max_val=NW,
                            skip_runtime_bounds_check_because="destinations are nodes")
                    if not (first and gg < 2):
                        pe.wait_ge(S("kT_sb"), g - 1)
                    for j in range(TPR):
                        t = pe.transpose(bank(gg % 2)[:, j * P:(j + 1) * P],
                                         kv_buf[h][:, gg % GPS * TPR + j, 0:P], ident[:, :])
                    t.then_inc(S("kT"), 1)
                    if not (first and gg < 1):
                        pe.wait_ge(S("relu"), g)
                    pe.matmul(bank(4), lhs2[:, :], rateb[h][:, gg % GPS * ROW:(gg % GPS + 1) * ROW], start=True, stop=True).then_inc(S("m1"), 1)
                    if not (first and gg < 1):
                        if not (first and gg < 2):
                            pe.wait_ge(S("ae"), g - 1)
                        edge_terms(g - 1, gg + 1)
                    pe.wait_ge(S("kT_sb"), g + 1)
                    if not (first and gg < 2):
                        pe.wait_ge(S("score"), g - 1)
                    for j in range(TPR):
                        mm = pe.matmul(bank(2 + gg % 2)[:, j * P:(j + 1) * P], kTb[gg % 2][:, j * P:(j + 1) * P],
                                       QT[:, ds(w[gg % 2 * TPR + j], P)], start=True, stop=True)
                    mm.then_inc(S("kq"), 1)
                    pe.wait_ge(S("relu"), g + 1)
                    if not (first and gg < 1):
                        pe.wait_ge(S("tanh"), g)
                    pe.matmul(bank(5), taw2[:, :], hid[gg % 2], start=True, stop=True).then_inc(S("m2"), 1)
                    pe.wait_ge(S("oh"), g + 1)
                    for j in range(TPR):
                        mm = pe.matmul(bank(7)[:, 0:NB], oh16[gg % 2][:, j * P:(j + 1) * P], ohh[gg % 2][:, j, :],
                                       start=(first and gg == 0 and j == 0), stop=False, skip_group_check=True)
                    mm.then_inc(S("hist"), 1)

            pe.wait_ge(S("kv_act"), NB)
            pe.wait_ge(S("kv_dve"), NB)
            pe.wait_ge(S("d0_in"), 16)
            pe.wait_ge(S("qtpad"), 1)
            pe.wait_ge(S("Wm"), 1)
            walk1(0, True)
            with pe.Fori(1, NSUP // 2) as i:
                walk1(i, False)
            pe.wait_ge(S("ae"), Q - 1)
            edge_terms(Q - 1, 1)

            pe.wait_ge(S("deg"), 1)
            pe.wait_ge(S("ae"), Q)
            pe.matmul(bank(6)[:, 0:NB], tri[:, :], deg[:, :], start=True, stop=True)
            pe.matmul(bank(6)[:, 32:32 + NB], ones[:, :], deg[:, :], start=True, stop=True).then_inc(S("cum"), 1)

            pe.wait_ge(S("score"), Q)
            for k in range(TPR):
                t = pe.transpose(bank(0)[0:Q, k * P:(k + 1) * P], aT[:, k:T:TPR, 0], ident[:, :])
            t.then_inc(S("scT"), 1)
            carried(0, 1, scan_tile(1)[:, 0:1, :], False)
            carried(1, 1, scan_tile(2)[:, 0:1, :], True)
            carried(2, 1, scan_tile(1)[:, 0:1, :], False)
            carried(3, 1, scan_tile(2)[:, 0:1, :], True)
            pe.wait_ge(S("attn"), 1)
            for k in range(TPR):
                t = pe.transpose(bank(0)[:, k * Q:(k + 1) * Q], scan_tile(0)[:, 0, k * P:(k + 1) * P], ident[0:Q, 0:Q])
            t.then_inc(S("wb"), 1)
            carried(4, H2, scan_tile(2, 2), False)

            def walk2(i, first):
                for gg in range(2 * GPS):
                    h, g = gg // GPS, 2 * GPS * i + gg
                    if gg % GPS == 0:
                        pe.wait_ge(S(f"v_in{h}"), 16 * (i + 1))
                    pe.wait_ge(S("sel"), g + 1)
                    if not (first and gg < 2):
                        pe.wait_ge(S("added"), TPR * (g - 1))
                    for j in range(TPR):
                        mm = pe.matmul(bank(2 + gg % 2)[:, j * P:(j + 1) * P], v_buf[h][:, gg % GPS * TPR + j, :],
                                       wk2[gg % 2][:, j * P:(j + 1) * P], start=True, stop=True)
                    mm.then_inc(S("sum"), 1)

            walk2(0, True)
            with pe.Fori(1, NSUP // 2) as i:
                walk2(i, False)
            turn_sums(0)

            pe.wait_ge(S("x1"), NG)
            turn(1, lambda b: nodes[1][:, b, :])
            pe.wait_ge(S("tr_sb"), 2 * NG)
            pe.wait_ge(S("ip_in"), 16 * 8)
            for g in range(-(-NB // 2)):
                if g >= 2:
                    pe.wait_ge(S("z_sb"), g - 1)
                for j in range(min(2, NB - 2 * g)):
                    b = 2 * g + j
                    mm = pe.matmul(bank(2 + g % 2)[:, j * KV:(j + 1) * KV], hT[:, b * P:(b + 1) * P], ipw1, start=True, stop=True)
                mm.then_inc(S("z"), 1)
            turn(2, lambda b: zt[:, b, 0:P])
            turn(3, lambda b: zt[:, b, P:KV])
            pe.wait_ge(S("tr_sb"), 4 * NG)
            for g in range(NG):
                if g >= 2:
                    pe.wait_ge(S("y_sb"), g - 1)
                for j in range(min(4, NB - 4 * g)):
                    b = 4 * g + j
                    for a in range(2):
                        mm = pe.matmul(bank(2 + g % 2)[:, j * P:(j + 1) * P], zT[a][:, b * P:(b + 1) * P], ipw2[:, a, :],
                                       start=(a == 0), stop=(a == 1))
                mm.then_inc(S("y"), 1)

            for l in range(2):
                turn(4 + l, lambda b: nodes[0][:, b, :])
                pe.wait_ge(S("tr_sb"), (5 + l) * NG)
                pe.wait_ge(S("Wx"), l + 1)
                for g in range(NGG):
                    if l * NGG + g >= 2:
                        pe.wait_ge(S("hw"), l * NGG + g - 1)
                    for j in range(min(3, NB - 3 * g)):
                        b = 3 * g + j
                        mm = pe.matmul(bank(2 + (l * NGG + g) % 2)[:, j * (P + H2):(j + 1) * (P + H2)], hT[:, b * P:(b + 1) * P], Wx[:, :],
                                       start=True, stop=True)
                    mm.then_inc(S("hwp"), 1)
                pe.wait_ge(S("A3"), l + 1)

                def sources(i, first):
                    for gg in range(4):
                        g = 4 * i + gg
                        pe.wait_ge(S("oh"), Q + l * Q + g + 1)
                        if not (first and gg < 2):
                            pe.wait_ge(S("asel"), l * Q + g - 1)
                        for j in range(TPR):
                            for m in range(3):
                                mm = pe.matmul(bank(gg % 2)[:, j * NB * H:(j + 1) * NB * H], oh16[gg % 2][:, j * P:(j + 1) * P],
                                               A3[:, m, :], start=(m == 0), stop=(m == 2))
                        mm.then_inc(S("apre"), 1)

                sources(0, True)
                with pe.Fori(1, Q // 4) as i:
                    sources(i, False)
                carried(5 + 5 * l, H2, scan_tile(0, 2), False)
                pe.wait_ge(S("asel"), (l + 1) * Q)
                for h in range(H):
                    for k in range(TPR):
                        t = pe.transpose(bank(h)[0:Q, k * P:(k + 1) * P], aT[:, k:T:TPR, h], ident[:, :])
                    t.then_inc(S("xT"), 1)
                carried(6 + 5 * l, H, scan_tile(0), False)
                carried(7 + 5 * l, H, scan_tile(3), True)
                carried(8 + 5 * l, H, scan_tile(0), False)
                carried(9 + 5 * l, H, scan_tile(3), True)
                pe.wait_ge(S("attn"), l + 2)
                for h in range(H):
                    for k in range(TPR):
                        t = pe.transpose(bank(h)[:, k * Q:(k + 1) * Q], scan_tile(2)[:, h, k * P:(k + 1) * P], ident[0:Q, 0:Q])
                    t.then_inc(S("wb"), 1)
                pe.wait_ge(S("wT"), H * (l + 1))
                with pe.Fori(0, 2) as half:
                    for s in range(RS):
                        pe.wait_ge(S("msg"), half * RS + l * NSUP + s + 1)
                        for gg in range(GPS):
                            g = half * (RS * GPS) + (l * Q + s * GPS + gg)
                            par = (s * GPS + gg) % 2
                            pe.wait_ge(S("sel"), g + Q + 1)
                            pe.wait_ge(S("added"), TPR * (g + Q - 1))
                            for j in range(TPR):
                                mm = pe.matmul(bank(2 + par)[:, j * P:(j + 1) * P], rows[:, s, gg * TPR + j, :],
                                               wk2[par][:, j * P:(j + 1) * P], start=True, stop=True)
                            mm.then_inc(S("sum"), 1)
                turn_sums(1 + l)

        @block.vector
        def _(v):
            c = Chain(v, S("dve"))
            carries = [0]
            roots = [0]

            def step(instruction):
                c.did(instruction)
                c.wait()

            def carry_over(n, tile, masks, row_masks, start, ops, back):
                k = carries[0]
                carries[0] += 1
                end = Q if back else 0
                c.did(v.memset(carry[0:n, end:end + 1], start))
                v.wait_ge(S("carT"), k + 1)
                run, came = carry[0:n, 1 - back:Q + 1 - back], bank(7)[0:n, 0:Q]
                if back:
                    v.tensor_tensor_scan(run[:, ::-1], row_masks[:, ::-1], came[:, ::-1], start, *ops).then_inc(S("carS"), 1)
                else:
                    v.tensor_tensor_scan(run, row_masks, came, start, *ops).then_inc(S("carS"), 1)
                v.wait_ge(S("carB"), k + 1)
                for h in range(n):
                    c.did(v.scalar_tensor_tensor(tile[:, h, :], masks, bank(7)[0:Q, P + h:P + h + 1], tile[:, h, :], *ops))
                c.wait()

            def scans(n, tile, masks, data, start, ops, back=False):
                for h in range(n):
                    o, m, x = tile[:, h, :], masks, data(h)
                    if back:
                        o, m, x = o[:, ::-1], m[:, ::-1], x[:, ::-1]
                    s = v.tensor_tensor_scan(o, m, x, start, *ops)
                    if h == n - 1:
                        s.then_inc(S("local"), 1)
                    else:
                        c.did(s)

            SUM, MAX = (ALU.mult, ALU.add), (ALU.add, ALU.max)

            def running_sum(n, tile, data):
                scans(n, tile, cont[:, :], data, 0.0, SUM)
                carry_over(n, tile, pre[:, :], rowf[0:n, 0, :], 0.0, SUM, False)

            def running_max(n, tile, data):
                scans(n, tile, pen[:, :], data, -BIG, MAX)
                carry_over(n, tile, prepen[:, :], rowf[0:n, 1, :], -BIG, MAX, False)

            def from_ends(n, tile, data):
                for h in range(n):
                    c.did(v.scalar_tensor_tensor(tile[:, h, :], contn[:, :], 1.0, data(h), ALU.is_lt, ALU.mult))
                c.wait()
                scans(n, tile, contn[:, :], lambda h: tile[:, h, :], 0.0, SUM, True)
                carry_over(n, tile, post[:, :], rowf[0:n, 2, :], 0.0, SUM, True)

            def layer_norm(X, Y, W):
                k = roots[0]
                roots[0] += 1
                sf, mf = stats[:, :, :].rearrange("p b s -> p (b s)"), mv[:, :, :].rearrange("p b s -> p (b s)")
                with v.Fori(0, NB // 5) as i:
                    for u in range(5):
                        v.bn_stats(sf[:, ds((i * 5 + u) * 6, 6)], X[:, ds((i * 5 + u) * W, W)]).then_inc(S("dve"), 1)
                c.n += NB
                c.wait()
                for b in range(NB):
                    c.did(v.bn_aggr(mv[:, b, :], stats[:, b, :]))
                c.wait()
                v.tensor_scalar(rstd[:, :], mv[:, :, 1], EPS, None, ALU.add).then_inc(S("var"), 1)
                v.wait_ge(S("std"), k + 1)
                step(v.reciprocal(rstd[:, :], rstd[:, :]))
                with v.Fori(0, NB // 5) as i:
                    for u in range(5):
                        v.tensor_scalar(Y[:, ds((i * 5 + u) * W, W)], X[:, ds((i * 5 + u) * W, W)],
                                        mf[:, ds((i * 5 + u) * 2, 1)], rstd[:, ds(i * 5 + u, 1)],
                                        ALU.subtract, ALU.mult).then_inc(S("dve"), 1)
                c.n += NB
                c.wait()

            def fl(t):
                return t.rearrange("p b f -> p (b f)")

            v.wait_ge(S("const"), NCONST)
            v.wait_ge(S("e_in"), 16 * N_E_IN)
            D, DP, DN, SR, TY, EW = [eraw[:, i, :] if i == 5 else eraw[:, i, :].bitcast(I32) for i in range(6)]
            Ei = [ef[:, i, :].bitcast(I32) for i in range(10)]
            c.did(v.memset(ef[:, 9, :], 0.0))
            c.did(v.tensor_tensor(cont[:, :], D, DP, ALU.is_equal))
            c.did(v.tensor_tensor(contn[:, :], D, DN, ALU.is_equal))
            c.did(v.tensor_copy(ef[:, 0, :], D))
            c.did(v.tensor_copy(ef[:, 1, :], SR))
            c.did(v.tensor_scalar(Ei[8], D, 7, None, ALU.arith_shift_right))
            c.did(v.tensor_scalar(Ei[7], SR, 7, None, ALU.arith_shift_right))
            c.did(v.scalar_tensor_tensor(ef[:, 4, :], SR, float(ET), TY, ALU.mult, ALU.add))
            c.wait()
            c.did(v.tensor_tensor_scan(pre[:, :], cont[:, :], ef[:, 9, :], 1.0, *SUM))
            c.did(v.tensor_tensor_scan(post[:, ::-1], contn[:, ::-1], ef[:, 9, :], 1.0, *SUM))
            c.did(v.tensor_copy(ef[:, 2, :], Ei[8]))
            c.did(v.tensor_copy(ef[:, 3, :], Ei[7]))
            c.wait()
            c.did(v.scalar_tensor_tensor(ef[:, 5, :], ef[:, 2, :], -float(P), ef[:, 0, :], ALU.mult, ALU.add))
            c.did(v.scalar_tensor_tensor(ef[:, 6, :], ef[:, 3, :], -float(P), ef[:, 1, :], ALU.mult, ALU.add))
            for k in range(TPR):
                i = v.tensor_scalar(ef[:, 7, k * P:(k + 1) * P], ef[:, 0, k * P:(k + 1) * P], ef[:, 0, k * P:k * P + 1], None, ALU.subtract)
                if k == TPR - 1:
                    i.then_inc(S("ef"), 1)
                else:
                    c.did(i)
            c.wait()
            v.tensor_copy(ef[:, 8, 0:ROW // 2].bitcast(BF16), ef[:, 6, :]).then_inc(S("lo_ready"), 1)
            c.did(v.tensor_scalar(pen[:, :], cont[:, :], -1.0, BIG, ALU.add, ALU.mult))
            c.did(v.tensor_scalar(prepen[:, :], pre[:, :], -1.0, BIG, ALU.add, ALU.mult))
            c.wait()
            c.did(v.tensor_copy(flags[:, 0, :], pre[:, ROW - 1:ROW].to_broadcast([Q, H2])))
            c.did(v.tensor_copy(flags[:, 1, :], prepen[:, ROW - 1:ROW].to_broadcast([Q, H2])))
            v.tensor_copy(flags[:, 2, :], post[:, 0:1].to_broadcast([Q, H2])).then_inc(S("flags"), 1)
            for a, t in enumerate((kvT, srcT, relT, loT, hiT, shiT)):
                v.wait_ge(S("efT"), a + 1)
                v.tensor_copy(t[:, :].rearrange("p (q k) -> p k q", k=TPR), bank(a)[:, 0:T].rearrange("p (k q) -> p k q", k=TPR)).then_inc(S("ef_sb"), 1)
            v.wait_ge(S("flT"), 1)
            v.tensor_copy(rowf[:, :, :], bank(6)[0:H2, 0:3 * Q].rearrange("p (a q) -> p a q", a=3)).then_inc(S("ef_sb"), 1)

            v.wait_ge(S("w_in"), 16 * 21)
            ab = wk[:, 0:2 * P].rearrange("p (a f) -> p a f", a=2)
            pr = wk[:, 2 * P:5 * P].rearrange("p (a f) -> p a f", a=3)
            step(v.tensor_reduce(smal[:, 0:2], ab, AX.X, ALU.add))
            step(v.tensor_scalar(smal[:, 0:2], smal[:, 0:2], 1.0 / P, None, ALU.mult))
            for i in range(2):
                c.did(v.tensor_scalar(ab[:, i, :], ab[:, i, :], smal[:, i:i + 1], None, ALU.subtract))
            c.wait()
            c.did(v.tensor_tensor(pr[:, 0, :], ab[:, 0, :], ab[:, 0, :], ALU.mult))
            c.did(v.tensor_tensor(pr[:, 1, :], ab[:, 0, :], ab[:, 1, :], ALU.mult))
            c.did(v.tensor_tensor(pr[:, 2, :], ab[:, 1, :], ab[:, 1, :], ALU.mult))
            c.wait()
            step(v.tensor_reduce(smal[:, 2:5], pr, AX.X, ALU.add))
            c.did(v.tensor_scalar(smal[:, 2:5], smal[:, 2:5], 1.0 / P, None, ALU.mult))
            c.wait()
            step(v.tensor_scalar(smal[:, 3:4], smal[:, 3:4], 2.0, None, ALU.mult))
            va, cab, vb = (smal[0:Q, i:i + 1] for i in (2, 3, 4))
            v.wait_ge(S("lo_out"), 16)
            v.wait_ge(S("efT"), 6)
            step(v.tensor_scalar(ef[:, 1, :], EW, va, cab, ALU.mult, ALU.add))
            step(v.tensor_tensor(ef[:, 1, :], ef[:, 1, :], EW, ALU.mult))
            step(v.tensor_scalar(ef[:, 1, :], ef[:, 1, :], vb, 0.0, ALU.add, ALU.max))
            v.tensor_scalar(ef[:, 1, :], ef[:, 1, :], EPS, None, ALU.add).then_inc(S("rvar"), 1)
            step(v.tensor_reduce(lhm[:, :], lhs2[:, :], AX.X, ALU.add))
            step(v.tensor_scalar(lhm[:, :], lhm[:, :], 1.0 / P, None, ALU.mult))
            step(v.tensor_scalar(lhs2[:, :], lhs2[:, :], lhm[:, 0:1], None, ALU.subtract))
            step(v.tensor_tensor(lhs2[:, :], lhs2[:, :], lnwb[:, :], ALU.mult))
            tw4 = tmpw[:, 0:4 * P].rearrange("p (a f) -> p a f", a=4)
            step(v.tensor_tensor(tw4[:, 0:2, :], tw4[:, 0:2, :], tw4[:, 2:4, :], ALU.mult))
            v.tensor_reduce(Wm[:, :, :], tw4[:, 0:2, :].rearrange("p a (h c) -> p a h c", c=C), AX.X, ALU.add).then_inc(S("Wm"), 1)
            for t in range(ET):
                i = v.tensor_scalar(wedge[:, t * P:(t + 1) * P], wedge[:, t * P:(t + 1) * P], smal[:, 8 + t:9 + t], P ** -0.5, ALU.mult, ALU.mult)
                if t == ET - 1:
                    i.then_inc(S("we"), 1)
                else:
                    c.did(i)
            v.wait_ge(S("rstd0"), 1)
            step(v.reciprocal(ef[:, 1, :], ef[:, 1, :]))
            v.tensor_tensor(ef[:, 0, :], ef[:, 1, :], EW, ALU.mult).then_inc(S("rate_ready"), 1)

            v.wait_ge(S("x_in"), 32)
            layer_norm(fl(nodes[0]), fl(nodes[1]), P)
            v.tensor_scalar(fl(nodes[1]), fl(nodes[1]), 0.0, None, ALU.max).then_inc(S("tsrc"), 1)
            v.wait_ge(S("nt_in"), 16)
            ntb = fl(nodes[2]).bitcast(I32)
            v.wait_ge(S("tr_sb"), NG)
            v.wait_ge(S("rate_out"), 16)
            v.wait_ge(S("zero_out"), 32)
            if NW > N:
                for t in range(NT):
                    c.did(v.memset(hTt[t][:, N:NW], 0.0))
            for t in range(NT):
                v.scalar_tensor_tensor(hTt[t][:, 0:N], ntb[:, 0:N], float(t), KT[:, 0:N], ALU.is_equal, ALU.mult).then_inc(S("hTt"), 1)
            v.memset(QT[:, NW:NWP], 0.0).then_inc(S("qtpad"), 1)

            def kv(b, h, i):
                v.wait_ge(S("kv"), b + 1)
                if i is not None:
                    v.wait_ge(S(f"kv_out{h}"), 16 * i)
                v.tensor_copy(stg[h][:, 0:ET // 2, 0:P], bank(2 * h).rearrange("p (t f) -> p t f", f=P)).then_inc(S("kv_dve"), 1)

            for h in range(2):
                kv(h, h, None)
            with v.Fori(1, (NB - 1) // 2) as i:
                for h in range(2):
                    kv(2 * i + h, h, i)
            kv(NB - 1, 0, (NB - 1) // 2)

            v.wait_ge(S("kv_out0"), 16 * (NB // 2 + 1))
            v.wait_ge(S("kv_out1"), 16 * (NB // 2))

            def walk1(i, first):
                for gg in range(2 * GPS):
                    g = 2 * GPS * i + gg
                    if not (first and gg < 2):
                        v.wait_ge(S("hist"), g - 1)
                    v.tensor_tensor(ohh[gg % 2][:, :, :], bc(iota16[:, 0:NB], 1, [P, TPR, NB]),
                                    bc(hiT[:, ds(g * TPR, TPR)], 2, [P, TPR, NB]), ALU.is_equal)
                    v.tensor_tensor(oh16[gg % 2][:, :].rearrange("p (j f) -> p j f", f=P), bc(iota16[:, :], 1, [P, TPR, P]),
                                    bc(loT[:, ds(g * TPR, TPR)], 2, [P, TPR, P]), ALU.is_equal).then_inc(S("oh"), 1)
                    if not (first and gg < 1):
                        v.wait_ge(S("m3"), g)
                        if gg % GPS == 1 and not (first and gg < GPS):
                            v.wait_ge(S("ae_out"), 16 * (2 * i + gg // GPS))
                        v.tensor_copy(aeb[:, (gg - 1) % GPS * ROW:((gg - 1) % GPS + 1) * ROW], bank(6)[0:H2, :]).then_inc(S("ae"), 1)
                    v.wait_ge(S("kq"), g + 1)
                    for j in range(TPR):
                        G = bank(2 + gg % 2)[:, j * P:(j + 1) * P]
                        s = v.scalar_tensor_tensor(G, iota[:, :], relT[:, ds(g * TPR + j, 1)], G, ALU.is_equal, ALU.mult,
                                                   accum_out=aT[:, ds(g * TPR + j, 1), 0])
                    s.then_inc(S("score"), 1)

            walk1(0, True)
            with v.Fori(1, NSUP // 2) as i:
                walk1(i, False)
            v.wait_ge(S("m3"), Q)
            v.tensor_copy(aeb[:, (GPS - 1) * ROW:GPS * ROW], bank(6)[0:H2, :]).then_inc(S("ae"), 1)

            v.wait_ge(S("hist"), Q)
            v.tensor_copy(deg[:, :], bank(7)[:, 0:NB]).then_inc(S("deg"), 1)
            v.wait_ge(S("cum"), 1)
            step(v.tensor_tensor_scan(nb_[:, :], ones[:, 0:NB], bank(6)[:, 32:32 + NB], 0.0, *SUM))
            step(v.tensor_tensor(nb_[:, :], nb_[:, :], bank(6)[:, 32:32 + NB], ALU.subtract))
            step(v.tensor_tensor(nb_[:, :], nb_[:, :], bank(6)[:, 0:NB], ALU.add))
            v.tensor_scalar(endi[:, :], nb_[:, :], -1.0, None, ALU.add).then_inc(S("endi"), 1)
            v.tensor_tensor(starti[:, :], nb_[:, :], deg[:, :], ALU.subtract).then_inc(S("endi"), 1)

            X, M, Z = (scan_tile(i)[:, 0:1, :] for i in range(3))
            v.wait_ge(S("scT"), 1)
            step(v.tensor_copy(X[:, 0, :], bank(0)[0:Q, :]))
            running_max(1, M, lambda h: X[:, 0, :])
            step(v.tensor_scalar(M[:, 0, :], M[:, 0, :], -1e9, None, ALU.max))
            from_ends(1, Z, lambda h: M[:, 0, :])
            v.tensor_tensor(X[:, 0, :], X[:, 0, :], Z[:, 0, :], ALU.subtract).then_inc(S("xm"), 1)
            v.wait_ge(S("exp"), 1)
            running_sum(1, M, lambda h: X[:, 0, :])
            from_ends(1, Z, lambda h: M[:, 0, :])
            step(v.tensor_scalar(Z[:, 0, :], Z[:, 0, :], 1e-10, None, ALU.add))
            step(v.reciprocal(Z[:, 0, :], Z[:, 0, :]))
            v.tensor_tensor(X[:, 0, :], X[:, 0, :], Z[:, 0, :], ALU.mult).then_inc(S("attn"), 1)
            v.wait_ge(S("wb"), 1)
            v.tensor_copy(aT[:, :, 0].rearrange("p (q k) -> p k q", k=TPR), bank(0)[:, 0:T].rearrange("p (k q) -> p k q", k=TPR)).then_inc(S("sm0"), 1)

            v.wait_ge(S("ae_in"), 16)
            running_sum(H2, scan_tile(2, 2), lambda h: scan_tile(0, 2)[:, h, :])
            v.tensor_copy(scan_tile(0, 2).rearrange("p h c -> p (h c)").rearrange("p (c h) -> p h c", h=H2),
                          scan_tile(2, 2)).then_inc(S("mae1"), 1)

            v.wait_ge(S("acc0"), 1)
            v.wait_ge(S("sm0"), 1)

            def windows(g):
                return nc.values_load_multi_w_load_instructions(
                    d0[0:1, ds(g * TPR, 2 * TPR)], engines=[mybir.EngineType.DVE], min_val=0, max_val=NW,
                    skip_runtime_bounds_check_because="destinations are nodes")[1]

            def add(n0, g, par, w):
                v.wait_ge(S("sum"), n0 + g + 1)
                for j in range(TPR):
                    n = (n0 + g) * TPR + j
                    if not (isinstance(n, int) and n == 0):
                        v.wait_ge(S("added"), n)
                    a = acc[:, ds(w[j], P)]
                    v.tensor_tensor(a, a, bank(2 + par)[:, j * P:(j + 1) * P], ALU.add).then_inc(S("added"), 1)

            def walk2(i, first):
                for h in range(2):
                    w = [None, None]
                    for gg in range(GPS):
                        g = 2 * GPS * i + h * GPS + gg
                        if not (first and h == 0 and gg < 2):
                            v.wait_ge(S("sum"), g - 1)
                        for j in range(TPR):
                            s = v.tensor_scalar(wk2[gg % 2][:, j * P:(j + 1) * P], iota[:, :], relT[:, ds(g * TPR + j, 1)],
                                                aT[:, ds(g * TPR + j, 1), 0], ALU.is_equal, ALU.mult)
                        s.then_inc(S("sel"), 1)
                        if gg > 0:
                            add(0, g - 1, (gg - 1) % 2, w[(gg - 1) // 2 % 2][(gg - 1) % 2 * TPR:])
                        if gg % 2 == 0:
                            w[gg // 2] = windows(g)
                    add(0, g, (GPS - 1) % 2, w[1][TPR:])

            v.wait_ge(S("d0_in"), 16)
            walk2(0, True)
            with v.Fori(1, NSUP // 2) as i:
                walk2(i, False)

            def take_sums(k):
                for g in range(NG):
                    v.wait_ge(S("accT"), k * NG + g + 1)
                    n = min(4, NB - 4 * g) * P
                    a = fl(nodes[0])[:, 4 * g * P:4 * g * P + n]
                    v.tensor_tensor(a, a, bank((k * NG + g) % 2)[:, 0:n], ALU.add).then_inc(S("x1"), 1)
                v.wait_ge(S("x1"), (k + 1) * NG)

            v.wait_ge(S("x_in"), 64)
            take_sums(0)

            v.wait_ge(S("sums_in"), 16 * NB)
            step(v.tensor_scalar(nb_[:, :], deg[:, :], 1.0, None, ALU.max))
            step(v.reciprocal(nb_[:, :], nb_[:, :]))
            step(v.tensor_tensor(mae[:, :, :], ncol[:, :, :], bc(nb_[:, :], 2, [P, NB, H2]), ALU.mult))

            layer_norm(fl(nodes[0]), fl(nodes[1]), P)
            v.tensor_scalar(fl(nodes[1]), fl(nodes[1]), 0.0, None, ALU.max).then_inc(S("tsrc"), 1)
            v.wait_ge(S("ip_in"), 16 * 8)
            b1, lw, lb = (ipv[:, i * KV:(i + 1) * KV] for i in range(3))
            b2, pw, pb = (ipv[:, 3 * KV + i * P:3 * KV + (i + 1) * P] for i in range(3))
            for g in range(-(-NB // 2)):
                n = min(2, NB - 2 * g)
                v.wait_ge(S("z"), g + 1)
                v.tensor_tensor(zt[:, 2 * g:2 * g + n, :], bank(2 + g % 2)[:, 0:n * KV].rearrange("p (b f) -> p b f", f=KV),
                                bc(b1, 1, [P, n, KV]), ALU.add).then_inc(S("z_sb"), 1)
            v.wait_ge(S("z_sb"), -(-NB // 2))
            step(v.tensor_scalar(fl(zt), fl(zt), 0.0, None, ALU.max))
            layer_norm(fl(zt), fl(zt), KV)
            step(v.tensor_tensor(zt, zt, bc(lw, 1, [P, NB, KV]), ALU.mult))
            v.tensor_tensor(zt, zt, bc(lb, 1, [P, NB, KV]), ALU.add).then_inc(S("tsrc"), 2)
            for g in range(NG):
                n = min(4, NB - 4 * g)
                v.wait_ge(S("y"), g + 1)
                v.tensor_tensor(nodes[1][:, 4 * g:4 * g + n, :], bank(2 + g % 2)[:, 0:n * P].rearrange("p (b f) -> p b f", f=P),
                                bc(b2, 1, [P, n, P]), ALU.add).then_inc(S("y_sb"), 1)
            v.wait_ge(S("y_sb"), NG)
            v.wait_ge(S("x1_out"), 16)
            layer_norm(fl(nodes[1]), fl(nodes[0]), P)
            step(v.tensor_tensor(nodes[0], nodes[0], bc(pw, 1, [P, NB, P]), ALU.mult))
            step(v.tensor_tensor(nodes[0], nodes[0], bc(pb, 1, [P, NB, P]), ALU.add))
            v.tensor_scalar(fl(nodes[0]), fl(nodes[0]), 0.0, 10.0, ALU.max, ALU.min).then_inc(S("tsrc"), 1)

            for l in range(2):
                v.wait_ge(S("gw_in"), 48 * (l + 1))
                att = wk[:, 0:2 * P].rearrange("p (a f) -> p a f", a=2)
                step(v.tensor_tensor(att, att, bc(Wx[:, 0:P], 1, [P, 2, P]), ALU.mult))
                v.tensor_reduce(Wx[:, P:P + H2].rearrange("p (a h) -> p a h", a=2), att.rearrange("p a (h c) -> p a h c", c=C),
                                AX.X, ALU.add).then_inc(S("Wx"), 1)
                for g in range(NGG):
                    n = min(3, NB - 3 * g)
                    v.wait_ge(S("hwp"), l * NGG + g + 1)
                    got = bank(2 + (l * NGG + g) % 2)[:, 0:n * (P + H2)].rearrange("p (b f) -> p b f", f=P + H2)
                    c.did(v.tensor_copy(ncol[:, 3 * g:3 * g + n, :], got[:, :, P:P + H2]))
                    v.tensor_copy(nodes[1][:, 3 * g:3 * g + n, :], got[:, :, 0:P]).then_inc(S("hw"), 1)
                c.wait()
                v.tensor_copy(nst[:, :, 0:H], ncol[:, :, H:H2]).then_inc(S("nst"), 1)
                step(v.tensor_tensor(al[:, :, :], ncol[:, :, 0:H], ncol[:, :, H:H2], ALU.add))
                step(v.tensor_tensor(al[:, :, :], al[:, :, :], mae[:, :, l * H:(l + 1) * H], ALU.add))
                v.scalar_tensor_tensor(nst[:, :, H:H2], al[:, :, :], 0.2, al[:, :, :], ALU.mult, ALU.max).then_inc(S("nst"), 1)
                a3 = a3r[:, :].rearrange("p (b h) -> p b h", h=H)
                step(v.tensor_copy(a3, ncol[:, :, 0:H]))
                for m in range(2):
                    step(v.tensor_copy(A3[:, m, :], a3r[:, :]))
                    step(v.tensor_tensor(a3r[:, :], a3r[:, :], A3[:, m, :], ALU.subtract))
                v.tensor_copy(A3[:, 2, :], a3r[:, :]).then_inc(S("A3"), 1)

                def select(g, gg):
                    v.wait_ge(S("apre"), l * Q + g + 1)
                    prod = wk2[gg % 2][:, 0:TPR * NB * H].rearrange("p (j b h) -> p j b h", j=TPR, h=H)
                    v.tensor_tensor(prod, bank(gg % 2)[:, 0:TPR * NB * H].rearrange("p (j b h) -> p j b h", j=TPR, h=H),
                                    bc(ohh[gg % 2][:, :, :], 3, [P, TPR, NB, H]), ALU.mult).then_inc(S("prod"), 1)
                    v.wait_ge(S("prod"), l * Q + g + 1)
                    v.tensor_reduce(aT[:, ds(g * TPR, TPR), :], prod.rearrange("p j b h -> p j h b"), AX.X, ALU.add).then_inc(S("asel"), 1)

                def sources(i, first):
                    for gg in range(4):
                        g = 4 * i + gg
                        if gg % 2 == 0:
                            v.wait_ge(S(f"lo_in{gg // 2}"), 16 * (l * (Q // 4) + i + 1))
                        if not (first and gg < 2):
                            v.wait_ge(S("apre"), l * Q + g - 1)
                            v.wait_ge(S("asel"), l * Q + g - 1)
                        v.tensor_tensor(ohh[gg % 2][:, :, :], bc(iota16[:, 0:NB], 1, [P, TPR, NB]),
                                        bc(shiT[:, ds(g * TPR, TPR)], 2, [P, TPR, NB]), ALU.is_equal)
                        v.tensor_scalar(oh16[gg % 2][:, :], src16[gg // 2][:, gg % 2 * ROW:(gg % 2 + 1) * ROW], ipart[:, 0:1], None,
                                        ALU.is_equal).then_inc(S("oh"), 1)
                        if not (first and gg == 0):
                            select(g - 1, gg + 1)

                sources(0, True)
                with v.Fori(1, Q // 4) as i:
                    sources(i, False)
                select(Q - 1, 1)
                c.did(v.memset(acc[:, :], 0.0))

                v.wait_ge(S("start_in"), 16 * (l + 1))
                V8 = scan_tile(2, 2).rearrange("p h c -> p (h c)").rearrange("p (c h) -> p c h", h=H2)
                AD, L, X, M = (scan_tile(i) for i in range(4))
                running_sum(H2, scan_tile(0, 2), lambda h: V8[:, :, h])
                for h in range(H):
                    v.wait_ge(S("xT"), l * H + h + 1)
                    i = v.tensor_tensor(X[:, h, :], bank(h)[0:Q, :], AD[:, h, :], ALU.add)
                    if h == H - 1:
                        i.then_inc(S("held"), 1)
                    else:
                        c.did(i)
                v.wait_ge(S("held"), l + 1)
                v.wait_ge(S("ael_in"), 16 * (l + 1))
                step(v.tensor_tensor(X, X, M, ALU.add))
                step(v.scalar_tensor_tensor(X, X, 0.2, X, ALU.mult, ALU.max))
                running_max(H, AD, lambda h: X[:, h, :])
                from_ends(H, M, lambda h: AD[:, h, :])
                step(v.tensor_tensor(M, M, L, ALU.max))
                v.tensor_tensor(X, X, M, ALU.subtract).then_inc(S("xm"), 1)
                v.tensor_tensor(L, L, M, ALU.subtract).then_inc(S("elm"), 1)
                v.wait_ge(S("exp"), 2 + 2 * l)
                running_sum(H, AD, lambda h: X[:, h, :])
                from_ends(H, M, lambda h: AD[:, h, :])
                v.wait_ge(S("exp"), 3 + 2 * l)
                step(v.tensor_tensor(M, M, L, ALU.add))
                step(v.tensor_scalar(M, M, 1e-16, None, ALU.add))
                step(v.reciprocal(M, M))
                v.tensor_tensor(X, X, M, ALU.mult).then_inc(S("attn"), 1)
                v.tensor_tensor(AD.rearrange("p h c -> p (h c)").rearrange("p (c h) -> p h c", h=H), L, M, ALU.mult).then_inc(S("el"), 1)
                for h in range(H):
                    v.wait_ge(S("wb"), 1 + l * H + h + 1)
                    v.tensor_copy(aT[:, :, h].rearrange("p (q k) -> p k q", k=TPR),
                                  bank(h)[:, 0:T].rearrange("p (k q) -> p k q", k=TPR)).then_inc(S("wT"), 1)
                v.wait_ge(S("wT"), H * (l + 1))
                c.wait()

                n0 = (1 + l) * Q
                with v.Fori(0, 2) as half:
                    for s in range(RS):
                        v.wait_ge(S(f"row{s}"), (half + 2 * l + 1) * 16 * SUP)
                        r = rows[:, s, :, :].rearrange("p j (h c) -> p j h c", c=C)
                        v.tensor_tensor(r, r, bc(aT[:, ds(half * (RS * SUP) + s * SUP, SUP), :], 3, [P, SUP, H, C]), ALU.mult).then_inc(S("msg"), 1)
                        w = [None, None]
                        for gg in range(GPS):
                            g = half * (RS * GPS) + (s * GPS + gg)
                            v.wait_ge(S("sum"), g + (n0 - 1))
                            for j in range(TPR):
                                i = v.tensor_scalar(wk2[gg % 2][:, j * P:(j + 1) * P], iota[:, :], relT[:, ds(g * TPR + j, 1)], None, ALU.is_equal)
                            i.then_inc(S("sel"), 1)
                            if gg > 0:
                                add(n0, g - 1, (gg - 1) % 2, w[(gg - 1) // 2][(gg - 1) % 2 * TPR:])
                            if gg % 2 == 0:
                                w[gg // 2] = windows(g)
                        add(n0, g, (GPS - 1) % 2, w[1][TPR:])

                bias, nw, nb = (vec6[:, 3 * l + i, :] for i in range(3))
                v.wait_ge(S("back_in"), 32 * (l + 1))
                v.wait_ge(S("al_in"), 16 * NB * (l + 1))
                r = fl(nodes[1]).rearrange("p (b h c) -> p b h c", h=H, c=C)
                step(v.tensor_tensor(r, r, bc(al[:, :, :], 3, [P, NB, H, C]), ALU.mult))
                step(v.tensor_tensor(nodes[1], nodes[1], bc(bias, 1, [P, NB, P]), ALU.add))
                v.tensor_tensor(nodes[0], nodes[0], nodes[1], ALU.add).then_inc(S("mixed"), 1)
                v.wait_ge(S("mixed"), l + 1)
                take_sums(1 + l)
                step(v.tensor_scalar(fl(nodes[0]), fl(nodes[0]), -10.0, 10.0, ALU.max, ALU.min))
                layer_norm(fl(nodes[0]), fl(nodes[0]), P)
                step(v.tensor_tensor(nodes[0], nodes[0], bc(nw, 1, [P, NB, P]), ALU.mult))
                step(v.tensor_tensor(nodes[0], nodes[0], bc(nb, 1, [P, NB, P]), ALU.add))
                v.tensor_scalar(fl(nodes[2]), fl(nodes[0]), 0.0, None, ALU.min).then_inc(S("elu"), 1)
                step(v.tensor_scalar(fl(nodes[0]), fl(nodes[0]), 0.0, None, ALU.max))
                v.wait_ge(S("elu_e"), l + 1)
                e = v.scalar_tensor_tensor(fl(nodes[0]), fl(nodes[2]), -1.0, fl(nodes[0]), ALU.add, ALU.add)
                if l == 0:
                    e.then_inc(S("tsrc"), 1)
                else:
                    step(e)
            v.wait_ge(S("x1_in"), 16)
            v.tensor_tensor(nodes[0], nodes[0], nodes[1], ALU.add).then_inc(S("final"), 1)


def kernel(**inputs):
    import numpy as _np
    import concourse.bacc as _bacc
    from concourse import mybir as _mybir
    from concourse.bass_utils import run_bass_kernel_spmd as _run

    nc = _bacc.Bacc("TRN2", target_bir_lowering=False, num_devices=1)
    arrays, aps = {}, {}
    for name, value in inputs.items():
        a = _np.ascontiguousarray(value)
        arrays["in_" + name] = a
        aps[name] = nc.dram_tensor("in_" + name, a.shape, _mybir.dt.from_np(a.dtype), kind="ExternalInput").ap()
    out = nc.dram_tensor("out_x", inputs["x"].shape, _mybir.dt.float32, kind="ExternalOutput").ap()
    build(nc, aps, out)
    r = _run(nc, [arrays], core_ids=[0])
    return r.results[0]["out_x"]
```

```python
import concourse.bass as bass
from concourse import mybir
from contextlib import ExitStack

F32 = mybir.dt.float32
BF16 = mybir.dt.bfloat16
I32 = mybir.dt.int32
ALU = mybir.AluOpType
ACT = mybir.ActivationFunctionType
AX = mybir.AxisListType
ds = bass.ds

P = 128
BIG = 1e30
NOWHERE = 8000


class Chain:

    def __init__(self, eng, sem):
        self.eng, self.sem, self.n = eng, sem, 0

    def did(self, instruction):
        instruction.then_inc(self.sem, 1)
        self.n += 1

    def wait(self):
        self.eng.wait_ge(self.sem, self.n)


def build(nc, A, out):
    N = A["x"].shape[0]
    E = A["src"].shape[0]
    NB = -(-N // P)
    LAST = N - (NB - 1) * P
    ROW = 512
    Q = -(-E // ROW)
    TPR = ROW // P
    T = Q * TPR
    EP = Q * ROW
    LROW = E - (Q - 1) * ROW
    NT = A["L0_gnn_W_Q"].shape[0]
    ET = A["L0_gnn_W_edge"].shape[0]
    H = A["L1_gnn_g1_att_src"].shape[0]
    C = P // H
    H2 = 2 * H
    NW = NB * P
    NWP = NW + P
    KV = 2 * P
    SUP = 16
    GPS = SUP // TPR
    NSUP = T // SUP
    RS = NSUP // 2
    NG = -(-NB // 4)
    EPS = 1e-5
    HALF = 1536
    NGG = -(-NB // 3)
    PAIRS = T // 2
    PPS = SUP // 2
    NCONST, N_E_IN, N_W_IN = 10, 13, 21
    assert EP == T * P and T % (2 * SUP) == 0 and RS * 2 == NSUP and NWP <= NOWHERE

    def dram(name, shape, dt=F32):
        return nc.dram_tensor(name, shape, dt).ap()

    kv_table = dram("kv_table", (N * ET, KV))
    v_spill = dram("v_spill", (NSUP, P, SUP * P))
    row_table = [dram(f"row_table{l}", (N, P)) for l in range(2)]
    rate_d = dram("rate_d", (2, EP))
    aedge_d = dram("aedge_d", (H2, EP))
    ends_d = dram("ends_d", (EP, H2))
    starts_d = [dram(f"starts_d{l}", (EP, H2)) for l in range(2)]
    loops_d = [dram(f"loops_d{l}", (EP, H2)) for l in range(2)]
    lo_d = dram("lo_d", (1, EP), BF16)
    x1_d = dram("x1_d", (P, NW))
    res_d = dram("res_d", (P, NW))
    hw_d = dram("hw_d", (P, NW))

    ctx = ExitStack()
    with ctx:
        def sb(name, shape, dt=F32):
            return ctx.enter_context(nc.sbuf_tensor(name, shape, dt))

        sems = {}

        def S(name):
            if name not in sems:
                sems[name] = ctx.enter_context(nc.semaphore(name))
            return sems[name]

        ps = ctx.enter_context(nc.psum_tensor("ps", [P, 8, 512], F32))

        def bank(i):
            return ps[:, i, :]

        acc = ps[:, :, :].rearrange("p b c -> p (b c)")[:, 0:NWP]

        ring = sb("ring", [P, RS * SUP * P])
        weights = sb("weights", [P, (3 * NT + ET + 4) * P])
        node = sb("node", [P, 3 * NW])
        nodes = [node[:, i * NW:(i + 1) * NW].rearrange("p (b f) -> p b f", f=P) for i in range(3)]

        def scan_tile(i, n=1):
            return node[0:Q, i * H * ROW:(i + n) * H * ROW].rearrange("p (h c) -> p h c", c=ROW)

        def cut(at, n):
            return ring[:, at:at + n]

        hTt = [cut(i * NW, NW) for i in range(NT)]
        KT = cut(NT * NW, NW)
        QT = cut((NT + 1) * NW, NWP)
        free0 = (NT + 1) * NW + NWP
        stg = [cut(free0 + i * ET * KV, ET * KV).rearrange("p (t f) -> p t f", f=KV) for i in range(2)]
        free1 = free0 + 2 * ET * KV
        eraw = ring[0:Q, free1:free1 + 6 * ROW].rearrange("p (a c) -> p a c", c=ROW)
        assert free1 + 6 * ROW <= RS * SUP * P
        ef = node[0:Q, 0:10 * ROW].rearrange("p (a c) -> p a c", c=ROW)
        zero_rows = node[0:Q, 10 * ROW:10 * ROW + H2 * ROW]
        kv_buf = [cut(i * SUP * KV, SUP * KV).rearrange("p (j f) -> p j f", f=KV) for i in range(2)]
        at = 2 * SUP * KV
        kTb = [cut(at + i * ROW, ROW) for i in range(2)]
        hid = [cut(at + (2 + i) * ROW, ROW) for i in range(2)]
        tw = [cut(at + (4 + i) * ROW, ROW) for i in range(2)]
        assert at + 6 * ROW <= (NT + 1) * NW
        aeb = ring[0:H2, free0:free0 + GPS * ROW]
        rateb = [ring[0:2, at + 6 * ROW + i * GPS * ROW:at + 6 * ROW + (i + 1) * GPS * ROW] for i in range(2)]
        assert at + 6 * ROW + 2 * GPS * ROW <= (NT + 1) * NW
        v_buf = [cut(i * SUP * P, SUP * P).rearrange("p (j f) -> p j f", f=P) for i in range(2)]
        zt = cut(0, NB * KV).rearrange("p (b f) -> p b f", f=KV)
        zT = [cut(NB * KV + i * NW, NW) for i in range(2)]
        hT = cut(NB * KV + 2 * NW, NW)
        rows = ring[:, :].rearrange("p (s j f) -> p s j f", s=RS, f=P)
        wqkv = weights[:, 0:3 * NT * P].rearrange("p (m t f) -> p m t f", m=3, t=NT)
        wedge = weights[:, 3 * NT * P:(3 * NT + ET) * P]
        tmpw = weights[:, (3 * NT + ET) * P:(3 * NT + ET + 4) * P]
        ipw1 = weights[:, 0:KV]
        ipw2 = weights[:, KV:2 * KV].rearrange("p (a f) -> p a f", a=2)
        ipv = weights[:, 2 * KV:2 * KV + 9 * P]

        ident = sb("ident", [P, P])
        iota = sb("iota", [P, 2 * P])
        iota16 = sb("iota16", [P, P], BF16)
        ipart = sb("ipart", [P, 1])
        tri = sb("tri", [P, P])
        ones = sb("ones", [P, P])
        eps_t = sb("eps_t", [P, 1])
        cont = sb("cont", [Q, ROW], BF16)
        contn = sb("contn", [Q, ROW], BF16)
        pre = sb("pre", [Q, ROW], BF16)
        post = sb("post", [Q, ROW], BF16)
        pen = sb("pen", [Q, ROW], BF16)
        prepen = sb("prepen", [Q, ROW], BF16)
        rowf = sb("rowf", [H2, 3, Q])
        flags = sb("flags", [Q, 3, H2])
        carry = sb("carry", [H2, Q + 1])
        relT = sb("relT", [P, T])
        relbT = sb("relbT", [P, T])
        kvT = sb("kvT", [P, T], I32)
        srcT = sb("srcT", [P, T], I32)
        loT = sb("loT", [P, T], BF16)
        hiT = sb("hiT", [P, T], BF16)
        shiT = sb("shiT", [P, T], BF16)
        idx = sb("idx", [P, RS * SUP], I32)
        d0 = sb("d0", [1, T], I32)
        b0 = sb("b0", [1, T], I32)
        aT = sb("aT", [P, T, H])
        endi = sb("endi", [P, NB], I32)
        starti = sb("starti", [P, NB], I32)
        deg = sb("deg", [P, NB])
        mae = sb("mae", [P, NB, H2])
        ncol = sb("ncol", [P, NB, H2])
        nst = sb("nst", [P, NB, H2])
        al = sb("al", [P, NB, H2])
        stats = sb("stats", [P, NB, 6])
        mv = sb("mv", [P, NB, 2])
        rstd = sb("rstd", [P, NB])
        vec6 = sb("vec6", [P, 6, P])
        Wx = sb("Wx", [P, P + H2])
        Wm = sb("Wm", [P, 2, H])
        taw2 = sb("taw2", [P, P])
        lhs2 = sb("lhs2", [2, P])
        lnwb = sb("lnwb", [2, P])
        tacol = sb("tacol", [P, 2])
        wk = sb("wk", [P, 2 * ROW])
        wk2 = [wk[:, i * ROW:(i + 1) * ROW] for i in range(2)]
        src16 = [sb(f"src16_{i}", [P, 2 * ROW], BF16) for i in range(2)]
        oh16 = [sb(f"oh16_{i}", [P, ROW], BF16) for i in range(2)]
        ohh = [sb(f"ohh{i}", [P, TPR, NB], BF16) for i in range(2)]
        A3 = sb("A3", [P, 3, NB * H], BF16)
        a3r = sb("a3r", [P, NB * H])
        smal = sb("smal", [P, 16])
        nb_ = sb("nb_", [P, NB])
        ticks = sb("ticks", [P, 4])
        lhm = sb("lhm", [2, 1])
        blk = sb("blk", [Q, TPR])

        block = ctx.enter_context(nc.Block())

        def row_of(ap):
            return ap.rearrange("(a n) -> a n", a=1)

        def spread(ap, n=P):
            return row_of(ap).to_broadcast([n, ap.shape[0]])

        def node_blocks(table, f=P):
            return (table[0:(NB - 1) * P, :].rearrange("(b p) f -> p b f", p=P), table[(NB - 1) * P:N, :])

        def bc(ap, axis, shape):
            return ap.unsqueeze(axis).to_broadcast(shape)

        @block.sync
        def _(sp):
            D, DP, DN, SR, TY, EW = [eraw[:, i, :] if i == 5 else eraw[:, i, :].bitcast(I32) for i in range(6)]
            xa, xb = node_blocks(A["x"])
            sp.dma_start(nodes[0][:, 0:NB - 1, :], xa).then_inc(S("x_in"), 16)
            sp.wait_ge(S("xpad"), 1)
            sp.dma_start(nodes[0][0:LAST, NB - 1, :], xb).then_inc(S("x_in"), 16)
            sp.wait_ge(S("epad"), 2)

            def edges(dst, src, shift):
                if shift < 0:
                    sp.dma_start(dst[0:1, 1:ROW], src[0:ROW - 1].unsqueeze(0)).then_inc(S("e_in"), 16)
                    sp.dma_start(dst[1:Q - 1, :], src[ROW - 1:(Q - 1) * ROW - 1].rearrange("(q c) -> q c", c=ROW)).then_inc(S("e_in"), 16)
                else:
                    sp.dma_start(dst[0:Q - 1, :], src[shift:shift + (Q - 1) * ROW].rearrange("(q c) -> q c", c=ROW)).then_inc(S("e_in"), 16)
                n = LROW - shift
                sp.dma_start(dst[Q - 1:Q, 0:n], src[(Q - 1) * ROW + shift:E].unsqueeze(0)).then_inc(S("e_in"), 16)

            edges(D, A["dst"], 0)
            edges(DP, A["dst"], -1)
            edges(DN, A["dst"], 1)
            edges(SR, A["src"], 0)
            edges(TY, A["edge_type_8"], 0)
            edges(EW, A["edge_weight"], 0)
            assert 13 == N_E_IN
            with nc.allow_non_contiguous_dma("one destination per tile"):
                sp.dma_start(d0[0:1, :], A["dst"].unsqueeze(0)[:, 0:E:P]).then_inc(S("d0_in"), 16)
                sp.dma_start(tacol[:, 0:1], A["L1_gnn_ta_ln_b"].unsqueeze(1)).then_inc(S("ta_in"), 16)
                sp.dma_start(tacol[:, 1:2], A["L1_gnn_ta_b2"].unsqueeze(1)).then_inc(S("ta_in"), 16)
            sp.wait_ge(S("zeros"), 1)
            for l in range(2):
                sp.dma_start(starts_d[l].rearrange("(q c) h -> q (c h)", c=ROW), zero_rows).then_inc(S("zero_out"), 16)
            sp.wait_ge(S("lo_ready"), 1)
            sp.dma_start(lo_d.rearrange("a (q c) -> q (a c)", c=ROW), ef[:, 8, 0:ROW // 2].bitcast(BF16)).then_inc(S("lo_out"), 16)
            sp.wait_ge(S("rate_ready"), 1)
            sp.dma_start(rate_d.rearrange("a (q c) -> q a c", c=ROW), ef[:, 0:2, :]).then_inc(S("rate_out"), 16)

            def kv_store(b, h):
                sp.wait_ge(S("kv_dve"), b + 1)
                sp.wait_ge(S("kv_act"), b + 1)
                if isinstance(b, int) and b == NB - 1:
                    sp.dma_start(kv_table[b * P * ET:N * ET, :].rearrange("(p t) f -> p t f", t=ET),
                                 stg[h][0:LAST, :, :]).then_inc(S(f"kv_out{h}"), 16)
                else:
                    sp.dma_start(kv_table[ds(b * P * ET, P * ET), :].rearrange("(p t) f -> p t f", t=ET),
                                 stg[h][:, :, :]).then_inc(S(f"kv_out{h}"), 16)

            sp.wait_ge(S("rate_out"), 16)
            with sp.Fori(0, (NB - 1) // 2) as i:
                for h in range(2):
                    kv_store(2 * i + h, h)
            kv_store(NB - 1, 0)

            def walk1(i, h, first):
                s = 2 * i + h
                if not first:
                    sp.wait_ge(S("m1"), (s - 1) * GPS)
                sp.dma_start(rateb[h], rate_d[:, ds(s * GPS * ROW, GPS * ROW)]).then_inc(S(f"rate_in{h}"), 16)
                sp.wait_ge(S(f"got{h}"), (i + 1) * 16 * SUP)
                sp.dma_start(v_spill[ds(s, 1), :, :].rearrange("a p (j f) -> p (a j) f", f=P),
                             kv_buf[h][:, :, P:KV]).then_inc(S(f"spill{h}"), 16)
                if not (first and h == 0):
                    ae_store(s - 1)

            def ae_store(s):
                sp.wait_ge(S("ae"), s * GPS + GPS)
                sp.dma_start(aedge_d[:, ds(s * GPS * ROW, GPS * ROW)], aeb).then_inc(S("ae_out"), 16)

            for h in range(2):
                walk1(0, h, True)
            with sp.Fori(1, NSUP // 2) as i:
                for h in range(2):
                    walk1(i, h, False)
            ae_store(NSUP - 1)

            sp.wait_ge(S("ae_out"), 16 * NSUP)
            sp.wait_ge(S("sm0"), 1)
            sp.dma_start(scan_tile(0, 2), aedge_d.rearrange("h (q c) -> q h c", c=ROW)).then_inc(S("ae_in"), 16)
            for h in range(2):
                sp.wait_ge(S(f"spill{h}"), 16 * NSUP // 2)

            def walk2(i, h, first):
                s = 2 * i + h
                if not first:
                    sp.wait_ge(S("sum"), (s - 1) * PPS)
                sp.dma_start(v_buf[h], v_spill[ds(s, 1), :, :].rearrange("a p (j f) -> p (a j) f", f=P)).then_inc(S(f"v_in{h}"), 16)

            for h in range(2):
                walk2(0, h, True)
            sp.wait_ge(S("mae1"), 1)
            sp.dma_start(ends_d.rearrange("(q c) h -> q (c h)", c=ROW),
                         scan_tile(0, 2).rearrange("p h c -> p (h c)")).then_inc(S("ends_out"), 16)
            with sp.Fori(1, NSUP // 2) as i:
                for h in range(2):
                    walk2(i, h, False)

            sp.wait_ge(S("ends_out"), 16)
            sp.dma_start(nodes[0][:, 0:NB - 1, :], xa).then_inc(S("x_in"), 16)
            sp.dma_start(nodes[0][0:LAST, NB - 1, :], xb).then_inc(S("x_in"), 16)
            sp.wait_ge(S("x1"), 1)
            sp.dma_start(x1_d, nodes[0].rearrange("p b f -> p (b f)")).then_inc(S("x1_out"), 16)
            sp.dma_start(ipw1, A["L1_gnn_ip_w1"]).then_inc(S("ip_in"), 16)
            sp.dma_start(ipw2, A["L1_gnn_ip_w2"].rearrange("(a p) f -> p a f", p=P)).then_inc(S("ip_in"), 16)
            at_ = 0
            for name in ("ip_b1", "ip_ln_w", "ip_ln_b", "ip_b2", "pn_w", "pn_b"):
                n = A["L1_gnn_" + name].shape[0]
                sp.dma_start(ipv[:, at_:at_ + n], spread(A["L1_gnn_" + name])).then_inc(S("ip_in"), 16)
                at_ += n

            for l in range(2):
                g = f"L1_gnn_g{l + 1}_"
                sp.wait_ge(S("x1"), l + 1)
                sp.dma_start(Wx[:, 0:P], A[g + "w"]).then_inc(S("gw_in"), 16)
                sp.dma_start(wk[:, 0:P], spread(A[g + "att_src"].rearrange("h c -> (h c)"))).then_inc(S("gw_in"), 16)
                sp.dma_start(wk[:, P:2 * P], spread(A[g + "att_dst"].rearrange("h c -> (h c)"))).then_inc(S("gw_in"), 16)
                sp.wait_ge(S("tsrc"), 5 + l)
                sp.dma_start(res_d, nodes[0].rearrange("p b f -> p (b f)")).then_inc(S("res_out"), 16)
                sp.wait_ge(S("hw"), 9 * (l + 1))
                ra, rb = node_blocks(row_table[l])
                sp.dma_start(ra, nodes[1][:, 0:NB - 1, :]).then_inc(S("row_out"), 16)
                sp.dma_start(rb, nodes[1][0:LAST, NB - 1, :]).then_inc(S("row_out"), 16)
                sp.dma_start(hw_d, nodes[1].rearrange("p b f -> p (b f)")).then_inc(S("hw_out"), 16)
                def lo_in(i, h, first):
                    if not first:
                        sp.wait_ge(S("oh"), Q + l * Q + 4 * i + 2 * h - 2)
                    sp.dma_start(src16[h][:, :], lo_d[:, ds((2 * i + h) * 2 * ROW, 2 * ROW)].to_broadcast([P, 2 * ROW])).then_inc(S(f"lo_in{h}"), 16)

                for h in range(2):
                    lo_in(0, h, True)
                with sp.Fori(1, Q // 4) as i:
                    for h in range(2):
                        lo_in(i, h, False)
                sp.wait_ge(S("held"), l + 1)
                sp.dma_start(scan_tile(3), aedge_d[l * H:(l + 1) * H, :].rearrange("h (q c) -> q h c", c=ROW)).then_inc(S("ael_in"), 16)
                sp.wait_ge(S("el"), l + 1)
                sp.dma_start(loops_d[l].rearrange("(q c) h -> q (c h)", c=ROW),
                             scan_tile(2, 2).rearrange("p h c -> p (h c)")).then_inc(S("loop_out"), 16)
                sp.wait_ge(S("loop_out"), 16 * (l + 1))
                sp.wait_ge(S("wT"), H * (l + 1))
                sp.dma_start(nodes[0].rearrange("p b f -> p (b f)"), res_d).then_inc(S("back_in"), 16)
                sp.dma_start(nodes[1].rearrange("p b f -> p (b f)"), hw_d).then_inc(S("back_in"), 16)
            sp.wait_ge(S("mixed"), 2)
            sp.dma_start(nodes[1].rearrange("p b f -> p (b f)"), x1_d).then_inc(S("x1_in"), 16)
            sp.wait_ge(S("final"), 1)
            oa, ob = node_blocks(out)
            sp.dma_start(oa, nodes[0][:, 0:NB - 1, :]).then_inc(S("out"), 16)
            sp.dma_start(ob, nodes[0][0:LAST, NB - 1, :]).then_inc(S("out"), 16)
            sp.wait_ge(S("out"), 32)

        @block.gpsimd
        def _(pool):
            pool.memset(nodes[0][:, NB - 1, :], 0.0).then_inc(S("xpad"), 1)
            c = Chain(pool, S("const"))
            c.did(pool.memset(ident[:, :], 0.0))
            pool.memset(eraw[:, 0:3, :].bitcast(I32), NOWHERE).then_inc(S("epad"), 1)
            pool.memset(eraw[:, 3:6, :], 0.0).then_inc(S("epad"), 1)
            c.did(pool.memset(ticks[:, :], 0.0))
            c.did(pool.memset(tri[:, :], 1.0))
            c.did(pool.memset(ones[:, :], 1.0))
            c.did(pool.memset(ncol[:, :, :], 0.0))
            c.did(pool.iota(iota[:, :], [[1, 2 * P]], base=0, channel_multiplier=0, allow_small_or_imprecise_dtypes=True))
            c.did(pool.iota(iota16[:, :], [[1, P]], base=0, channel_multiplier=0, allow_small_or_imprecise_dtypes=True))
            c.did(pool.iota(ipart[:, :], [[0, 1]], base=0, channel_multiplier=1, allow_small_or_imprecise_dtypes=True))
            c.wait()
            c.did(pool.affine_select(out=ident[:, :], in_=ident[:, :], compare_op=ALU.not_equal, fill=1.0, base=0,
                                     pattern=[[-1, P]], channel_multiplier=1))
            c.did(pool.affine_select(out=tri[:, :], in_=tri[:, :], compare_op=ALU.is_ge, fill=0.0, base=0,
                                     pattern=[[1, P]], channel_multiplier=-1))
            assert c.n == NCONST
            pool.wait_ge(S("hTt"), 2 * NT)
            pool.memset(zero_rows, 0.0).then_inc(S("zeros"), 1)

            def tick(n):
                if not (isinstance(n, int) and n == 0):
                    pool.wait_ge(S("tick"), n)
                pool.tensor_tensor(ticks[:, 0:1], ticks[:, 1:2], ticks[:, 2:3], ALU.add).then_inc(S("tick"), 1)

            def walk1(i, h, first):
                s = 2 * i + h
                if not first:
                    pool.wait_ge(S(f"got{h}"), i * 16 * SUP)
                    pool.wait_ge(S("kT"), (s - 1) * GPS)
                    pool.wait_ge(S(f"spill{h}"), 16 * i)
                tick(2 * s)
                pool.tensor_copy(idx[:, h * SUP:(h + 1) * SUP], kvT[:, ds(s * SUP, SUP)]).then_inc(S("idx"), 1)
                pool.wait_ge(S("idx"), s + 1)
                tick(2 * s + 1)
                for j in range(SUP):
                    pool.indirect_dma_start(kv_buf[h][:, j, :], None, kv_table,
                                            bass.IndirectOffsetOnAxis(ap=idx[:, h * SUP + j:h * SUP + j + 1], axis=0)).then_inc(S(f"got{h}"), 16)

            pool.wait_ge(S("kv_out0"), 16 * (NB // 2 + 1))
            pool.wait_ge(S("kv_out1"), 16 * (NB // 2))
            pool.wait_ge(S("ef_sb"), 2)
            for h in range(2):
                walk1(0, h, True)
            with pool.Fori(1, NSUP // 2) as i:
                for h in range(2):
                    walk1(i, h, False)

            pool.wait_ge(S("ends_out"), 16)
            pool.wait_ge(S("endi"), 2)
            for b in range(NB):
                n = LAST if b == NB - 1 else P
                pool.indirect_dma_start(ncol[0:n, b, :], None, ends_d,
                                        bass.IndirectOffsetOnAxis(ap=endi[0:n, b:b + 1], axis=0)).then_inc(S("sums_in"), 16)

            for l in range(2):
                pool.wait_ge(S("row_out"), 32 * (l + 1))
                pool.memset(al[:, :, :], 0.0).then_inc(S("al0"), 1)
                for half in range(2):
                    if l + half > 0:
                        for s in range(RS):
                            pool.wait_ge(S(f"row{s}"), (2 * l + half) * 16 * SUP)
                    pool.tensor_copy(idx[:, :], srcT[:, half * RS * SUP:(half + 1) * RS * SUP]).then_inc(S("idx"), 1)
                    pool.wait_ge(S("idx"), NSUP + 2 * l + half + 1)
                    for s in range(RS):
                        if half:
                            pool.wait_ge(S("sum"), (1 + l) * PAIRS + (s + 1) * PPS)
                        for j in range(SUP):
                            pool.indirect_dma_start(rows[:, s, j, :], None, row_table[l],
                                                    bass.IndirectOffsetOnAxis(ap=idx[:, s * SUP + j:s * SUP + j + 1], axis=0)).then_inc(S(f"row{s}"), 16)
                        if s > 0:
                            continue
                        if half == 0:
                            pool.wait_ge(S("nst"), 2 * (l + 1))
                            pool.wait_ge(S("zero_out"), 32)
                            for b in range(NB):
                                n = LAST if b == NB - 1 else P
                                pool.indirect_dma_start(starts_d[l], bass.IndirectOffsetOnAxis(ap=starti[0:n, b:b + 1], axis=0),
                                                        nst[0:n, b, :], None).then_inc(S("start_out"), 16)
                        else:
                            pool.wait_ge(S("loop_out"), 16 * (l + 1))
                            pool.wait_ge(S("al0"), l + 1)
                            for b in range(NB):
                                n = LAST if b == NB - 1 else P
                                pool.indirect_dma_start(al[0:n, b, :], None, loops_d[l],
                                                        bass.IndirectOffsetOnAxis(ap=endi[0:n, b:b + 1], axis=0)).then_inc(S("al_in"), 16)

        @block.scalar
        def _(act):
            def root(k):
                act.wait_ge(S("var"), k + 1)
                act.activation(rstd[:, :], rstd[:, :], ACT.Sqrt).then_inc(S("std"), 1)

            def turned(k, dst):
                for g in range(NG):
                    n = min(4, NB - 4 * g) * P
                    act.wait_ge(S("tr"), k * NG + g + 1)
                    act.activation(dst[:, 4 * g * P:4 * g * P + n], bank((k * NG + g) % 2)[:, 0:n], ACT.Copy).then_inc(S("tr_sb"), 1)

            act.dma_start(nodes[2][:, :, :].rearrange("p b f -> p (b f)").bitcast(I32)[:, 0:N], spread(A["node_type_4"])).then_inc(S("nt_in"), 16)
            for dst, src in ((tmpw[:, 0:P], A["L1_gnn_g1_ew"]), (tmpw[:, P:2 * P], A["L1_gnn_g2_ew"]),
                             (tmpw[:, 2 * P:3 * P], spread(A["L1_gnn_g1_att_edge"].rearrange("h c -> (h c)"))),
                             (tmpw[:, 3 * P:4 * P], spread(A["L1_gnn_g2_att_edge"].rearrange("h c -> (h c)"))),
                             (wk[:, 0:P], A["L1_gnn_ta_w1"].to_broadcast([P, P])),
                             (wk[:, P:2 * P], spread(A["L1_gnn_ta_b1"])),
                             (lhs2[0:1, :], A["L1_gnn_ta_w1"]), (lhs2[1:2, :], row_of(A["L1_gnn_ta_b1"])),
                             (lnwb[:, :], spread(A["L1_gnn_ta_ln_w"], 2)), (smal[:, 8:8 + ET], spread(A["L0_gnn_mu"])),
                             (taw2[:, :], A["L1_gnn_ta_w2"]),
                             (wqkv[:, 0, :, :], A["L0_gnn_W_K"].rearrange("t i o -> i t o")),
                             (wqkv[:, 1, :, :], A["L0_gnn_W_Q"].rearrange("t i o -> i t o")),
                             (wqkv[:, 2, :, :], A["L0_gnn_W_V"].rearrange("t i o -> i t o")),
                             (wedge.rearrange("p (t o) -> p t o", o=P), A["L0_gnn_W_edge"].rearrange("t i o -> i t o"))):
                act.dma_start(dst, src).then_inc(S("w_in"), 16)
            for i, (g, name) in enumerate((l, n) for l in (1, 2) for n in ("g{}_b", "n{}_w", "n{}_b")):
                act.dma_start(vec6[:, i, :], spread(A["L1_gnn_" + name.format(g)])).then_inc(S("w_in"), 16)
            root(0)
            turned(0, KT)
            for g in range(NG):
                n = min(512, NW - g * 512)
                act.wait_ge(S("k"), g + 1)
                act.activation(KT[:, g * 512:g * 512 + n], bank(6 + g % 2)[:, 0:n], ACT.Copy).then_inc(S("k_sb"), 1)
            act.wait_ge(S("rvar"), 1)
            act.activation(ef[:, 1, :], ef[:, 1, :], ACT.Sqrt).then_inc(S("rstd0"), 1)

            def kv(b, h, i):
                act.wait_ge(S("kv"), b + 1)
                act.activation(QT[:, ds(b * P, P)], bank(6 + h)[:, 0:P], ACT.Copy).then_inc(S("q_sb"), 1)
                if i is not None:
                    act.wait_ge(S(f"kv_out{h}"), 16 * i)
                act.activation(stg[h][:, ET // 2:ET, 0:P], bank(2 * h + 1).rearrange("p (t f) -> p t f", f=P), ACT.Copy).then_inc(S("kv_act"), 1)

            for h in range(2):
                kv(h, h, None)
            with act.Fori(1, (NB - 1) // 2) as i:
                for h in range(2):
                    kv(2 * i + h, h, i)
            kv(NB - 1, 0, (NB - 1) // 2)

            def walk1(i, first):
                for gg in range(2 * GPS):
                    g = 2 * GPS * i + gg
                    f = first and gg < 2
                    act.wait_ge(S("kT"), g + 1)
                    if not f:
                        act.wait_ge(S("kq"), g - 1)
                    act.activation(kTb[gg % 2], bank(gg % 2), ACT.Copy).then_inc(S("kT_sb"), 1)
                    act.wait_ge(S("m1"), g + 1)
                    if not f:
                        act.wait_ge(S("m2"), g - 1)
                    act.activation(hid[gg % 2], bank(4), ACT.Relu, bias=tacol[:, 0:1]).then_inc(S("relu"), 1)
                    act.wait_ge(S("m2"), g + 1)
                    if not f:
                        act.wait_ge(S("m3"), g - 1)
                    act.activation(tw[gg % 2], bank(5), ACT.Tanh, bias=tacol[:, 1:2]).then_inc(S("tanh"), 1)

            act.wait_ge(S("ta_in"), 32)
            walk1(0, True)
            with act.Fori(1, NSUP // 2) as i:
                walk1(i, False)
            act.wait_ge(S("xm"), 1)
            act.activation(scan_tile(0)[:, 0, :], scan_tile(0)[:, 0, :], ACT.Exp).then_inc(S("exp"), 1)

            root(1)
            turned(1, hT)
            root(2)
            turned(2, zT[0])
            turned(3, zT[1])
            root(3)
            for l in range(2):
                turned(4 + l, hT)
                act.wait_ge(S("row_out"), 32 * (l + 1))
                act.wait_ge(S("hw_out"), 16 * (l + 1))
                act.wait_ge(S("res_out"), 16 * (l + 1))
                act.wait_ge(S("start_out"), 16 * NB * (l + 1))
                act.dma_start(scan_tile(2, 2).rearrange("p h c -> p (h c)"),
                              starts_d[l].rearrange("(q c) h -> q (c h)", c=ROW)).then_inc(S("start_in"), 16)
                act.wait_ge(S("xm"), 2 + l)
                act.activation(scan_tile(2), scan_tile(2), ACT.Exp).then_inc(S("exp"), 1)
                act.wait_ge(S("elm"), 1 + l)
                act.activation(scan_tile(1), scan_tile(1), ACT.Exp).then_inc(S("exp"), 1)
                root(4 + l)
                act.wait_ge(S("elu"), l + 1)
                act.activation(nodes[2], nodes[2], ACT.Exp).then_inc(S("elu_e"), 1)

        @block.tensor
        def _(pe):
            def turn(k, blocks):
                pe.wait_ge(S("tsrc"), k + 1)
                for g in range(NG):
                    n = k * NG + g
                    if n >= 2:
                        pe.wait_ge(S("tr_sb"), n - 1)
                    nb = min(4, NB - 4 * g)
                    for j in range(nb):
                        t = pe.transpose(bank(n % 2)[:, j * P:(j + 1) * P], blocks(4 * g + j), ident[:, :])
                    t.then_inc(S("tr"), 1)

            def carried(k, n, tile, back):
                pe.wait_ge(S("local"), k + 1)
                pe.transpose(bank(7)[0:n, 0:Q], tile[:, :, 0 if back else ROW - 1], ident[0:Q, 0:Q]).then_inc(S("carT"), 1)
                pe.wait_ge(S("carS"), k + 1)
                pe.transpose(bank(7)[0:Q, P:P + n], carry[0:n, 1:Q + 1] if back else carry[0:n, 0:Q],
                             ident[0:n, 0:n]).then_inc(S("carB"), 1)

            pe.wait_ge(S("const"), NCONST)
            turn(0, lambda b: nodes[1][:, b, :])

            pe.wait_ge(S("w_in"), 16 * N_W_IN)
            for g in range(NG):
                pe.wait_ge(S("hTt"), NT if (g + 1) * 512 <= HALF else 2 * NT)
                if g >= 2:
                    pe.wait_ge(S("k_sb"), g - 1)
                n = min(512, NW - g * 512)
                for t in range(NT):
                    mm = pe.matmul(bank(6 + g % 2)[:, 0:n], wqkv[:, 0, t, :], hTt[t][:, g * 512:g * 512 + n],
                                   start=(t == 0), stop=(t == NT - 1))
                mm.then_inc(S("k"), 1)
            pe.wait_ge(S("ef"), 1)
            pe.wait_ge(S("tr_sb"), NG)
            pe.wait_ge(S("k_sb"), NG)
            for a, e in enumerate((4, 1, 7, 5, 2, 3, 9)):
                for k in range(TPR):
                    t = pe.transpose(bank(a)[:, k * Q:(k + 1) * Q], ef[:, e, k * P:(k + 1) * P], ident[0:Q, 0:Q])
                t.then_inc(S("efT"), 1)
            pe.wait_ge(S("flags"), 1)
            for a in range(3):
                t = pe.transpose(bank(7)[0:H2, a * Q:(a + 1) * Q], flags[:, a, :], ident[0:Q, 0:Q])
            t.then_inc(S("flT"), 1)
            pe.wait_ge(S("ef_sb"), 8)
            pe.wait_ge(S("we"), 1)
            for b in range(NB):
                h = b % 2
                if b >= 2:
                    pe.wait_ge(S("kv_dve"), b - 1)
                    pe.wait_ge(S("kv_act"), b - 1)
                for half in range(2):
                    pe.matmul(bank(2 * h + half), KT[:, b * P:(b + 1) * P], wedge[:, half * 512:(half + 1) * 512],
                              start=True, stop=True)
                for t in range(NT):
                    pe.matmul(bank(4 + h)[:, 0:P], hTt[t][:, b * P:(b + 1) * P], wqkv[:, 2, t, :],
                              start=(t == 0), stop=(t == NT - 1))
                for t in range(NT):
                    mm = pe.matmul(bank(6 + h)[:, 0:P], wqkv[:, 1, t, :], hTt[t][:, b * P:(b + 1) * P],
                                   start=(t == 0), stop=(t == NT - 1))
                mm.then_inc(S("kv"), 1)

            def edge_terms(g, gg):
                pe.wait_ge(S("tanh"), g + 1)
                pe.matmul(bank(6)[0:H2, :], Wm[:, :, :].rearrange("p l h -> p (l h)"), tw[gg % 2], start=True, stop=True).then_inc(S("m3"), 1)

            def walk1(i, first):
                for gg in range(2 * GPS):
                    h, g = gg // GPS, 2 * GPS * i + gg
                    if gg % GPS == 0:
                        pe.wait_ge(S(f"got{h}"), (i + 1) * 16 * SUP)
                        pe.wait_ge(S(f"rate_in{h}"), 16 * (i + 1))
                    if gg % 2 == 0:
                        _, w = nc.values_load_multi_w_load_instructions(
                            d0[0:1, ds(g * TPR, 2 * TPR)], engines=[mybir.EngineType.PE], min_val=0, max_val=NW,
                            skip_runtime_bounds_check_because="destinations are nodes")
                    if not (first and gg < 2):
                        pe.wait_ge(S("kT_sb"), g - 1)
                    for j in range(TPR):
                        t = pe.transpose(bank(gg % 2)[:, j * P:(j + 1) * P],
                                         kv_buf[h][:, gg % GPS * TPR + j, 0:P], ident[:, :])
                    t.then_inc(S("kT"), 1)
                    if not (first and gg < 1):
                        pe.wait_ge(S("relu"), g)
                    pe.matmul(bank(4), lhs2[:, :], rateb[h][:, gg % GPS * ROW:(gg % GPS + 1) * ROW], start=True, stop=True).then_inc(S("m1"), 1)
                    if not (first and gg < 1):
                        if not (first and gg < 2):
                            pe.wait_ge(S("ae"), g - 1)
                        edge_terms(g - 1, gg + 1)
                    pe.wait_ge(S("kT_sb"), g + 1)
                    if not (first and gg < 2):
                        pe.wait_ge(S("score"), g - 1)
                    for j in range(TPR):
                        mm = pe.matmul(bank(2 + gg % 2)[:, j * P:(j + 1) * P], kTb[gg % 2][:, j * P:(j + 1) * P],
                                       QT[:, ds(w[gg % 2 * TPR + j], P)], start=True, stop=True)
                    mm.then_inc(S("kq"), 1)
                    pe.wait_ge(S("relu"), g + 1)
                    if not (first and gg < 1):
                        pe.wait_ge(S("tanh"), g)
                    pe.matmul(bank(5), taw2[:, :], hid[gg % 2], start=True, stop=True).then_inc(S("m2"), 1)
                    pe.wait_ge(S("oh"), g + 1)
                    for j in range(TPR):
                        mm = pe.matmul(bank(7)[:, 0:NB], oh16[gg % 2][:, j * P:(j + 1) * P], ohh[gg % 2][:, j, :],
                                       start=(first and gg == 0 and j == 0), stop=False, skip_group_check=True)
                    mm.then_inc(S("hist"), 1)

            pe.wait_ge(S("kv_act"), NB)
            pe.wait_ge(S("kv_dve"), NB)
            pe.wait_ge(S("d0_in"), 16)
            pe.wait_ge(S("qtpad"), 1)
            pe.wait_ge(S("Wm"), 1)
            walk1(0, True)
            with pe.Fori(1, NSUP // 2) as i:
                walk1(i, False)
            pe.wait_ge(S("ae"), Q - 1)
            edge_terms(Q - 1, 1)

            pe.wait_ge(S("deg"), 1)
            pe.wait_ge(S("ae"), Q)
            pe.matmul(bank(6)[:, 0:NB], tri[:, :], deg[:, :], start=True, stop=True)
            pe.matmul(bank(6)[:, 32:32 + NB], ones[:, :], deg[:, :], start=True, stop=True).then_inc(S("cum"), 1)

            pe.wait_ge(S("score"), Q)
            for k in range(TPR):
                t = pe.transpose(bank(0)[0:Q, k * P:(k + 1) * P], aT[:, k:T:TPR, 0], ident[:, :])
            t.then_inc(S("scT"), 1)
            carried(0, 1, scan_tile(1)[:, 0:1, :], False)
            carried(1, 1, scan_tile(2)[:, 0:1, :], True)
            carried(2, 1, scan_tile(1)[:, 0:1, :], False)
            carried(3, 1, scan_tile(2)[:, 0:1, :], True)
            pe.wait_ge(S("attn"), 1)
            for k in range(TPR):
                t = pe.transpose(bank(0)[:, k * Q:(k + 1) * Q], scan_tile(0)[:, 0, k * P:(k + 1) * P], ident[0:Q, 0:Q])
            t.then_inc(S("wb"), 1)
            carried(4, H2, scan_tile(2, 2), False)

            def block_starts(t):
                return nc.values_load_multi_w_load_instructions(
                    b0[0:1, ds(t, 8)], engines=[mybir.EngineType.PE], min_val=0, max_val=NW - P,
                    skip_runtime_bounds_check_because="destinations are nodes")[1]

            def sum_super(k, s, n0, tile):
                for pr in range(PPS):
                    if pr % 4 == 0:
                        w = block_starts(s * SUP + pr * 2)
                    pe.wait_ge(S("sel"), s * PPS + (n0 + pr + 1))
                    for j in range(2):
                        for half in range(2):
                            mm = pe.matmul(acc[:, ds(w[pr % 4 * 2 + j] + half * P, P)],
                                           wk2[pr % 2][:, (j * 2 + half) * P:(j * 2 + half + 1) * P], tile(pr * 2 + j),
                                           start=False, stop=True, skip_group_check=True)
                    mm.then_inc(S("sum"), 1)

            pe.wait_ge(S("cleared"), 1)
            with pe.Fori(0, NSUP // 2) as i:
                for h in range(2):
                    pe.wait_ge(S(f"v_in{h}"), 16 * (i + 1))
                    sum_super(0, 2 * i + h, 0, lambda j: v_buf[h][:, j, :])

            turn(1, lambda b: nodes[1][:, b, :])
            pe.wait_ge(S("tr_sb"), 2 * NG)
            pe.wait_ge(S("ip_in"), 16 * 8)
            for g in range(-(-NB // 2)):
                if g >= 2:
                    pe.wait_ge(S("z_sb"), g - 1)
                for j in range(min(2, NB - 2 * g)):
                    b = 2 * g + j
                    mm = pe.matmul(bank(2 + g % 2)[:, j * KV:(j + 1) * KV], hT[:, b * P:(b + 1) * P], ipw1, start=True, stop=True)
                mm.then_inc(S("z"), 1)
            turn(2, lambda b: zt[:, b, 0:P])
            turn(3, lambda b: zt[:, b, P:KV])
            pe.wait_ge(S("tr_sb"), 4 * NG)
            for g in range(NG):
                if g >= 2:
                    pe.wait_ge(S("y_sb"), g - 1)
                for j in range(min(4, NB - 4 * g)):
                    b = 4 * g + j
                    for a in range(2):
                        mm = pe.matmul(bank(2 + g % 2)[:, j * P:(j + 1) * P], zT[a][:, b * P:(b + 1) * P], ipw2[:, a, :],
                                       start=(a == 0), stop=(a == 1))
                mm.then_inc(S("y"), 1)

            for l in range(2):
                turn(4 + l, lambda b: nodes[0][:, b, :])
                pe.wait_ge(S("tr_sb"), (5 + l) * NG)
                pe.wait_ge(S("Wx"), l + 1)
                for g in range(NGG):
                    if l * NGG + g >= 2:
                        pe.wait_ge(S("hw"), l * NGG + g - 1)
                    for j in range(min(3, NB - 3 * g)):
                        b = 3 * g + j
                        mm = pe.matmul(bank(2 + (l * NGG + g) % 2)[:, j * (P + H2):(j + 1) * (P + H2)], hT[:, b * P:(b + 1) * P], Wx[:, :],
                                       start=True, stop=True)
                    mm.then_inc(S("hwp"), 1)
                pe.wait_ge(S("A3"), l + 1)

                def sources(i, first):
                    for gg in range(4):
                        g = 4 * i + gg
                        pe.wait_ge(S("oh"), Q + l * Q + g + 1)
                        if not (first and gg < 2):
                            pe.wait_ge(S("asel"), l * Q + g - 1)
                        for j in range(TPR):
                            for m in range(3):
                                mm = pe.matmul(bank(gg % 2)[:, j * NB * H:(j + 1) * NB * H], oh16[gg % 2][:, j * P:(j + 1) * P],
                                               A3[:, m, :], start=(m == 0), stop=(m == 2))
                        mm.then_inc(S("apre"), 1)

                sources(0, True)
                with pe.Fori(1, Q // 4) as i:
                    sources(i, False)
                carried(5 + 4 * l, H2, scan_tile(0, 2), False)
                pe.wait_ge(S("asel"), (l + 1) * Q)
                for h in range(H):
                    for k in range(TPR):
                        t = pe.transpose(bank(h)[0:Q, k * P:(k + 1) * P], aT[:, k:T:TPR, h], ident[:, :])
                    t.then_inc(S("xT"), 1)
                carried(6 + 4 * l, H, scan_tile(0), False)
                carried(7 + 4 * l, H, scan_tile(3), True)
                pe.wait_ge(S("exp"), 2 + 2 * l)
                for h in range(H):
                    for k in range(TPR):
                        t = pe.transpose(bank(h)[:, k * Q:(k + 1) * Q], scan_tile(2)[:, h, k * P:(k + 1) * P], ident[0:Q, 0:Q])
                    t.then_inc(S("wb"), 1)
                carried(8 + 4 * l, H, scan_tile(0), False)
                pe.wait_ge(S("cleared"), l + 2)
                with pe.Fori(0, 2) as half:
                    for s in range(RS):
                        pe.wait_ge(S("msg"), half * RS + (l * NSUP + s + 1))
                        sum_super(1 + l, half * RS + s, (1 + l) * PAIRS, lambda j: rows[:, s, j, :])

        @block.vector
        def _(v):
            c = Chain(v, S("dve"))
            carries = [0]
            roots = [0]

            def step(instruction):
                c.did(instruction)
                c.wait()

            def carry_over(n, tile, masks, row_masks, start, ops, back):
                k = carries[0]
                carries[0] += 1
                end = Q if back else 0
                c.did(v.memset(carry[0:n, end:end + 1], start))
                v.wait_ge(S("carT"), k + 1)
                run, came = carry[0:n, 1 - back:Q + 1 - back], bank(7)[0:n, 0:Q]
                if back:
                    v.tensor_tensor_scan(run[:, ::-1], row_masks[:, ::-1], came[:, ::-1], start, *ops).then_inc(S("carS"), 1)
                else:
                    v.tensor_tensor_scan(run, row_masks, came, start, *ops).then_inc(S("carS"), 1)
                v.wait_ge(S("carB"), k + 1)
                for h in range(n):
                    c.did(v.scalar_tensor_tensor(tile[:, h, :], masks, bank(7)[0:Q, P + h:P + h + 1], tile[:, h, :], *ops))
                c.wait()

            def scans(n, tile, masks, data, start, ops, back=False):
                for h in range(n):
                    o, m, x = tile[:, h, :], masks, data(h)
                    if back:
                        o, m, x = o[:, ::-1], m[:, ::-1], x[:, ::-1]
                    s = v.tensor_tensor_scan(o, m, x, start, *ops)
                    if h == n - 1:
                        s.then_inc(S("local"), 1)
                    else:
                        c.did(s)

            SUM, MAX = (ALU.mult, ALU.add), (ALU.add, ALU.max)

            def running_sum(n, tile, data):
                scans(n, tile, cont[:, :], data, 0.0, SUM)
                carry_over(n, tile, pre[:, :], rowf[0:n, 0, :], 0.0, SUM, False)

            def running_max(n, tile, data):
                scans(n, tile, pen[:, :], data, -BIG, MAX)
                carry_over(n, tile, prepen[:, :], rowf[0:n, 1, :], -BIG, MAX, False)

            def from_ends(n, tile, data):
                for h in range(n):
                    c.did(v.scalar_tensor_tensor(tile[:, h, :], contn[:, :], 1.0, data(h), ALU.is_lt, ALU.mult))
                c.wait()
                scans(n, tile, contn[:, :], lambda h: tile[:, h, :], 0.0, SUM, True)
                carry_over(n, tile, post[:, :], rowf[0:n, 2, :], 0.0, SUM, True)

            def layer_norm(X, Y, W):
                k = roots[0]
                roots[0] += 1
                sf, mf = stats[:, :, :].rearrange("p b s -> p (b s)"), mv[:, :, :].rearrange("p b s -> p (b s)")
                with v.Fori(0, NB // 5) as i:
                    for u in range(5):
                        v.bn_stats(sf[:, ds((i * 5 + u) * 6, 6)], X[:, ds((i * 5 + u) * W, W)]).then_inc(S("dve"), 1)
                c.n += NB
                c.wait()
                for b in range(NB):
                    c.did(v.bn_aggr(mv[:, b, :], stats[:, b, :]))
                c.wait()
                v.tensor_scalar(rstd[:, :], mv[:, :, 1], EPS, None, ALU.add).then_inc(S("var"), 1)
                v.wait_ge(S("std"), k + 1)
                step(v.reciprocal(rstd[:, :], rstd[:, :]))
                with v.Fori(0, NB // 5) as i:
                    for u in range(5):
                        v.tensor_scalar(Y[:, ds((i * 5 + u) * W, W)], X[:, ds((i * 5 + u) * W, W)],
                                        mf[:, ds((i * 5 + u) * 2, 1)], rstd[:, ds(i * 5 + u, 1)],
                                        ALU.subtract, ALU.mult).then_inc(S("dve"), 1)
                c.n += NB
                c.wait()

            def fl(t):
                return t.rearrange("p b f -> p (b f)")

            v.wait_ge(S("x_in"), 32)
            layer_norm(fl(nodes[0]), fl(nodes[1]), P)
            v.tensor_scalar(fl(nodes[1]), fl(nodes[1]), 0.0, None, ALU.max).then_inc(S("tsrc"), 1)

            v.wait_ge(S("w_in"), 16 * 21)
            ab = wk[:, 0:2 * P].rearrange("p (a f) -> p a f", a=2)
            pr = wk[:, 2 * P:5 * P].rearrange("p (a f) -> p a f", a=3)
            step(v.tensor_reduce(smal[:, 0:2], ab, AX.X, ALU.add))
            step(v.tensor_scalar(smal[:, 0:2], smal[:, 0:2], 1.0 / P, None, ALU.mult))
            for i in range(2):
                c.did(v.tensor_scalar(ab[:, i, :], ab[:, i, :], smal[:, i:i + 1], None, ALU.subtract))
            c.wait()
            c.did(v.tensor_tensor(pr[:, 0, :], ab[:, 0, :], ab[:, 0, :], ALU.mult))
            c.did(v.tensor_tensor(pr[:, 1, :], ab[:, 0, :], ab[:, 1, :], ALU.mult))
            c.did(v.tensor_tensor(pr[:, 2, :], ab[:, 1, :], ab[:, 1, :], ALU.mult))
            c.wait()
            step(v.tensor_reduce(smal[:, 2:5], pr, AX.X, ALU.add))
            c.did(v.tensor_scalar(smal[:, 2:5], smal[:, 2:5], 1.0 / P, None, ALU.mult))
            c.wait()
            step(v.tensor_scalar(smal[:, 3:4], smal[:, 3:4], 2.0, None, ALU.mult))
            step(v.tensor_reduce(lhm[:, :], lhs2[:, :], AX.X, ALU.add))
            step(v.tensor_scalar(lhm[:, :], lhm[:, :], 1.0 / P, None, ALU.mult))
            step(v.tensor_scalar(lhs2[:, :], lhs2[:, :], lhm[:, 0:1], None, ALU.subtract))
            step(v.tensor_tensor(lhs2[:, :], lhs2[:, :], lnwb[:, :], ALU.mult))
            tw4 = tmpw[:, 0:4 * P].rearrange("p (a f) -> p a f", a=4)
            step(v.tensor_tensor(tw4[:, 0:2, :], tw4[:, 0:2, :], tw4[:, 2:4, :], ALU.mult))
            v.tensor_reduce(Wm[:, :, :], tw4[:, 0:2, :].rearrange("p a (h c) -> p a h c", c=C), AX.X, ALU.add).then_inc(S("Wm"), 1)
            for t in range(ET):
                i = v.tensor_scalar(wedge[:, t * P:(t + 1) * P], wedge[:, t * P:(t + 1) * P], smal[:, 8 + t:9 + t], P ** -0.5, ALU.mult, ALU.mult)
                if t == ET - 1:
                    i.then_inc(S("we"), 1)
                else:
                    c.did(i)
            v.memset(QT[:, NW:NWP], 0.0).then_inc(S("qtpad"), 1)
            if NW > N:
                for t in range(NT):
                    c.did(v.memset(hTt[t][:, N:NW], 0.0))
            v.wait_ge(S("nt_in"), 16)
            ntb = fl(nodes[2]).bitcast(I32)
            v.wait_ge(S("tr_sb"), NG)
            for lo, hi in ((0, HALF), (HALF, N)):
                for t in range(NT):
                    v.scalar_tensor_tensor(hTt[t][:, lo:hi], ntb[:, lo:hi], float(t), KT[:, lo:hi], ALU.is_equal, ALU.mult).then_inc(S("hTt"), 1)
            v.wait_ge(S("hTt"), 2 * NT)

            v.wait_ge(S("e_in"), 16 * N_E_IN)
            D, DP, DN, SR, TY, EW = [eraw[:, i, :] if i == 5 else eraw[:, i, :].bitcast(I32) for i in range(6)]
            Ei = [ef[:, i, :].bitcast(I32) for i in range(10)]
            c.did(v.memset(ef[:, 9, :], 0.0))
            c.did(v.tensor_tensor(cont[:, :], D, DP, ALU.is_equal))
            c.did(v.tensor_tensor(contn[:, :], D, DN, ALU.is_equal))
            c.did(v.tensor_copy(ef[:, 0, :], D))
            c.did(v.tensor_copy(ef[:, 1, :], SR))
            c.did(v.tensor_scalar(Ei[8], D, 7, None, ALU.arith_shift_right))
            c.did(v.tensor_scalar(Ei[7], SR, 7, None, ALU.arith_shift_right))
            c.did(v.scalar_tensor_tensor(ef[:, 4, :], SR, float(ET), TY, ALU.mult, ALU.add))
            c.wait()
            c.did(v.tensor_tensor_scan(pre[:, :], cont[:, :], ef[:, 9, :], 1.0, *SUM))
            c.did(v.tensor_tensor_scan(post[:, ::-1], contn[:, ::-1], ef[:, 9, :], 1.0, *SUM))
            c.did(v.tensor_copy(ef[:, 2, :], Ei[8]))
            c.did(v.tensor_copy(ef[:, 3, :], Ei[7]))
            c.wait()
            c.did(v.scalar_tensor_tensor(ef[:, 5, :], ef[:, 2, :], -float(P), ef[:, 0, :], ALU.mult, ALU.add))
            c.did(v.scalar_tensor_tensor(ef[:, 6, :], ef[:, 3, :], -float(P), ef[:, 1, :], ALU.mult, ALU.add))
            step(v.tensor_scalar(blk[:, :], ef[:, 2, 0:ROW:P], float(P), None, ALU.mult))
            for k in range(TPR):
                c.did(v.tensor_scalar(ef[:, 9, k * P:(k + 1) * P], ef[:, 0, k * P:(k + 1) * P], blk[:, k:k + 1], None, ALU.subtract))
            for k in range(TPR):
                i = v.tensor_scalar(ef[:, 7, k * P:(k + 1) * P], ef[:, 0, k * P:(k + 1) * P], ef[:, 0, k * P:k * P + 1], None, ALU.subtract)
                if k == TPR - 1:
                    i.then_inc(S("ef"), 1)
                else:
                    c.did(i)
            c.wait()
            v.tensor_copy(ef[:, 8, 0:ROW // 2].bitcast(BF16), ef[:, 6, :]).then_inc(S("lo_ready"), 1)
            c.did(v.tensor_scalar(pen[:, :], cont[:, :], -1.0, BIG, ALU.add, ALU.mult))
            c.did(v.tensor_scalar(prepen[:, :], pre[:, :], -1.0, BIG, ALU.add, ALU.mult))
            c.wait()
            c.did(v.tensor_copy(flags[:, 0, :], pre[:, ROW - 1:ROW].to_broadcast([Q, H2])))
            c.did(v.tensor_copy(flags[:, 1, :], prepen[:, ROW - 1:ROW].to_broadcast([Q, H2])))
            v.tensor_copy(flags[:, 2, :], post[:, 0:1].to_broadcast([Q, H2])).then_inc(S("flags"), 1)
            for a, t in enumerate((kvT, srcT, relT, loT, hiT, shiT, relbT)):
                v.wait_ge(S("efT"), a + 1)
                v.tensor_copy(t[:, :].rearrange("p (q k) -> p k q", k=TPR), bank(a)[:, 0:T].rearrange("p (k q) -> p k q", k=TPR)).then_inc(S("ef_sb"), 1)
            v.wait_ge(S("d0_in"), 16)
            v.tensor_scalar(b0[:, :], d0[:, :], 7, 7, ALU.arith_shift_right, ALU.arith_shift_left).then_inc(S("b0"), 1)
            v.wait_ge(S("flT"), 1)
            v.tensor_copy(rowf[:, :, :], bank(7)[0:H2, 0:3 * Q].rearrange("p (a q) -> p a q", a=3)).then_inc(S("ef_sb"), 1)

            va, cab, vb = (smal[0:Q, i:i + 1] for i in (2, 3, 4))
            v.wait_ge(S("lo_out"), 16)
            v.wait_ge(S("efT"), 7)
            step(v.tensor_scalar(ef[:, 1, :], EW, va, cab, ALU.mult, ALU.add))
            step(v.tensor_tensor(ef[:, 1, :], ef[:, 1, :], EW, ALU.mult))
            step(v.tensor_scalar(ef[:, 1, :], ef[:, 1, :], vb, 0.0, ALU.add, ALU.max))
            v.tensor_scalar(ef[:, 1, :], ef[:, 1, :], EPS, None, ALU.add).then_inc(S("rvar"), 1)
            v.wait_ge(S("rstd0"), 1)
            step(v.reciprocal(ef[:, 1, :], ef[:, 1, :]))
            v.tensor_tensor(ef[:, 0, :], ef[:, 1, :], EW, ALU.mult).then_inc(S("rate_ready"), 1)

            def kv(b, h, i):
                v.wait_ge(S("kv"), b + 1)
                if i is not None:
                    v.wait_ge(S(f"kv_out{h}"), 16 * i)
                v.tensor_copy(stg[h][:, 0:ET // 2, 0:P], bank(2 * h).rearrange("p (t f) -> p t f", f=P))
                v.tensor_copy(stg[h][:, :, P:KV], bc(bank(4 + h)[:, 0:P], 1, [P, ET, P])).then_inc(S("kv_dve"), 1)

            for h in range(2):
                kv(h, h, None)
            with v.Fori(1, (NB - 1) // 2) as i:
                for h in range(2):
                    kv(2 * i + h, h, i)
            kv(NB - 1, 0, (NB - 1) // 2)

            v.wait_ge(S("kv_out0"), 16 * (NB // 2 + 1))
            v.wait_ge(S("kv_out1"), 16 * (NB // 2))

            def walk1(i, first):
                for gg in range(2 * GPS):
                    g = 2 * GPS * i + gg
                    if not (first and gg < 2):
                        v.wait_ge(S("hist"), g - 1)
                    v.tensor_tensor(ohh[gg % 2][:, :, :], bc(iota16[:, 0:NB], 1, [P, TPR, NB]),
                                    bc(hiT[:, ds(g * TPR, TPR)], 2, [P, TPR, NB]), ALU.is_equal)
                    v.tensor_tensor(oh16[gg % 2][:, :].rearrange("p (j f) -> p j f", f=P), bc(iota16[:, :], 1, [P, TPR, P]),
                                    bc(loT[:, ds(g * TPR, TPR)], 2, [P, TPR, P]), ALU.is_equal).then_inc(S("oh"), 1)
                    if not (first and gg < 1):
                        v.wait_ge(S("m3"), g)
                        if gg % GPS == 1 and not (first and gg < GPS):
                            v.wait_ge(S("ae_out"), 16 * (2 * i + gg // GPS))
                        v.tensor_copy(aeb[:, (gg - 1) % GPS * ROW:((gg - 1) % GPS + 1) * ROW], bank(6)[0:H2, :]).then_inc(S("ae"), 1)
                    v.wait_ge(S("kq"), g + 1)
                    for j in range(TPR):
                        G = bank(2 + gg % 2)[:, j * P:(j + 1) * P]
                        s = v.scalar_tensor_tensor(G, iota[:, 0:P], relT[:, ds(g * TPR + j, 1)], G, ALU.is_equal, ALU.mult,
                                                   accum_out=aT[:, ds(g * TPR + j, 1), 0])
                    s.then_inc(S("score"), 1)

            walk1(0, True)
            with v.Fori(1, NSUP // 2) as i:
                walk1(i, False)
            v.wait_ge(S("m3"), Q)
            v.tensor_copy(aeb[:, (GPS - 1) * ROW:GPS * ROW], bank(6)[0:H2, :]).then_inc(S("ae"), 1)

            v.wait_ge(S("hist"), Q)
            v.tensor_copy(deg[:, :], bank(7)[:, 0:NB]).then_inc(S("deg"), 1)
            v.wait_ge(S("cum"), 1)
            step(v.tensor_tensor_scan(nb_[:, :], ones[:, 0:NB], bank(6)[:, 32:32 + NB], 0.0, *SUM))
            step(v.tensor_tensor(nb_[:, :], nb_[:, :], bank(6)[:, 32:32 + NB], ALU.subtract))
            step(v.tensor_tensor(nb_[:, :], nb_[:, :], bank(6)[:, 0:NB], ALU.add))
            v.tensor_scalar(endi[:, :], nb_[:, :], -1.0, None, ALU.add).then_inc(S("endi"), 1)
            v.tensor_tensor(starti[:, :], nb_[:, :], deg[:, :], ALU.subtract).then_inc(S("endi"), 1)

            X, M, Z = (scan_tile(i)[:, 0:1, :] for i in range(3))
            v.wait_ge(S("scT"), 1)
            step(v.tensor_copy(X[:, 0, :], bank(0)[0:Q, :]))
            running_max(1, M, lambda h: X[:, 0, :])
            step(v.tensor_scalar(M[:, 0, :], M[:, 0, :], -1e9, None, ALU.max))
            from_ends(1, Z, lambda h: M[:, 0, :])
            v.tensor_tensor(X[:, 0, :], X[:, 0, :], Z[:, 0, :], ALU.subtract).then_inc(S("xm"), 1)
            v.wait_ge(S("exp"), 1)
            running_sum(1, M, lambda h: X[:, 0, :])
            from_ends(1, Z, lambda h: M[:, 0, :])
            step(v.tensor_scalar(Z[:, 0, :], Z[:, 0, :], 1e-10, None, ALU.add))
            step(v.reciprocal(Z[:, 0, :], Z[:, 0, :]))
            v.tensor_tensor(X[:, 0, :], X[:, 0, :], Z[:, 0, :], ALU.mult).then_inc(S("attn"), 1)
            v.wait_ge(S("wb"), 1)
            v.tensor_copy(aT[:, :, 0].rearrange("p (q k) -> p k q", k=TPR), bank(0)[:, 0:T].rearrange("p (k q) -> p k q", k=TPR)).then_inc(S("sm0"), 1)

            v.wait_ge(S("ae_in"), 16)
            running_sum(H2, scan_tile(2, 2), lambda h: scan_tile(0, 2)[:, h, :])
            v.tensor_copy(scan_tile(0, 2).rearrange("p h c -> p (h c)").rearrange("p (c h) -> p h c", h=H2),
                          scan_tile(2, 2)).then_inc(S("mae1"), 1)

            v.wait_ge(S("sm0"), 1)
            v.memset(acc, 0.0).then_inc(S("cleared"), 1)

            def selections(s, n0, first, weighted):
                for pr in range(PPS):
                    if not (first and pr < 2):
                        v.wait_ge(S("sum"), s * PPS + (n0 + pr - 1))
                    for j in range(2):
                        t = s * SUP + (pr * 2 + j)
                        o = wk2[pr % 2][:, j * 2 * P:(j + 1) * 2 * P]
                        if weighted:
                            i = v.tensor_scalar(o, iota[:, :], relbT[:, ds(t, 1)], aT[:, ds(t, 1), 0], ALU.is_equal, ALU.mult)
                        else:
                            i = v.tensor_scalar(o, iota[:, :], relbT[:, ds(t, 1)], None, ALU.is_equal)
                    i.then_inc(S("sel"), 1)

            selections(0, 0, True, True)
            with v.Fori(1, NSUP) as s:
                selections(s, 0, False, True)

            v.wait_ge(S("x_in"), 64)
            v.wait_ge(S("sum"), PAIRS)
            v.tensor_tensor(fl(nodes[0]), fl(nodes[0]), acc[:, 0:NW], ALU.add).then_inc(S("x1"), 1)
            v.wait_ge(S("x1"), 1)

            v.wait_ge(S("sums_in"), 16 * NB)
            step(v.tensor_scalar(nb_[:, :], deg[:, :], 1.0, None, ALU.max))
            step(v.reciprocal(nb_[:, :], nb_[:, :]))
            step(v.tensor_tensor(mae[:, :, :], ncol[:, :, :], bc(nb_[:, :], 2, [P, NB, H2]), ALU.mult))

            layer_norm(fl(nodes[0]), fl(nodes[1]), P)
            v.tensor_scalar(fl(nodes[1]), fl(nodes[1]), 0.0, None, ALU.max).then_inc(S("tsrc"), 1)
            v.wait_ge(S("ip_in"), 16 * 8)
            b1, lw, lb = (ipv[:, i * KV:(i + 1) * KV] for i in range(3))
            b2, pw, pb = (ipv[:, 3 * KV + i * P:3 * KV + (i + 1) * P] for i in range(3))
            for g in range(-(-NB // 2)):
                n = min(2, NB - 2 * g)
                v.wait_ge(S("z"), g + 1)
                v.tensor_tensor(zt[:, 2 * g:2 * g + n, :], bank(2 + g % 2)[:, 0:n * KV].rearrange("p (b f) -> p b f", f=KV),
                                bc(b1, 1, [P, n, KV]), ALU.add).then_inc(S("z_sb"), 1)
            v.wait_ge(S("z_sb"), -(-NB // 2))
            step(v.tensor_scalar(fl(zt), fl(zt), 0.0, None, ALU.max))
            layer_norm(fl(zt), fl(zt), KV)
            step(v.tensor_tensor(zt, zt, bc(lw, 1, [P, NB, KV]), ALU.mult))
            v.tensor_tensor(zt, zt, bc(lb, 1, [P, NB, KV]), ALU.add).then_inc(S("tsrc"), 2)
            for g in range(NG):
                n = min(4, NB - 4 * g)
                v.wait_ge(S("y"), g + 1)
                v.tensor_tensor(nodes[1][:, 4 * g:4 * g + n, :], bank(2 + g % 2)[:, 0:n * P].rearrange("p (b f) -> p b f", f=P),
                                bc(b2, 1, [P, n, P]), ALU.add).then_inc(S("y_sb"), 1)
            v.wait_ge(S("y_sb"), NG)
            v.wait_ge(S("x1_out"), 16)
            layer_norm(fl(nodes[1]), fl(nodes[0]), P)
            step(v.tensor_tensor(nodes[0], nodes[0], bc(pw, 1, [P, NB, P]), ALU.mult))
            step(v.tensor_tensor(nodes[0], nodes[0], bc(pb, 1, [P, NB, P]), ALU.add))
            v.tensor_scalar(fl(nodes[0]), fl(nodes[0]), 0.0, 10.0, ALU.max, ALU.min).then_inc(S("tsrc"), 1)

            for l in range(2):
                v.wait_ge(S("gw_in"), 48 * (l + 1))
                att = wk[:, 0:2 * P].rearrange("p (a f) -> p a f", a=2)
                step(v.tensor_tensor(att, att, bc(Wx[:, 0:P], 1, [P, 2, P]), ALU.mult))
                v.tensor_reduce(Wx[:, P:P + H2].rearrange("p (a h) -> p a h", a=2), att.rearrange("p a (h c) -> p a h c", c=C),
                                AX.X, ALU.add).then_inc(S("Wx"), 1)
                for g in range(NGG):
                    n = min(3, NB - 3 * g)
                    v.wait_ge(S("hwp"), l * NGG + g + 1)
                    got = bank(2 + (l * NGG + g) % 2)[:, 0:n * (P + H2)].rearrange("p (b f) -> p b f", f=P + H2)
                    c.did(v.tensor_copy(ncol[:, 3 * g:3 * g + n, :], got[:, :, P:P + H2]))
                    v.tensor_copy(nodes[1][:, 3 * g:3 * g + n, :], got[:, :, 0:P]).then_inc(S("hw"), 1)
                c.wait()
                v.tensor_copy(nst[:, :, 0:H], ncol[:, :, H:H2]).then_inc(S("nst"), 1)
                a3 = a3r[:, :].rearrange("p (b h) -> p b h", h=H)
                step(v.tensor_tensor(a3, ncol[:, :, 0:H], ncol[:, :, H:H2], ALU.add))
                step(v.tensor_tensor(a3, a3, mae[:, :, l * H:(l + 1) * H], ALU.add))
                v.scalar_tensor_tensor(nst[:, :, H:H2], a3, 0.2, a3, ALU.mult, ALU.max).then_inc(S("nst"), 1)
                v.wait_ge(S("nst"), 2 * (l + 1))
                step(v.tensor_copy(a3, ncol[:, :, 0:H]))
                for m in range(2):
                    step(v.tensor_copy(A3[:, m, :], a3r[:, :]))
                    step(v.tensor_tensor(a3r[:, :], a3r[:, :], A3[:, m, :], ALU.subtract))
                v.tensor_copy(A3[:, 2, :], a3r[:, :]).then_inc(S("A3"), 1)

                def select(g, gg):
                    v.wait_ge(S("apre"), l * Q + g + 1)
                    prod = wk2[gg % 2][:, 0:TPR * NB * H].rearrange("p (j b h) -> p j b h", j=TPR, h=H)
                    v.tensor_tensor(prod, bank(gg % 2)[:, 0:TPR * NB * H].rearrange("p (j b h) -> p j b h", j=TPR, h=H),
                                    bc(ohh[gg % 2][:, :, :], 3, [P, TPR, NB, H]), ALU.mult).then_inc(S("prod"), 1)
                    v.wait_ge(S("prod"), l * Q + g + 1)
                    v.tensor_reduce(aT[:, ds(g * TPR, TPR), :], prod.rearrange("p j b h -> p j h b"), AX.X, ALU.add).then_inc(S("asel"), 1)

                def sources(i, first):
                    for gg in range(4):
                        g = 4 * i + gg
                        if gg % 2 == 0:
                            v.wait_ge(S(f"lo_in{gg // 2}"), 16 * (l * (Q // 4) + i + 1))
                        if not (first and gg < 2):
                            v.wait_ge(S("apre"), l * Q + g - 1)
                            v.wait_ge(S("asel"), l * Q + g - 1)
                        v.tensor_tensor(ohh[gg % 2][:, :, :], bc(iota16[:, 0:NB], 1, [P, TPR, NB]),
                                        bc(shiT[:, ds(g * TPR, TPR)], 2, [P, TPR, NB]), ALU.is_equal)
                        v.tensor_scalar(oh16[gg % 2][:, :], src16[gg // 2][:, gg % 2 * ROW:(gg % 2 + 1) * ROW], ipart[:, 0:1], None,
                                        ALU.is_equal).then_inc(S("oh"), 1)
                        if not (first and gg == 0):
                            select(g - 1, gg + 1)

                sources(0, True)
                with v.Fori(1, Q // 4) as i:
                    sources(i, False)
                select(Q - 1, 1)

                v.wait_ge(S("start_in"), 16 * (l + 1))
                V8 = scan_tile(2, 2).rearrange("p h c -> p (h c)").rearrange("p (c h) -> p c h", h=H2)
                AD, L, X, M = (scan_tile(i) for i in range(4))
                running_sum(H2, scan_tile(0, 2), lambda h: V8[:, :, h])
                for h in range(H):
                    v.wait_ge(S("xT"), l * H + h + 1)
                    i = v.tensor_tensor(X[:, h, :], bank(h)[0:Q, :], AD[:, h, :], ALU.add)
                    if h == H - 1:
                        i.then_inc(S("held"), 1)
                    else:
                        c.did(i)
                v.wait_ge(S("held"), l + 1)
                v.wait_ge(S("ael_in"), 16 * (l + 1))
                step(v.tensor_tensor(X, X, M, ALU.add))
                step(v.scalar_tensor_tensor(X, X, 0.2, X, ALU.mult, ALU.max))
                running_max(H, AD, lambda h: X[:, h, :])
                from_ends(H, M, lambda h: AD[:, h, :])
                step(v.tensor_tensor(M, M, L, ALU.max))
                v.tensor_tensor(X, X, M, ALU.subtract).then_inc(S("xm"), 1)
                v.tensor_tensor(L, L, M, ALU.subtract).then_inc(S("elm"), 1)
                v.wait_ge(S("exp"), 2 + 2 * l)
                running_sum(H, AD, lambda h: X[:, h, :])
                for h in range(H):
                    v.wait_ge(S("wb"), 1 + l * H + h + 1)
                    v.tensor_copy(aT[:, :, h].rearrange("p (q k) -> p k q", k=TPR),
                                  bank(h)[:, 0:T].rearrange("p (k q) -> p k q", k=TPR)).then_inc(S("wT"), 1)
                v.wait_ge(S("wT"), H * (l + 1))
                v.memset(acc, 0.0).then_inc(S("cleared"), 1)
                v.wait_ge(S("exp"), 3 + 2 * l)
                ends = scan_tile(2, 2).rearrange("p h c -> p (h c)").rearrange("p (c h) -> p h c", h=H2)
                c.did(v.tensor_copy(ends[:, 0:H, :], AD))
                v.tensor_copy(ends[:, H:H2, :], L).then_inc(S("el"), 1)

                with v.Fori(0, 2) as half:
                    for s in range(RS):
                        v.wait_ge(S(f"row{s}"), (half + 2 * l + 1) * 16 * SUP)
                        r = rows[:, s, :, :].rearrange("p j (h c) -> p j h c", c=C)
                        v.tensor_tensor(r, r, bc(aT[:, ds(half * (RS * SUP) + s * SUP, SUP), :], 3, [P, SUP, H, C]), ALU.mult).then_inc(S("msg"), 1)
                        selections(half * RS + s, (1 + l) * PAIRS, False, False)

                bias, nw, nb = (vec6[:, 3 * l + i, :] for i in range(3))
                v.wait_ge(S("back_in"), 32 * (l + 1))
                v.wait_ge(S("al0"), l + 1)
                v.wait_ge(S("al_in"), 16 * NB * (l + 1))
                share, loop = al[:, :, 0:H], al[:, :, H:H2]
                step(v.tensor_tensor(share, share, loop, ALU.add))
                step(v.tensor_scalar(share, share, 1e-16, None, ALU.add))
                step(v.reciprocal(share, share))
                step(v.tensor_tensor(loop, loop, share, ALU.mult))
                r = fl(nodes[1]).rearrange("p (b h c) -> p b h c", h=H, c=C)
                step(v.tensor_tensor(r, r, bc(loop, 3, [P, NB, H, C]), ALU.mult))
                step(v.tensor_tensor(nodes[1], nodes[1], bc(bias, 1, [P, NB, P]), ALU.add))
                v.tensor_tensor(nodes[0], nodes[0], nodes[1], ALU.add).then_inc(S("mixed"), 1)
                v.wait_ge(S("mixed"), l + 1)
                v.wait_ge(S("sum"), (2 + l) * PAIRS)
                step(v.tensor_tensor(fl(nodes[2]).rearrange("p (b h c) -> p b h c", h=H, c=C),
                                     acc[:, 0:NW].rearrange("p (b h c) -> p b h c", h=H, c=C), bc(share, 3, [P, NB, H, C]), ALU.mult))
                v.tensor_tensor(nodes[0], nodes[0], nodes[2], ALU.add).then_inc(S("x1"), 1)
                v.wait_ge(S("x1"), 2 + l)
                step(v.tensor_scalar(fl(nodes[0]), fl(nodes[0]), -10.0, 10.0, ALU.max, ALU.min))
                layer_norm(fl(nodes[0]), fl(nodes[0]), P)
                step(v.tensor_tensor(nodes[0], nodes[0], bc(nw, 1, [P, NB, P]), ALU.mult))
                step(v.tensor_tensor(nodes[0], nodes[0], bc(nb, 1, [P, NB, P]), ALU.add))
                v.tensor_scalar(fl(nodes[2]), fl(nodes[0]), 0.0, None, ALU.min).then_inc(S("elu"), 1)
                step(v.tensor_scalar(fl(nodes[0]), fl(nodes[0]), 0.0, None, ALU.max))
                v.wait_ge(S("elu_e"), l + 1)
                e = v.scalar_tensor_tensor(fl(nodes[0]), fl(nodes[2]), -1.0, fl(nodes[0]), ALU.add, ALU.add)
                if l == 0:
                    e.then_inc(S("tsrc"), 1)
                else:
                    step(e)
            v.wait_ge(S("x1_in"), 16)
            v.tensor_tensor(nodes[0], nodes[0], nodes[1], ALU.add).then_inc(S("final"), 1)


def kernel(**inputs):
    import numpy as _np
    import concourse.bacc as _bacc
    from concourse import mybir as _mybir
    from concourse.bass_utils import run_bass_kernel_spmd as _run

    nc = _bacc.Bacc("TRN2", target_bir_lowering=False, num_devices=1)
    arrays, aps = {}, {}
    for name, value in inputs.items():
        a = _np.ascontiguousarray(value)
        arrays["in_" + name] = a
        aps[name] = nc.dram_tensor("in_" + name, a.shape, _mybir.dt.from_np(a.dtype), kind="ExternalInput").ap()
    out = nc.dram_tensor("out_x", inputs["x"].shape, _mybir.dt.float32, kind="ExternalOutput").ap()
    build(nc, aps, out)
    r = _run(nc, [arrays], core_ids=[0])
    return r.results[0]["out_x"]
```

```python
import concourse.bass as bass
from concourse import mybir
from contextlib import ExitStack

F32 = mybir.dt.float32
BF16 = mybir.dt.bfloat16
I32 = mybir.dt.int32
ALU = mybir.AluOpType
ACT = mybir.ActivationFunctionType
AX = mybir.AxisListType
ds = bass.ds

P = 128
BIG = 1e30
NOWHERE = 8000


class Chain:

    def __init__(self, eng, sem):
        self.eng, self.sem, self.n = eng, sem, 0

    def did(self, instruction):
        instruction.then_inc(self.sem, 1)
        self.n += 1

    def wait(self, n=None):
        self.eng.wait_ge(self.sem, self.n if n is None else n)


def build(nc, A, out):
    N = A["x"].shape[0]
    E = A["src"].shape[0]
    NB = -(-N // P)
    LAST = N - (NB - 1) * P
    ROW = 512
    Q = -(-E // ROW)
    TPR = ROW // P
    T = Q * TPR
    EP = Q * ROW
    LROW = E - (Q - 1) * ROW
    NT = A["L0_gnn_W_Q"].shape[0]
    ET = A["L0_gnn_W_edge"].shape[0]
    H = A["L1_gnn_g1_att_src"].shape[0]
    C = P // H
    H2 = 2 * H
    NW = NB * P
    NWP = NW + P
    KV = 2 * P
    SUP = 16
    GPS = SUP // TPR
    NSUP = T // SUP
    RS = NSUP // 2
    NG = -(-NB // 4)
    EPS = 1e-5
    OF_ACT = range(3, SUP, 4)
    OF_DVE = [j for j in range(SUP) if j not in OF_ACT]
    Q_AFTER = {7: 0, 13: 1, 19: 2}
    HALF = 1536
    NGG = -(-NB // 3)
    PAIRS = T // 2
    PPS = SUP // 2
    UNIT = 2 * TPR
    UNITS = T // UNIT
    assert (NB - 1) % 3 == 0
    NCONST, N_E_IN, N_W_IN = 11, 13, 21
    assert EP == T * P and T % (2 * SUP) == 0 and RS * 2 == NSUP and NWP <= NOWHERE

    def dram(name, shape, dt=F32):
        return nc.dram_tensor(name, shape, dt).ap()

    kv_table = dram("kv_table", (N * ET, KV))
    v_spill = dram("v_spill", (NSUP, P, SUP * P))
    row_table = [dram(f"row_table{l}", (N, P)) for l in range(2)]
    rate_d = dram("rate_d", (2, EP))
    aedge_d = dram("aedge_d", (H2, EP))
    ends_d = dram("ends_d", (EP, H2))
    starts_d = [dram(f"starts_d{l}", (EP, H2)) for l in range(2)]
    loops_d = [dram(f"loops_d{l}", (EP, H2)) for l in range(2)]
    lo_d = dram("lo_d", (1, EP), BF16)
    x1_d = dram("x1_d", (P, NW))
    res_d = dram("res_d", (P, NW))
    hw_d = dram("hw_d", (P, NW))

    ctx = ExitStack()
    with ctx:
        def sb(name, shape, dt=F32):
            return ctx.enter_context(nc.sbuf_tensor(name, shape, dt))

        sems = {}

        def S(name):
            if name not in sems:
                sems[name] = ctx.enter_context(nc.semaphore(name))
            return sems[name]

        ps = ctx.enter_context(nc.psum_tensor("ps", [P, 8, 512], F32))

        def bank(i):
            return ps[:, i, :]

        def q_bank(g):
            return bank(6 + g % 2 if g < len(Q_AFTER) else g % 2)

        acc = ps[:, :, :].rearrange("p b c -> p (b c)")[:, 0:NWP]

        ring = sb("ring", [P, RS * SUP * P])
        weights = sb("weights", [P, (3 * NT + ET + 4) * P])
        node = sb("node", [P, 3 * NW])
        nodes = [node[:, i * NW:(i + 1) * NW].rearrange("p (b f) -> p b f", f=P) for i in range(3)]

        def scan_tile(i, n=1):
            return node[0:Q, i * H * ROW:(i + n) * H * ROW].rearrange("p (h c) -> p h c", c=ROW)

        def cut(at, n):
            return ring[:, at:at + n]

        hTt = [cut(i * NW, NW) for i in range(NT)]
        KT = cut(NT * NW, NW)
        QT = cut((NT + 1) * NW, NWP)
        free0 = (NT + 1) * NW + NWP
        stg = [cut(free0 + i * ET * KV, ET * KV).rearrange("p (t f) -> p t f", f=KV) for i in range(3)]
        free1 = free0 + 2 * ET * KV
        eraw = ring[0:Q, free1:free1 + 6 * ROW].rearrange("p (a c) -> p a c", c=ROW)
        assert free1 + 6 * ROW <= RS * SUP * P
        ef = node[0:Q, 0:10 * ROW].rearrange("p (a c) -> p a c", c=ROW)
        zero_rows = node[0:Q, 10 * ROW:10 * ROW + H2 * ROW]
        kv_buf = [cut(i, SUP * KV).rearrange("p (j f) -> p j f", f=KV) for i in (free0, 0)]
        at = SUP * KV
        kTb = [cut(at + i * ROW, ROW) for i in range(2)]
        hid = [cut(at + (2 + i) * ROW, ROW) for i in range(2)]
        tw = [cut(at + (4 + i) * ROW, ROW) for i in range(2)]
        assert at + 6 * ROW <= (NT + 1) * NW
        aeb = ring[0:H2, free1:free1 + GPS * ROW]
        rateb = [ring[0:2, at + 6 * ROW + i * GPS * ROW:at + 6 * ROW + (i + 1) * GPS * ROW] for i in range(2)]
        assert at + 6 * ROW + 2 * GPS * ROW <= (NT + 1) * NW
        v_buf = [cut(i * SUP * P, SUP * P).rearrange("p (j f) -> p j f", f=P) for i in range(4)]
        onehots = [cut((4 + i) * SUP * P, SUP * P) for i in range(4)]
        kv_over = cut(8 * SUP * P, (NB - 1) * KV).rearrange("p (b f) -> p b f", f=KV)
        over = cut(8 * SUP * P + (NB - 1) * KV, (NB - 1) * P).rearrange("p (b f) -> p b f", f=P)
        assert 2 * ET * KV == SUP * KV and 8 * SUP * P + 3 * (NB - 1) * P <= RS * SUP * P
        assert (NB - 1) % 8 == 0 and NSUP % 4 == 2
        zt = cut(0, NB * KV).rearrange("p (b f) -> p b f", f=KV)
        zT = [cut(NB * KV + i * NW, NW) for i in range(2)]
        hT = cut(NB * KV + 2 * NW, NW)
        rows = ring[:, :].rearrange("p (s j f) -> p s j f", s=RS, f=P)
        aT = weights[:, 0:T * H].rearrange("p (t h) -> p t h", h=H)
        wqkv = weights[:, 0:3 * NT * P].rearrange("p (m t f) -> p m t f", m=3, t=NT)
        wedge = weights[:, 3 * NT * P:(3 * NT + ET) * P]
        tmpw = weights[:, (3 * NT + ET) * P:(3 * NT + ET + 4) * P]
        ipw1 = weights[:, 0:KV]
        ipw2 = weights[:, KV:2 * KV].rearrange("p (a f) -> p a f", a=2)
        ipv = weights[:, 2 * KV:2 * KV + 5 * P]

        ident = sb("ident", [P, P])
        iota = sb("iota", [P, 2 * P])
        iota16 = sb("iota16", [P, P], BF16)
        ipart = sb("ipart", [P, 1])
        lncol = sb("lncol", [P, 4])
        tri = sb("tri", [P, P])
        ones = sb("ones", [P, P])
        cont = sb("cont", [Q, ROW], BF16)
        contn = sb("contn", [Q, ROW], BF16)
        pre = sb("pre", [Q, ROW], BF16)
        post = sb("post", [Q, ROW], BF16)
        pen = sb("pen", [Q, ROW], BF16)
        prepen = sb("prepen", [Q, ROW], BF16)
        rowf = sb("rowf", [H2, 3, Q])
        flags = sb("flags", [Q, 3, H2])
        carry = sb("carry", [H2, Q + 1])
        relT = sb("relT", [P, T])
        relbT = sb("relbT", [P, T])
        kvT = sb("kvT", [P, T + 2 * SUP], I32)
        srcT = sb("srcT", [P, T], I32)
        loT = sb("loT", [P, T], BF16)
        hiT = sb("hiT", [P, T], BF16)
        shiT = sb("shiT", [P, T], BF16)
        idx = sb("idx", [P, RS * SUP], I32)
        d0 = sb("d0", [1, T], I32)
        b0 = sb("b0", [1, T], I32)
        sc = sb("sc", [P, T])
        nsc = sb("nsc", [P, T])
        border = sb("border", [1, NB - 1], I32)
        endi = sb("endi", [P, NB], I32)
        starti = sb("starti", [P, NB], I32)
        deg = sb("deg", [P, NB])
        mae = sb("mae", [P, NB, H2])
        ncol = sb("ncol", [P, NB, H2])
        nst = sb("nst", [P, NB, H2])
        al = sb("al", [P, NB, H2])
        stats = sb("stats", [P, NB, 6])
        mv = sb("mv", [P, NB, 2])
        rstd = sb("rstd", [P, NB])
        vec6 = sb("vec6", [P, 6, P])
        Wx = sb("Wx", [P, P + H2])
        Wm = sb("Wm", [P, 2, H])
        taw2 = sb("taw2", [P, P])
        lhs2 = sb("lhs2", [2, P])
        lnwb = sb("lnwb", [2, P])
        tacol = sb("tacol", [P, 2])
        wk = sb("wk", [P, 2 * ROW])
        wk2 = [wk[:, i * ROW:(i + 1) * ROW] for i in range(2)]
        src16 = [sb(f"src16_{i}", [P, 2 * ROW], BF16) for i in range(2)]
        oh16 = [sb(f"oh16_{i}", [P, 2 * ROW], BF16) for i in range(2)]
        ohh = [sb(f"ohh{i}", [P, 2 * TPR, NB], BF16) for i in range(2)]
        A3 = sb("A3", [P, 3, NB * H], BF16)
        a3r = sb("a3r", [P, NB * H])
        smal = sb("smal", [P, 16])
        nb_ = sb("nb_", [P, NB])
        ticks = sb("ticks", [P, 4])
        lhm = sb("lhm", [2, 1])
        blk = sb("blk", [Q, TPR])

        block = ctx.enter_context(nc.Block())

        def row_of(ap):
            return ap.rearrange("(a n) -> a n", a=1)

        def spread(ap, n=P):
            return row_of(ap).to_broadcast([n, ap.shape[0]])

        def node_blocks(table, f=P):
            return (table[0:(NB - 1) * P, :].rearrange("(b p) f -> p b f", p=P), table[(NB - 1) * P:N, :])

        def bc(ap, axis, shape):
            return ap.unsqueeze(axis).to_broadcast(shape)

        @block.sync
        def _(sp):
            D, DP, DN, SR, TY, EW = [eraw[:, i, :] if i == 5 else eraw[:, i, :].bitcast(I32) for i in range(6)]
            xa, xb = node_blocks(A["x"])
            sp.dma_start(nodes[0][:, 0:NB - 1, :], xa).then_inc(S("x_in"), 16)
            sp.wait_ge(S("xpad"), 1)
            sp.dma_start(nodes[0][0:LAST, NB - 1, :], xb).then_inc(S("x_in"), 16)
            sp.wait_ge(S("epad"), 2)

            def edges(dst, src, shift):
                if shift < 0:
                    sp.dma_start(dst[0:1, 1:ROW], src[0:ROW - 1].unsqueeze(0)).then_inc(S("e_in"), 16)
                    sp.dma_start(dst[1:Q - 1, :], src[ROW - 1:(Q - 1) * ROW - 1].rearrange("(q c) -> q c", c=ROW)).then_inc(S("e_in"), 16)
                else:
                    sp.dma_start(dst[0:Q - 1, :], src[shift:shift + (Q - 1) * ROW].rearrange("(q c) -> q c", c=ROW)).then_inc(S("e_in"), 16)
                n = LROW - shift
                sp.dma_start(dst[Q - 1:Q, 0:n], src[(Q - 1) * ROW + shift:E].unsqueeze(0)).then_inc(S("e_in"), 16)

            edges(D, A["dst"], 0)
            edges(DP, A["dst"], -1)
            edges(DN, A["dst"], 1)
            edges(SR, A["src"], 0)
            edges(TY, A["edge_type_8"], 0)
            edges(EW, A["edge_weight"], 0)
            assert 13 == N_E_IN
            with nc.allow_non_contiguous_dma("one destination per tile"):
                sp.dma_start(d0[0:1, :], A["dst"].unsqueeze(0)[:, 0:E:P]).then_inc(S("d0_in"), 16)
                sp.dma_start(tacol[:, 0:1], A["L1_gnn_ta_ln_b"].unsqueeze(1)).then_inc(S("ta_in"), 16)
                sp.dma_start(tacol[:, 1:2], A["L1_gnn_ta_b2"].unsqueeze(1)).then_inc(S("ta_in"), 16)
                for a in range(2):
                    sp.dma_start(lncol[:, a:a + 1], A["L1_gnn_ip_ln_w"][a * P:(a + 1) * P].unsqueeze(1)).then_inc(S("ta_in"), 16)
                    sp.dma_start(lncol[:, 2 + a:3 + a], A["L1_gnn_ip_ln_b"][a * P:(a + 1) * P].unsqueeze(1)).then_inc(S("ta_in"), 16)
            sp.wait_ge(S("zeros"), 1)
            for l in range(2):
                sp.dma_start(starts_d[l].rearrange("(q c) h -> q (c h)", c=ROW), zero_rows).then_inc(S("zero_out"), 16)
            sp.wait_ge(S("lo_ready"), 1)
            sp.dma_start(lo_d.rearrange("a (q c) -> q (a c)", c=ROW), ef[:, 8, 0:ROW // 2].bitcast(BF16)).then_inc(S("lo_out"), 16)
            sp.wait_ge(S("rate_ready"), 1)
            sp.dma_start(rate_d.rearrange("a (q c) -> q a c", c=ROW), ef[:, 0:7:6, :]).then_inc(S("rate_out"), 16)

            def kv_store(b):
                sp.wait_ge(S("kv_dve"), b + 1)
                sp.wait_ge(S("kv_act"), b + 1)
                n = LAST if b == NB - 1 else P
                sp.dma_start(kv_table[b * P * ET:(b * P + n) * ET, :].rearrange("(p t) f -> p t f", t=ET),
                             stg[b % 3][0:n, :, :]).then_inc(S(f"kv_out{b % 3}"), 16)

            sp.wait_ge(S("lo_out"), 16)
            sp.wait_ge(S("rate_out"), 16)
            for b in range(NB):
                kv_store(b)

            sp.wait_ge(S("q"), NG)

            def walk1(i, h, first):
                s = 2 * i + h
                if not first:
                    sp.wait_ge(S("m1"), (s - 1) * GPS)
                sp.dma_start(rateb[h], rate_d[:, ds(s * GPS * ROW, GPS * ROW)]).then_inc(S(f"rate_in{h}"), 16)
                sp.wait_ge(S(f"got{h}"), (i + 1) * 16 * SUP)
                sp.dma_start(v_spill[ds(s, 1), :, :].rearrange("a p (j f) -> p (a j) f", f=P),
                             kv_buf[h][:, :, P:KV]).then_inc(S(f"spill{h}"), 16)
                if not (first and h == 0):
                    ae_store(s - 1)

            def ae_store(s):
                sp.wait_ge(S("ae"), s * GPS + GPS)
                sp.dma_start(aedge_d[:, ds(s * GPS * ROW, GPS * ROW)], aeb).then_inc(S("ae_out"), 16)

            for h in range(2):
                walk1(0, h, True)
            with sp.Fori(1, NSUP // 2) as i:
                for h in range(2):
                    walk1(i, h, False)
            ae_store(NSUP - 1)

            sp.wait_ge(S("ae_out"), 16 * NSUP)
            sp.wait_ge(S("sm0"), 1)
            sp.dma_start(scan_tile(0, 2), aedge_d.rearrange("h (q c) -> q h c", c=ROW)).then_inc(S("ae_in"), 16)
            for h in range(2):
                sp.wait_ge(S(f"spill{h}"), 16 * NSUP // 2)

            def load_v(s, k):
                if not isinstance(s, int) or s >= 4:
                    sp.wait_ge(S("sum"), s - 3)
                sp.dma_start(v_buf[k], v_spill[ds(s, 1), :, :].rearrange("a p (j f) -> p (a j) f", f=P)).then_inc(S(f"v_in{k}"), 16)

            for s in range(6):
                load_v(s, s % 4)
            sp.wait_ge(S("mae1"), 1)
            sp.dma_start(ends_d.rearrange("(q c) h -> q (c h)", c=ROW),
                         scan_tile(0, 2).rearrange("p h c -> p (h c)")).then_inc(S("ends_out"), 16)
            with sp.Fori(0, (NSUP - 6) // 4) as i:
                for u in range(4):
                    load_v(4 * i + (6 + u), (6 + u) % 4)

            sp.wait_ge(S("ends_out"), 16)
            sp.dma_start(nodes[0][:, 0:NB - 1, :], xa).then_inc(S("x_in"), 16)
            sp.dma_start(nodes[0][0:LAST, NB - 1, :], xb).then_inc(S("x_in"), 16)
            sp.wait_ge(S("x1"), 1)
            sp.dma_start(x1_d, nodes[0].rearrange("p b f -> p (b f)")).then_inc(S("x1_out"), 16)
            sp.dma_start(ipw1, A["L1_gnn_ip_w1"]).then_inc(S("ip_in"), 16)
            sp.dma_start(ipw2, A["L1_gnn_ip_w2"].rearrange("(a p) f -> p a f", p=P)).then_inc(S("ip_in"), 16)
            at_ = 0
            for name in ("ip_b1", "ip_b2", "pn_w", "pn_b"):
                n = A["L1_gnn_" + name].shape[0]
                sp.dma_start(ipv[:, at_:at_ + n], spread(A["L1_gnn_" + name])).then_inc(S("ip_in"), 16)
                at_ += n

            for l in range(2):
                g = f"L1_gnn_g{l + 1}_"
                sp.wait_ge(S("x1"), l + 1)
                sp.dma_start(Wx[:, 0:P], A[g + "w"]).then_inc(S("gw_in"), 16)
                sp.dma_start(wk[:, 0:P], spread(A[g + "att_src"].rearrange("h c -> (h c)"))).then_inc(S("gw_in"), 16)
                sp.dma_start(wk[:, P:2 * P], spread(A[g + "att_dst"].rearrange("h c -> (h c)"))).then_inc(S("gw_in"), 16)
                ra, rb = node_blocks(row_table[l])
                for q in range(NGG):
                    sp.wait_ge(S("hw"), l * NGG + q + 1)
                    if q < NGG - 1:
                        sp.dma_start(ra[:, 3 * q:3 * q + 3, :], nodes[1][:, 3 * q:3 * q + 3, :]).then_inc(S("row_out"), 16)
                    else:
                        sp.dma_start(rb, nodes[1][0:LAST, NB - 1, :]).then_inc(S("row_out"), 16)

                def lo_in(i, h, first):
                    if not first:
                        sp.wait_ge(S("lo_oh"), 2 * i + (l * UNITS + h - 1))
                    sp.dma_start(src16[h][:, :], lo_d[:, ds((2 * i + h) * 2 * ROW, 2 * ROW)].to_broadcast([P, 2 * ROW])).then_inc(S(f"lo_in{h}"), 16)

                for h in range(2):
                    lo_in(0, h, True)
                sp.wait_ge(S("tsrc"), (4 + l) * NG)
                sp.dma_start(hw_d, nodes[1].rearrange("p b f -> p (b f)")).then_inc(S("hw_out"), 16)
                sp.dma_start(res_d, nodes[0].rearrange("p b f -> p (b f)")).then_inc(S("res_out"), 16)
                with sp.Fori(1, UNITS // 2) as i:
                    for h in range(2):
                        lo_in(i, h, False)
                sp.wait_ge(S("held"), l + 1)
                sp.dma_start(scan_tile(3), aedge_d[l * H:(l + 1) * H, :].rearrange("h (q c) -> q h c", c=ROW)).then_inc(S("ael_in"), 16)
                sp.wait_ge(S("el"), l + 1)
                sp.dma_start(loops_d[l].rearrange("(q c) h -> q (c h)", c=ROW),
                             scan_tile(2, 2).rearrange("p h c -> p (h c)")).then_inc(S("loop_out"), 16)
                sp.wait_ge(S("loop_out"), 16 * (l + 1))
                sp.wait_ge(S("wT"), H * (l + 1))
                sp.dma_start(nodes[0].rearrange("p b f -> p (b f)"), res_d).then_inc(S("back_in"), 16)
                sp.dma_start(nodes[1].rearrange("p b f -> p (b f)"), hw_d).then_inc(S("back_in"), 16)
            sp.wait_ge(S("x1"), 3)
            sp.dma_start(nodes[1].rearrange("p b f -> p (b f)"), x1_d).then_inc(S("x1_in"), 16)
            oa, ob = node_blocks(out)
            for g in range(NG):
                sp.wait_ge(S("final"), g + 1)
                lo, hi = 4 * g, min(4 * g + 4, NB - 1)
                if hi > lo:
                    sp.dma_start(oa[:, lo:hi, :], nodes[0][:, lo:hi, :]).then_inc(S("out"), 16)
            sp.dma_start(ob, nodes[0][0:LAST, NB - 1, :]).then_inc(S("out"), 16)
            sp.wait_ge(S("out"), 16 * NG)
            assert (NB - 1) % 4 == 0

        @block.gpsimd
        def _(pool):
            pool.memset(nodes[0][:, NB - 1, :], 0.0).then_inc(S("xpad"), 1)
            c = Chain(pool, S("const"))
            c.did(pool.memset(ident[:, :], 0.0))
            pool.memset(eraw[:, 0:3, :].bitcast(I32), NOWHERE).then_inc(S("epad"), 1)
            pool.memset(eraw[:, 3:6, :], 0.0).then_inc(S("epad"), 1)
            c.did(pool.memset(ticks[:, :], 0.0))
            c.did(pool.memset(kvT[:, T:T + 2 * SUP], 0))
            c.did(pool.memset(tri[:, :], 1.0))
            c.did(pool.memset(ones[:, :], 1.0))
            c.did(pool.memset(ncol[:, :, :], 0.0))
            c.did(pool.iota(iota[:, :], [[1, 2 * P]], base=0, channel_multiplier=0, allow_small_or_imprecise_dtypes=True))
            c.did(pool.iota(iota16[:, :], [[1, P]], base=0, channel_multiplier=0, allow_small_or_imprecise_dtypes=True))
            c.did(pool.iota(ipart[:, :], [[0, 1]], base=0, channel_multiplier=-1, allow_small_or_imprecise_dtypes=True))
            c.wait()
            c.did(pool.affine_select(out=ident[:, :], in_=ident[:, :], compare_op=ALU.not_equal, fill=1.0, base=0,
                                     pattern=[[-1, P]], channel_multiplier=1))
            c.did(pool.affine_select(out=tri[:, :], in_=tri[:, :], compare_op=ALU.is_ge, fill=0.0, base=0,
                                     pattern=[[1, P]], channel_multiplier=-1))
            assert c.n == NCONST
            pool.wait_ge(S("hTt"), 2 * NT)
            pool.memset(zero_rows, 0.0).then_inc(S("zeros"), 1)

            def tick(n):
                if not (isinstance(n, int) and n == 0):
                    pool.wait_ge(S("tick"), n)
                pool.tensor_tensor(ticks[:, 0:1], ticks[:, 1:2], ticks[:, 2:3], ALU.add).then_inc(S("tick"), 1)

            def walk1(i, h, first):
                s = 2 * i + h
                pool.wait_ge(S("idx"), s + 1)
                if not first:
                    pool.wait_ge(S("kT"), (s - 1) * GPS)
                    pool.wait_ge(S(f"spill{h}"), 16 * i)
                tick(s)
                for j in range(SUP):
                    pool.indirect_dma_start(kv_buf[h][:, j, :], None, kv_table,
                                            bass.IndirectOffsetOnAxis(ap=idx[:, h * SUP + j:h * SUP + j + 1], axis=0)).then_inc(S(f"got{h}"), 16)

            for h in range(3):
                pool.wait_ge(S(f"kv_out{h}"), 16 * ((NB + 2 - h) // 3))
            pool.wait_ge(S("rate_ready"), 1)
            walk1(0, 0, True)
            pool.wait_ge(S("q"), NG)
            walk1(0, 1, True)
            with pool.Fori(1, NSUP // 2) as i:
                for h in range(2):
                    walk1(i, h, False)

            pool.wait_ge(S("border_idx"), 1)
            for h in range(2):
                pool.wait_ge(S(f"spill{h}"), 16 * NSUP // 2)
            for b in range(NB - 1):
                pool.indirect_dma_start(kv_over[:, b, :], None, kv_table,
                                        bass.IndirectOffsetOnAxis(ap=idx[:, b:b + 1], axis=0)).then_inc(S("v_over"), 16)
            pool.wait_ge(S("ends_out"), 16)
            pool.wait_ge(S("endi"), 2)
            for b in range(NB):
                n = LAST if b == NB - 1 else P
                pool.indirect_dma_start(ncol[0:n, b, :], None, ends_d,
                                        bass.IndirectOffsetOnAxis(ap=endi[0:n, b:b + 1], axis=0)).then_inc(S("sums_in"), 16)

            for l in range(2):
                pool.wait_ge(S("nst"), 2 * (l + 1))
                pool.wait_ge(S("zero_out"), 32)
                for b in range(NB):
                    n = LAST if b == NB - 1 else P
                    pool.indirect_dma_start(starts_d[l], bass.IndirectOffsetOnAxis(ap=starti[0:n, b:b + 1], axis=0),
                                            nst[0:n, b, :], None).then_inc(S("start_out"), 16)
                pool.wait_ge(S("row_out"), 16 * NGG * (l + 1))
                pool.memset(al[:, :, :], 0.0).then_inc(S("al0"), 1)
                for half in range(2):
                    if l + half == 0:
                        pool.wait_ge(S("idx"), NSUP + 2)
                        pool.wait_ge(S("v_over"), 16 * (NB - 1))
                    if l + half > 0:
                        for s in range(RS):
                            pool.wait_ge(S(f"row{s}"), (2 * l + half) * 16 * SUP)
                    pool.tensor_copy(idx[:, :], srcT[:, half * RS * SUP:(half + 1) * RS * SUP]).then_inc(S("idx"), 1)
                    pool.wait_ge(S("idx"), NSUP + 2 * l + half + 3)
                    for s in range(RS):
                        if half:
                            pool.wait_ge(S("sum"), NSUP + 1 + l * PAIRS + (s + 1) * PPS)
                        for j in range(SUP):
                            pool.indirect_dma_start(rows[:, s, j, :], None, row_table[l],
                                                    bass.IndirectOffsetOnAxis(ap=idx[:, s * SUP + j:s * SUP + j + 1], axis=0)).then_inc(S(f"row{s}"), 16)

                pool.wait_ge(S("loop_out"), 16 * (l + 1))
                pool.wait_ge(S("al0"), l + 1)
                for b in range(NB):
                    n = LAST if b == NB - 1 else P
                    pool.indirect_dma_start(al[0:n, b, :], None, loops_d[l],
                                            bass.IndirectOffsetOnAxis(ap=endi[0:n, b:b + 1], axis=0)).then_inc(S("al_in"), 16)

        @block.scalar
        def _(act):
            def root(k):
                act.wait_ge(S("var"), k + 1)
                act.activation(rstd[:, :], rstd[:, :], ACT.Sqrt).then_inc(S("std"), 1)

            def turned(k, dst, scale=None, bias=None):
                for g in range(NG):
                    n = min(4, NB - 4 * g) * P
                    act.wait_ge(S("tr"), k * NG + g + 1)
                    o, i = dst[:, 4 * g * P:4 * g * P + n], bank((k * NG + g) % 2)[:, 0:n]
                    if scale is None:
                        act.activation(o, i, ACT.Copy).then_inc(S("tr_sb"), 1)
                    else:
                        act.activation(o, i, ACT.Identity, bias=bias, scale=scale).then_inc(S("tr_sb"), 1)

            act.dma_start(nodes[2][:, :, :].rearrange("p b f -> p (b f)").bitcast(I32)[:, 0:N], spread(A["node_type_4"])).then_inc(S("nt_in"), 16)
            for dst, src in ((tmpw[:, 0:P], A["L1_gnn_g1_ew"]), (tmpw[:, P:2 * P], A["L1_gnn_g2_ew"]),
                             (tmpw[:, 2 * P:3 * P], spread(A["L1_gnn_g1_att_edge"].rearrange("h c -> (h c)"))),
                             (tmpw[:, 3 * P:4 * P], spread(A["L1_gnn_g2_att_edge"].rearrange("h c -> (h c)"))),
                             (wk[:, 0:P], A["L1_gnn_ta_w1"].to_broadcast([P, P])),
                             (wk[:, P:2 * P], spread(A["L1_gnn_ta_b1"])),
                             (lhs2[0:1, :], A["L1_gnn_ta_w1"]), (lhs2[1:2, :], row_of(A["L1_gnn_ta_b1"])),
                             (lnwb[:, :], spread(A["L1_gnn_ta_ln_w"], 2)), (smal[:, 8:8 + ET], spread(A["L0_gnn_mu"])),
                             (taw2[:, :], A["L1_gnn_ta_w2"]),
                             (wqkv[:, 0, :, :], A["L0_gnn_W_K"].rearrange("t i o -> i t o")),
                             (wqkv[:, 1, :, :], A["L0_gnn_W_Q"].rearrange("t i o -> i t o")),
                             (wqkv[:, 2, :, :], A["L0_gnn_W_V"].rearrange("t i o -> i t o")),
                             (wedge.rearrange("p (t o) -> p t o", o=P), A["L0_gnn_W_edge"].rearrange("t i o -> i t o"))):
                act.dma_start(dst, src).then_inc(S("w_in"), 16)
            for i, (g, name) in enumerate((l, n) for l in (1, 2) for n in ("g{}_b", "n{}_w", "n{}_b")):
                act.dma_start(vec6[:, i, :], spread(A["L1_gnn_" + name.format(g)])).then_inc(S("w_in"), 16)
            root(0)
            turned(0, KT)
            for g in range(NG):
                n = min(512, NW - g * 512)
                act.wait_ge(S("k"), g + 1)
                act.activation(KT[:, g * 512:g * 512 + n], bank(6 + g % 2)[:, 0:n], ACT.Copy).then_inc(S("k_sb"), 1)
            act.wait_ge(S("rvar"), 1)
            act.activation(ef[:, 6, :], ef[:, 6, :], ACT.Sqrt).then_inc(S("rstd0"), 1)

            def take_q(g):
                n = min(512, NW - g * 512)
                act.wait_ge(S("q"), g + 1)
                act.activation(QT[:, g * 512:g * 512 + n], q_bank(g)[:, 0:n], ACT.Copy).then_inc(S("q_sb"), 1)

            for b in range(NB):
                act.wait_ge(S("kv"), b + 1)
                if b >= 3:
                    act.wait_ge(S(f"kv_out{b % 3}"), 16 * (b // 3))
                act.activation(stg[b % 3][:, ET // 2:ET, 0:P], bank(2 * (b % 2) + 1).rearrange("p (t f) -> p t f", f=P), ACT.Copy).then_inc(S("kv_act"), 1)
                if b in Q_AFTER:
                    take_q(Q_AFTER[b])
            for g in range(len(Q_AFTER), NG):
                take_q(g)

            def walk1(i, first):
                for gg in range(2 * GPS):
                    g = 2 * GPS * i + gg
                    f = first and gg < 2
                    act.wait_ge(S("kT"), g + 1)
                    if not f:
                        act.wait_ge(S("kq"), g - 1)
                    act.activation(kTb[gg % 2], bank(gg % 2), ACT.Copy).then_inc(S("kT_sb"), 1)
                    act.wait_ge(S("m1"), g + 1)
                    if not f:
                        act.wait_ge(S("m2"), g - 1)
                    act.activation(hid[gg % 2], bank(4), ACT.Relu, bias=tacol[:, 0:1]).then_inc(S("relu"), 1)
                    act.wait_ge(S("m2"), g + 1)
                    if not f:
                        act.wait_ge(S("m3"), g - 1)
                    act.activation(tw[gg % 2], bank(5), ACT.Tanh, bias=tacol[:, 1:2]).then_inc(S("tanh"), 1)

            act.wait_ge(S("ta_in"), 16 * 6)
            walk1(0, True)
            with act.Fori(1, NSUP // 2) as i:
                walk1(i, False)
            act.wait_ge(S("xm"), 1)
            act.activation(scan_tile(0)[:, 0, :], scan_tile(0)[:, 0, :], ACT.Exp).then_inc(S("exp"), 1)

            act.wait_ge(S("nsc"), 1)

            def walk2(s, h):
                if not isinstance(s, int) or s >= 4:
                    act.wait_ge(S("sum"), s - 3)
                for relu in (False, True):
                    if relu:
                        act.wait_ge(S("dist"), s + 1)
                    for j in OF_ACT:
                        t = s * SUP + j
                        o = onehots[h][:, j * P:(j + 1) * P]
                        if relu:
                            a = act.activation(o, o, ACT.Relu, bias=sc[:, ds(t, 1)], scale=nsc[:, ds(t, 1)])
                        else:
                            a = act.activation(o, iota[:, 0:P], ACT.Abs, bias=relbT[:, ds(t, 1)], scale=-1.0)
                    a.then_inc(S("sel_act" if relu else "dist"), 1)

            for s in range(6):
                walk2(s, s % 4)
            with act.Fori(0, (NSUP - 6) // 4) as i:
                for u in range(4):
                    walk2(4 * i + (6 + u), (6 + u) % 4)

            root(1)
            turned(1, hT)
            for g in range(-(-NB // 2)):
                n = min(2, NB - 2 * g)
                act.wait_ge(S("z_sb"), g + 1)
                act.activation(zt[:, 2 * g:2 * g + n, :], zt[:, 2 * g:2 * g + n, :], ACT.Relu).then_inc(S("z_relu"), 1)
            root(2)
            turned(2, zT[0], lncol[:, 0:1], lncol[:, 2:3])
            turned(3, zT[1], lncol[:, 1:2], lncol[:, 3:4])
            root(3)
            for l in range(2):
                turned(4 + l, hT)

                def digits(i, first):
                    for h in range(2):
                        act.wait_ge(S(f"lo_in{h}"), 16 * (i + (l * UNITS // 2 + 1)))
                        if not first:
                            act.wait_ge(S("apre"), 2 * i + (l * UNITS + h - 1))
                        act.activation(oh16[h][:, :], src16[h][:, :], ACT.Abs, bias=ipart[:, 0:1]).then_inc(S("lo_abs"), 1)
                        act.wait_ge(S("lo_abs"), 2 * i + (l * UNITS + h + 1))
                        act.activation(oh16[h][:, :], oh16[h][:, :], ACT.Relu, bias=ones[:, 0:1], scale=-1.0).then_inc(S("lo_oh"), 1)

                digits(0, True)
                with act.Fori(1, UNITS // 2) as i:
                    digits(i, False)
                act.wait_ge(S("row_out"), 16 * NGG * (l + 1))
                act.wait_ge(S("hw_out"), 16 * (l + 1))
                act.wait_ge(S("res_out"), 16 * (l + 1))
                act.wait_ge(S("start_out"), 16 * NB * (l + 1))
                act.dma_start(scan_tile(2, 2).rearrange("p h c -> p (h c)"),
                              starts_d[l].rearrange("(q c) h -> q (c h)", c=ROW)).then_inc(S("start_in"), 16)
                act.wait_ge(S("xm"), 2 + l)
                act.activation(scan_tile(2), scan_tile(2), ACT.Exp).then_inc(S("exp"), 1)
                act.wait_ge(S("elm"), 1 + l)
                act.activation(scan_tile(1), scan_tile(1), ACT.Exp).then_inc(S("exp"), 1)
                root(4 + l)
                for g in range(NG):
                    act.wait_ge(S("elu"), l * NG + g + 1)
                    e = nodes[2][:, 4 * g:min(4 * g + 4, NB), :]
                    act.activation(e, e, ACT.Exp).then_inc(S("elu_e"), 1)

        @block.tensor
        def _(pe):
            def turn(k, came, blocks, groups=range(NG)):
                for g in groups:
                    n = k * NG + g
                    pe.wait_ge(S("tsrc"), came + g + 1)
                    if n >= 2:
                        pe.wait_ge(S("tr_sb"), n - 1)
                    nb = min(4, NB - 4 * g)
                    for j in range(nb):
                        t = pe.transpose(bank(n % 2)[:, j * P:(j + 1) * P], blocks(4 * g + j), ident[:, :])
                    t.then_inc(S("tr"), 1)

            def carried(k, n, tile, back):
                pe.wait_ge(S("local"), k + 1)
                pe.transpose(bank(7)[0:n, 0:Q], tile[:, :, 0 if back else ROW - 1], ident[0:Q, 0:Q]).then_inc(S("carT"), 1)
                pe.wait_ge(S("carS"), k + 1)
                pe.transpose(bank(7)[0:Q, P:P + n], carry[0:n, 1:Q + 1] if back else carry[0:n, 0:Q],
                             ident[0:n, 0:n]).then_inc(S("carB"), 1)

            pe.wait_ge(S("const"), NCONST)
            turn(0, 0, lambda b: nodes[1][:, b, :])

            pe.wait_ge(S("w_in"), 16 * N_W_IN)
            for g in range(NG):
                pe.wait_ge(S("hTt"), NT if (g + 1) * 512 <= HALF else 2 * NT)
                if g >= 2:
                    pe.wait_ge(S("k_sb"), g - 1)
                n = min(512, NW - g * 512)
                for t in range(NT):
                    mm = pe.matmul(bank(6 + g % 2)[:, 0:n], wqkv[:, 0, t, :], hTt[t][:, g * 512:g * 512 + n],
                                   start=(t == 0), stop=(t == NT - 1))
                mm.then_inc(S("k"), 1)
            def q_group(g):
                if g >= 2:
                    pe.wait_ge(S("q_sb"), g - 1)
                n = min(512, NW - g * 512)
                for t in range(NT):
                    mm = pe.matmul(q_bank(g)[:, 0:n], wqkv[:, 1, t, :], hTt[t][:, g * 512:g * 512 + n],
                                   start=(t == 0), stop=(t == NT - 1))
                mm.then_inc(S("q"), 1)

            pe.wait_ge(S("tr_sb"), NG)
            pe.wait_ge(S("k_sb"), NG)
            pe.wait_ge(S("we"), 1)
            for b in range(NB):
                h = b % 2
                if b >= 2:
                    pe.wait_ge(S("kv_dve"), b - 1)
                    pe.wait_ge(S("kv_act"), b - 1)
                for half in range(2):
                    pe.matmul(bank(2 * h + half), KT[:, b * P:(b + 1) * P], wedge[:, half * 512:(half + 1) * 512],
                              start=True, stop=True)
                for t in range(NT):
                    mm = pe.matmul(bank(4 + h)[:, 0:P], hTt[t][:, b * P:(b + 1) * P], wqkv[:, 2, t, :],
                                   start=(t == 0), stop=(t == NT - 1))
                mm.then_inc(S("kv"), 1)
                if b in Q_AFTER:
                    q_group(Q_AFTER[b])
            pe.wait_ge(S("ef"), 1)
            pe.wait_ge(S("q_sb"), len(Q_AFTER))
            pe.wait_ge(S("kv_dve"), NB)
            pe.wait_ge(S("kv_act"), NB)
            for a, e in enumerate((4, 1, 7, 5, 2, 3, 9)):
                for k in range(TPR):
                    t = pe.transpose(bank(a)[:, k * Q:(k + 1) * Q], ef[:, e, k * P:(k + 1) * P], ident[0:Q, 0:Q])
                t.then_inc(S("efT"), 1)
            pe.wait_ge(S("flags"), 1)
            for a in range(3):
                t = pe.transpose(bank(7)[0:H2, a * Q:(a + 1) * Q], flags[:, a, :], ident[0:Q, 0:Q])
            t.then_inc(S("flT"), 1)
            pe.wait_ge(S("ef_sb"), 2)
            for g in range(len(Q_AFTER), NG):
                q_group(g)
            pe.wait_ge(S("ef_sb"), 8)
            pe.wait_ge(S("q_sb"), NG)

            def edge_terms(g, gg):
                pe.wait_ge(S("tanh"), g + 1)
                pe.matmul(bank(6)[0:H2, :], Wm[:, :, :].rearrange("p l h -> p (l h)"), tw[gg % 2], start=True, stop=True).then_inc(S("m3"), 1)

            def walk1(i, first):
                for gg in range(2 * GPS):
                    h, g = gg // GPS, 2 * GPS * i + gg
                    if gg % GPS == 0:
                        pe.wait_ge(S(f"got{h}"), (i + 1) * 16 * SUP)
                        pe.wait_ge(S(f"rate_in{h}"), 16 * (i + 1))
                    if gg % 2 == 0:
                        _, w = nc.values_load_multi_w_load_instructions(
                            d0[0:1, ds(g * TPR, 2 * TPR)], engines=[mybir.EngineType.PE], min_val=0, max_val=NW,
                            skip_runtime_bounds_check_because="destinations are nodes")
                    if not (first and gg < 2):
                        pe.wait_ge(S("kT_sb"), g - 1)
                    for j in range(TPR):
                        t = pe.transpose(bank(gg % 2)[:, j * P:(j + 1) * P],
                                         kv_buf[h][:, gg % GPS * TPR + j, 0:P], ident[:, :])
                    t.then_inc(S("kT"), 1)
                    if not (first and gg < 1):
                        pe.wait_ge(S("relu"), g)
                    pe.matmul(bank(4), lhs2[:, :], rateb[h][:, gg % GPS * ROW:(gg % GPS + 1) * ROW], start=True, stop=True).then_inc(S("m1"), 1)
                    if not (first and gg < 1):
                        if not (first and gg < 2):
                            pe.wait_ge(S("ae"), g - 1)
                        edge_terms(g - 1, gg + 1)
                    pe.wait_ge(S("kT_sb"), g + 1)
                    if not (first and gg < 2):
                        pe.wait_ge(S("score"), g - 1)
                    for j in range(TPR):
                        mm = pe.matmul(bank(2 + gg % 2)[:, j * P:(j + 1) * P], kTb[gg % 2][:, j * P:(j + 1) * P],
                                       QT[:, ds(w[gg % 2 * TPR + j], P)], start=True, stop=True)
                    mm.then_inc(S("kq"), 1)
                    pe.wait_ge(S("relu"), g + 1)
                    if not (first and gg < 1):
                        pe.wait_ge(S("tanh"), g)
                    pe.matmul(bank(5), taw2[:, :], hid[gg % 2], start=True, stop=True).then_inc(S("m2"), 1)
                    pe.wait_ge(S("oh"), g + 1)
                    for j in range(TPR):
                        mm = pe.matmul(bank(7)[:, 0:NB], oh16[gg % 2][:, j * P:(j + 1) * P], ohh[gg % 2][:, j, :],
                                       start=(first and gg == 0 and j == 0), stop=False, skip_group_check=True)
                    mm.then_inc(S("hist"), 1)

            pe.wait_ge(S("d0_in"), 16)
            pe.wait_ge(S("qtpad"), 1)
            pe.wait_ge(S("Wm"), 1)
            walk1(0, True)
            with pe.Fori(1, NSUP // 2) as i:
                walk1(i, False)
            pe.wait_ge(S("ae"), Q - 1)
            edge_terms(Q - 1, 1)

            pe.wait_ge(S("deg"), 1)
            pe.wait_ge(S("ae"), Q)
            pe.matmul(bank(6)[:, 0:NB], tri[:, :], deg[:, :], start=True, stop=True)
            pe.matmul(bank(6)[:, 32:32 + NB], ones[:, :], deg[:, :], start=True, stop=True).then_inc(S("cum"), 1)

            pe.wait_ge(S("score"), Q)
            for k in range(TPR):
                t = pe.transpose(bank(0)[0:Q, k * P:(k + 1) * P], sc[:, k:T:TPR], ident[:, :])
            t.then_inc(S("scT"), 1)
            carried(0, 1, scan_tile(1)[:, 0:1, :], False)
            carried(1, 1, scan_tile(2)[:, 0:1, :], True)
            carried(2, 1, scan_tile(1)[:, 0:1, :], False)
            carried(3, 1, scan_tile(2)[:, 0:1, :], True)
            pe.wait_ge(S("attn"), 1)
            for k in range(TPR):
                t = pe.transpose(bank(0)[:, k * Q:(k + 1) * Q], scan_tile(0)[:, 0, k * P:(k + 1) * P], ident[0:Q, 0:Q])
            t.then_inc(S("wb"), 1)

            def blocks(t):
                return nc.values_load_multi_w_load_instructions(
                    b0[0:1, ds(t, 8)], engines=[mybir.EngineType.PE], min_val=0, max_val=NB - 1,
                    skip_runtime_bounds_check_because="destinations are nodes")[1]

            def sum_tile(block, onehot, row):
                for half in range(2):
                    mm = pe.matmul(acc[:, ds(block * P + half * P, P)], onehot[:, half * P:(half + 1) * P], row,
                                   start=False, stop=True, skip_group_check=True)
                return mm

            pe.wait_ge(S("b0"), 1)
            pe.wait_ge(S("cleared"), 1)

            def walk2(s, k, round_):
                pe.wait_ge(S(f"v_in{k}"), 16 * round_)
                pe.wait_ge(S("sel"), s + 1)
                pe.wait_ge(S("sel_act"), s + 1)
                for j in range(SUP):
                    if j % 8 == 0:
                        w = blocks(s * SUP + j)
                    mm = pe.matmul(acc[:, ds(w[j % 8] * P, P)], onehots[k][:, j * P:(j + 1) * P], v_buf[k][:, j, :],
                                   start=False, stop=True, skip_group_check=True)
                mm.then_inc(S("sum"), 1)

            for s in range(6):
                if s == 3:
                    carried(4, H2, scan_tile(2, 2), False)
                walk2(s, s % 4, 1 + s // 4)
            with pe.Fori(0, (NSUP - 6) // 4) as i:
                for u in range(4):
                    walk2(4 * i + (6 + u), (6 + u) % 4, i + (1 + (6 + u) // 4))
            pe.wait_ge(S("over"), 1)
            pe.wait_ge(S("v_over"), 16 * (NB - 1))
            for b in range(NB - 1):
                mm = pe.matmul(acc[:, (b + 1) * P:(b + 2) * P], over[:, b, :], kv_over[:, b, P:KV], start=False, stop=True, skip_group_check=True)
            mm.then_inc(S("sum"), 1)

            turn(1, NG, lambda b: nodes[1][:, b, :])
            pe.wait_ge(S("tr_sb"), 2 * NG)
            pe.wait_ge(S("ip_in"), 16 * 6)
            for g in range(-(-NB // 2)):
                if g >= 2:
                    pe.wait_ge(S("z_sb"), g - 1)
                for j in range(min(2, NB - 2 * g)):
                    b = 2 * g + j
                    mm = pe.matmul(bank(2 + g % 2)[:, j * KV:(j + 1) * KV], hT[:, b * P:(b + 1) * P], ipw1, start=True, stop=True)
                mm.then_inc(S("z"), 1)
            turn(2, 2 * NG, lambda b: zt[:, b, 0:P])
            turn(3, 2 * NG, lambda b: zt[:, b, P:KV])
            pe.wait_ge(S("tr_sb"), 4 * NG)
            for g in range(NG):
                if g >= 2:
                    pe.wait_ge(S("y_sb"), g - 1)
                for j in range(min(4, NB - 4 * g)):
                    b = 4 * g + j
                    for a in range(2):
                        mm = pe.matmul(bank(2 + g % 2)[:, j * P:(j + 1) * P], zT[a][:, b * P:(b + 1) * P], ipw2[:, a, :],
                                       start=(a == 0), stop=(a == 1))
                mm.then_inc(S("y"), 1)

            for l in range(2):
                pe.wait_ge(S("Wx"), l + 1)
                q = 0
                for g in range(NG + 1):
                    if g < NG:
                        turn(4 + l, (3 + l) * NG, lambda b: nodes[0][:, b, :], [g])
                    while q < NGG and min(3 * q + 2, NB - 1) // 4 < g:
                        k = l * NGG + q
                        pe.wait_ge(S("tr_sb"), (4 + l) * NG + min(3 * q + 2, NB - 1) // 4 + 1)
                        if k >= 2:
                            pe.wait_ge(S("hw"), k - 1)
                        for j in range(min(3, NB - 3 * q)):
                            b = 3 * q + j
                            mm = pe.matmul(bank(2 + k % 2)[:, j * (P + H2):(j + 1) * (P + H2)], hT[:, b * P:(b + 1) * P], Wx[:, :],
                                           start=True, stop=True)
                        mm.then_inc(S("hwp"), 1)
                        q += 1
                pe.wait_ge(S("A3"), l + 1)

                def sources(i, first):
                    for h in range(2):
                        u = 2 * i + h
                        pe.wait_ge(S("lo_oh"), u + (l * UNITS + 1))
                        if not first:
                            pe.wait_ge(S("prod"), u + (l * UNITS - 1))
                        for j in range(UNIT):
                            for m in range(3):
                                mm = pe.matmul(bank(2 * h + j // TPR)[:, j % TPR * NB * H:(j % TPR + 1) * NB * H],
                                               oh16[h][:, j * P:(j + 1) * P], A3[:, m, :], start=(m == 0), stop=(m == 2))
                        mm.then_inc(S("apre"), 1)

                sources(0, True)
                with pe.Fori(1, UNITS // 2) as i:
                    sources(i, False)
                carried(5 + 4 * l, H2, scan_tile(0, 2), False)
                pe.wait_ge(S("asel"), (l + 1) * UNITS)
                for h in range(H):
                    for k in range(TPR):
                        t = pe.transpose(bank(h)[0:Q, k * P:(k + 1) * P], aT[:, k:T:TPR, h], ident[:, :])
                    t.then_inc(S("xT"), 1)
                carried(6 + 4 * l, H, scan_tile(0), False)
                carried(7 + 4 * l, H, scan_tile(3), True)
                pe.wait_ge(S("exp"), 2 + 2 * l)
                for h in range(H):
                    for k in range(TPR):
                        t = pe.transpose(bank(h)[:, k * Q:(k + 1) * Q], scan_tile(2)[:, h, k * P:(k + 1) * P], ident[0:Q, 0:Q])
                    t.then_inc(S("wb"), 1)
                carried(8 + 4 * l, H, scan_tile(0), False)
                pe.wait_ge(S("cleared"), l + 2)
                with pe.Fori(0, 2) as half:
                    for s in range(RS):
                        pe.wait_ge(S("msg"), half * RS + (l * NSUP + s + 1))
                        for pr in range(PPS):
                            n = (half * RS + s) * PPS + pr
                            if pr % 4 == 0:
                                w = blocks(half * (RS * SUP) + (s * SUP + pr * 2))
                            pe.wait_ge(S("sel"), n + (NSUP + l * PAIRS + 1))
                            for j in range(2):
                                mm = sum_tile(w[pr % 4 * 2 + j], wk2[pr % 2][:, j * 2 * P:(j + 1) * 2 * P], rows[:, s, pr * 2 + j, :])
                            mm.then_inc(S("sum"), 1)

        @block.vector
        def _(v):
            c = Chain(v, S("dve"))
            carries = [0]
            roots = [0]

            def step(instruction):
                c.did(instruction)
                c.wait()

            def carry_over(n, tile, masks, row_masks, start, ops, back):
                k = carries[0]
                carries[0] += 1
                end = Q if back else 0
                c.did(v.memset(carry[0:n, end:end + 1], start))
                v.wait_ge(S("carT"), k + 1)
                run, came = carry[0:n, 1 - back:Q + 1 - back], bank(7)[0:n, 0:Q]
                if back:
                    v.tensor_tensor_scan(run[:, ::-1], row_masks[:, ::-1], came[:, ::-1], start, *ops).then_inc(S("carS"), 1)
                else:
                    v.tensor_tensor_scan(run, row_masks, came, start, *ops).then_inc(S("carS"), 1)
                v.wait_ge(S("carB"), k + 1)
                for h in range(n):
                    c.did(v.scalar_tensor_tensor(tile[:, h, :], masks, bank(7)[0:Q, P + h:P + h + 1], tile[:, h, :], *ops))
                c.wait()

            def attend(l):
                v.wait_ge(S("gw_in"), 48 * (l + 1))
                att = wk[:, 0:2 * P].rearrange("p (a f) -> p a f", a=2)
                step(v.tensor_tensor(att, att, bc(Wx[:, 0:P], 1, [P, 2, P]), ALU.mult))
                v.tensor_reduce(Wx[:, P:P + H2].rearrange("p (a h) -> p a h", a=2), att.rearrange("p a (h c) -> p a h c", c=C),
                                AX.X, ALU.add).then_inc(S("Wx"), 1)

            def borders(b):
                return nc.values_load_multi_w_load_instructions(
                    border[0:1, b:b + 8], engines=[mybir.EngineType.DVE], min_val=0, max_val=T - 1,
                    skip_runtime_bounds_check_because="edges lie in tiles")[1]

            def scans(n, tile, masks, data, start, ops, back=False):
                for h in range(n):
                    o, m, x = tile[:, h, :], masks, data(h)
                    if back:
                        o, m, x = o[:, ::-1], m[:, ::-1], x[:, ::-1]
                    s = v.tensor_tensor_scan(o, m, x, start, *ops)
                    if h == n - 1:
                        s.then_inc(S("local"), 1)
                    else:
                        c.did(s)

            SUM, MAX = (ALU.mult, ALU.add), (ALU.add, ALU.max)

            def running_sum(n, tile, data):
                scans(n, tile, cont[:, :], data, 0.0, SUM)
                carry_over(n, tile, pre[:, :], rowf[0:n, 0, :], 0.0, SUM, False)

            def running_max(n, tile, data):
                scans(n, tile, pen[:, :], data, -BIG, MAX)
                carry_over(n, tile, prepen[:, :], rowf[0:n, 1, :], -BIG, MAX, False)

            def from_ends(n, tile, data):
                for h in range(n):
                    c.did(v.scalar_tensor_tensor(tile[:, h, :], contn[:, :], 1.0, data(h), ALU.is_lt, ALU.mult))
                c.wait()
                scans(n, tile, contn[:, :], lambda h: tile[:, h, :], 0.0, SUM, True)
                carry_over(n, tile, post[:, :], rowf[0:n, 2, :], 0.0, SUM, True)

            def group(g):
                return range(4 * g, min(4 * g + 4, NB))

            def moments(X):
                for b in range(NB):
                    c.did(v.bn_stats(stats[:, b, :], X[:, b, :]))
                c.wait()
                scales()

            def scales():
                k = roots[0]
                roots[0] += 1
                for b in range(NB):
                    c.did(v.bn_aggr(mv[:, b, :], stats[:, b, :]))
                c.wait()
                v.tensor_scalar(rstd[:, :], mv[:, :, 1], EPS, None, ALU.add).then_inc(S("var"), 1)
                v.wait_ge(S("std"), k + 1)
                step(v.reciprocal(rstd[:, :], rstd[:, :]))

            def normed(X, Y, b):
                return v.tensor_scalar(Y[:, b, :], X[:, b, :], mv[:, b, 0:1], rstd[:, b:b + 1], ALU.subtract, ALU.mult)

            def norm_relu(X, Y):
                moments(X)
                at = []
                for g in range(NG + 1):
                    if g < NG:
                        for b in group(g):
                            c.did(normed(X, Y, b))
                        at.append(c.n)
                    if g > 0:
                        y = Y[:, 4 * g - 4:min(4 * g, NB), :]
                        c.wait(at[g - 1])
                        v.tensor_scalar(y, y, 0.0, None, ALU.max).then_inc(S("tsrc"), 1)

            def norm_affine(X, Y, w, bias, g, ats):
                if g < NG:
                    for b in group(g):
                        c.did(v.scalar_tensor_tensor(Y[:, b, :], X[:, b, :], mv[:, b, 0:1], w, ALU.subtract, ALU.mult))
                    ats[0].append(c.n)
                if 0 < g <= NG:
                    c.wait(ats[0][g - 1])
                    for b in group(g - 1):
                        c.did(v.scalar_tensor_tensor(Y[:, b, :], Y[:, b, :], rstd[:, b:b + 1], bias, ALU.mult, ALU.add))
                    ats[1].append(c.n)

            def fl(t):
                return t.rearrange("p b f -> p (b f)")

            v.wait_ge(S("x_in"), 32)
            norm_relu(nodes[0], nodes[1])

            v.wait_ge(S("w_in"), 16 * 21)
            ab = wk[:, 0:2 * P].rearrange("p (a f) -> p a f", a=2)
            pr = wk[:, 2 * P:5 * P].rearrange("p (a f) -> p a f", a=3)
            step(v.tensor_reduce(smal[:, 0:2], ab, AX.X, ALU.add))
            step(v.tensor_scalar(smal[:, 0:2], smal[:, 0:2], 1.0 / P, None, ALU.mult))
            for i in range(2):
                c.did(v.tensor_scalar(ab[:, i, :], ab[:, i, :], smal[:, i:i + 1], None, ALU.subtract))
            c.wait()
            c.did(v.tensor_tensor(pr[:, 0, :], ab[:, 0, :], ab[:, 0, :], ALU.mult))
            c.did(v.tensor_tensor(pr[:, 1, :], ab[:, 0, :], ab[:, 1, :], ALU.mult))
            c.did(v.tensor_tensor(pr[:, 2, :], ab[:, 1, :], ab[:, 1, :], ALU.mult))
            c.wait()
            step(v.tensor_reduce(smal[:, 2:5], pr, AX.X, ALU.add))
            c.did(v.tensor_scalar(smal[:, 2:5], smal[:, 2:5], 1.0 / P, None, ALU.mult))
            c.wait()
            step(v.tensor_scalar(smal[:, 3:4], smal[:, 3:4], 2.0, None, ALU.mult))
            step(v.tensor_reduce(lhm[:, :], lhs2[:, :], AX.X, ALU.add))
            step(v.tensor_scalar(lhm[:, :], lhm[:, :], 1.0 / P, None, ALU.mult))
            step(v.tensor_scalar(lhs2[:, :], lhs2[:, :], lhm[:, 0:1], None, ALU.subtract))
            step(v.tensor_tensor(lhs2[:, :], lhs2[:, :], lnwb[:, :], ALU.mult))
            tw4 = tmpw[:, 0:4 * P].rearrange("p (a f) -> p a f", a=4)
            step(v.tensor_tensor(tw4[:, 0:2, :], tw4[:, 0:2, :], tw4[:, 2:4, :], ALU.mult))
            v.tensor_reduce(Wm[:, :, :], tw4[:, 0:2, :].rearrange("p a (h c) -> p a h c", c=C), AX.X, ALU.add).then_inc(S("Wm"), 1)
            for t in range(ET):
                i = v.tensor_scalar(wedge[:, t * P:(t + 1) * P], wedge[:, t * P:(t + 1) * P], smal[:, 8 + t:9 + t], P ** -0.5, ALU.mult, ALU.mult)
                if t == ET - 1:
                    i.then_inc(S("we"), 1)
                else:
                    c.did(i)
            v.memset(QT[:, NW:NWP], 0.0).then_inc(S("qtpad"), 1)
            if NW > N:
                for t in range(NT):
                    c.did(v.memset(hTt[t][:, N:NW], 0.0))
            v.wait_ge(S("nt_in"), 16)
            ntb = fl(nodes[2]).bitcast(I32)
            v.wait_ge(S("tr_sb"), NG)
            for lo, hi in ((0, HALF), (HALF, N)):
                for t in range(NT):
                    v.scalar_tensor_tensor(hTt[t][:, lo:hi], ntb[:, lo:hi], float(t), KT[:, lo:hi], ALU.is_equal, ALU.mult).then_inc(S("hTt"), 1)
            v.wait_ge(S("hTt"), 2 * NT)

            v.wait_ge(S("e_in"), 16 * N_E_IN)
            D, DP, DN, SR, TY, EW = [eraw[:, i, :] if i == 5 else eraw[:, i, :].bitcast(I32) for i in range(6)]
            Ei = [ef[:, i, :].bitcast(I32) for i in range(10)]
            c.did(v.memset(ef[:, 9, :], 0.0))
            c.did(v.tensor_tensor(cont[:, :], D, DP, ALU.is_equal))
            c.did(v.tensor_tensor(contn[:, :], D, DN, ALU.is_equal))
            c.did(v.tensor_copy(ef[:, 0, :], D))
            c.did(v.tensor_copy(ef[:, 1, :], SR))
            c.did(v.tensor_scalar(Ei[8], D, 7, None, ALU.arith_shift_right))
            c.did(v.tensor_scalar(Ei[7], SR, 7, None, ALU.arith_shift_right))
            c.did(v.scalar_tensor_tensor(ef[:, 4, :], SR, float(ET), TY, ALU.mult, ALU.add))
            c.wait()
            c.did(v.tensor_tensor_scan(pre[:, :], cont[:, :], ef[:, 9, :], 1.0, *SUM))
            c.did(v.tensor_tensor_scan(post[:, ::-1], contn[:, ::-1], ef[:, 9, :], 1.0, *SUM))
            c.did(v.tensor_copy(ef[:, 2, :], Ei[8]))
            c.did(v.tensor_copy(ef[:, 3, :], Ei[7]))
            c.wait()
            c.did(v.scalar_tensor_tensor(ef[:, 5, :], ef[:, 2, :], -float(P), ef[:, 0, :], ALU.mult, ALU.add))
            c.did(v.scalar_tensor_tensor(ef[:, 6, :], ef[:, 3, :], -float(P), ef[:, 1, :], ALU.mult, ALU.add))
            step(v.tensor_scalar(blk[:, :], ef[:, 2, 0:ROW:P], float(P), None, ALU.mult))
            for k in range(TPR):
                c.did(v.tensor_scalar(ef[:, 9, k * P:(k + 1) * P], ef[:, 0, k * P:(k + 1) * P], blk[:, k:k + 1], None, ALU.subtract))
            for k in range(TPR):
                i = v.tensor_scalar(ef[:, 7, k * P:(k + 1) * P], ef[:, 0, k * P:(k + 1) * P], ef[:, 0, k * P:k * P + 1], None, ALU.subtract)
                if k == TPR - 1:
                    i.then_inc(S("ef"), 1)
                else:
                    c.did(i)
            c.wait()
            v.tensor_copy(ef[:, 8, 0:ROW // 2].bitcast(BF16), ef[:, 6, :]).then_inc(S("lo_ready"), 1)
            c.did(v.tensor_scalar(pen[:, :], cont[:, :], -1.0, BIG, ALU.add, ALU.mult))
            c.did(v.tensor_scalar(prepen[:, :], pre[:, :], -1.0, BIG, ALU.add, ALU.mult))
            c.wait()
            c.did(v.tensor_copy(flags[:, 0, :], pre[:, ROW - 1:ROW].to_broadcast([Q, H2])))
            c.did(v.tensor_copy(flags[:, 1, :], prepen[:, ROW - 1:ROW].to_broadcast([Q, H2])))
            v.tensor_copy(flags[:, 2, :], post[:, 0:1].to_broadcast([Q, H2])).then_inc(S("flags"), 1)
            va, cab, vb = (smal[0:Q, i:i + 1] for i in (2, 3, 4))
            step(v.tensor_scalar(ef[:, 6, :], EW, va, cab, ALU.mult, ALU.add))
            step(v.tensor_tensor(ef[:, 6, :], ef[:, 6, :], EW, ALU.mult))
            step(v.tensor_scalar(ef[:, 6, :], ef[:, 6, :], vb, 0.0, ALU.add, ALU.max))
            v.tensor_scalar(ef[:, 6, :], ef[:, 6, :], EPS, None, ALU.add).then_inc(S("rvar"), 1)
            v.wait_ge(S("rstd0"), 1)
            step(v.reciprocal(ef[:, 6, :], ef[:, 6, :]))
            v.tensor_tensor(ef[:, 0, :], ef[:, 6, :], EW, ALU.mult).then_inc(S("rate_ready"), 1)

            for b in range(NB):
                v.wait_ge(S("kv"), b + 1)
                if b >= 3:
                    v.wait_ge(S(f"kv_out{b % 3}"), 16 * (b // 3))
                elif b == 2:
                    v.wait_ge(S("rate_ready"), 1)
                v.tensor_copy(stg[b % 3][:, 0:ET // 2, 0:P], bank(2 * (b % 2)).rearrange("p (t f) -> p t f", f=P))
                v.tensor_copy(stg[b % 3][:, :, P:KV], bc(bank(4 + b % 2)[:, 0:P], 1, [P, ET, P])).then_inc(S("kv_dve"), 1)

            for a, t in enumerate((kvT, srcT, relT, loT, hiT, shiT, relbT)):
                v.wait_ge(S("efT"), a + 1)
                v.tensor_copy(t[:, 0:T].rearrange("p (q k) -> p k q", k=TPR), bank(a)[:, 0:T].rearrange("p (k q) -> p k q", k=TPR)).then_inc(S("ef_sb"), 1)
                if a == 0:
                    v.wait_ge(S("ef_sb"), 1)
                    for h in range(2):
                        v.tensor_copy(idx[:, h * SUP:(h + 1) * SUP], kvT[:, h * SUP:(h + 1) * SUP]).then_inc(S("idx"), 1)
            v.wait_ge(S("d0_in"), 16)
            v.tensor_scalar(b0[:, :], d0[:, :], 7, None, ALU.arith_shift_right).then_inc(S("b0"), 1)
            v.wait_ge(S("flT"), 1)
            v.tensor_copy(rowf[:, :, :], bank(7)[0:H2, 0:3 * Q].rearrange("p (a q) -> p a q", a=3)).then_inc(S("ef_sb"), 1)

            v.wait_ge(S("ef_sb"), 8)

            def walk1(i, first):
                for gg in range(2 * GPS):
                    g = 2 * GPS * i + gg
                    if not (first and gg < 2):
                        v.wait_ge(S("hist"), g - 1)
                    v.tensor_tensor(ohh[gg % 2][:, 0:TPR, :], bc(iota16[:, 0:NB], 1, [P, TPR, NB]),
                                    bc(hiT[:, ds(g * TPR, TPR)], 2, [P, TPR, NB]), ALU.is_equal)
                    v.tensor_tensor(oh16[gg % 2][:, 0:ROW].rearrange("p (j f) -> p j f", f=P), bc(iota16[:, :], 1, [P, TPR, P]),
                                    bc(loT[:, ds(g * TPR, TPR)], 2, [P, TPR, P]), ALU.is_equal).then_inc(S("oh"), 1)
                    if not (first and gg < 1):
                        v.wait_ge(S("m3"), g)
                        if gg % GPS == 1 and not (first and gg < GPS):
                            v.wait_ge(S("ae_out"), 16 * (2 * i + gg // GPS))
                        v.tensor_copy(aeb[:, (gg - 1) % GPS * ROW:((gg - 1) % GPS + 1) * ROW], bank(6)[0:H2, :]).then_inc(S("ae"), 1)
                    v.wait_ge(S("kq"), g + 1)
                    if gg % GPS == 0:
                        v.wait_ge(S(f"got{gg // GPS}"), (i + 1) * 16 * SUP)
                        v.tensor_copy(idx[:, gg // GPS * SUP:(gg // GPS + 1) * SUP],
                                      kvT[:, ds((2 * i + gg // GPS + 2) * SUP, SUP)]).then_inc(S("idx"), 1)
                    for j in range(TPR):
                        G = bank(2 + gg % 2)[:, j * P:(j + 1) * P]
                        s = v.scalar_tensor_tensor(G, iota[:, 0:P], relT[:, ds(g * TPR + j, 1)], G, ALU.is_equal, ALU.mult,
                                                   accum_out=sc[:, ds(g * TPR + j, 1)])
                    s.then_inc(S("score"), 1)

            walk1(0, True)
            with v.Fori(1, NSUP // 2) as i:
                walk1(i, False)
            v.wait_ge(S("m3"), Q)
            v.tensor_copy(aeb[:, (GPS - 1) * ROW:GPS * ROW], bank(6)[0:H2, :]).then_inc(S("ae"), 1)

            v.wait_ge(S("hist"), Q)
            v.tensor_copy(deg[:, :], bank(7)[:, 0:NB]).then_inc(S("deg"), 1)
            v.wait_ge(S("cum"), 1)
            step(v.tensor_tensor_scan(nb_[:, :], ones[:, 0:NB], bank(6)[:, 32:32 + NB], 0.0, *SUM))
            step(v.tensor_tensor(nb_[:, :], nb_[:, :], bank(6)[:, 32:32 + NB], ALU.subtract))
            step(v.tensor_tensor(nb_[:, :], nb_[:, :], bank(6)[:, 0:NB], ALU.add))
            v.tensor_scalar(endi[:, :], nb_[:, :], -1.0, None, ALU.add).then_inc(S("endi"), 1)
            v.tensor_tensor(starti[:, :], nb_[:, :], deg[:, :], ALU.subtract).then_inc(S("endi"), 1)
            v.wait_ge(S("endi"), 2)
            v.tensor_scalar(border[:, :], starti[0:1, 1:NB], 7, None, ALU.arith_shift_right).then_inc(S("border"), 1)
            v.wait_ge(S("border"), 1)
            for h in range(2):
                v.wait_ge(S(f"got{h}"), NSUP // 2 * 16 * SUP)
            for b in range(0, NB - 1, 8):
                t = borders(b)
                for k in range(8):
                    i = v.tensor_copy(idx[:, b + k:b + k + 1], kvT[:, ds(t[k], 1)])
                    if b + k < NB - 2:
                        c.did(i)
            i.then_inc(S("border_idx"), 1)

            X, M, Z = (scan_tile(i)[:, 0:1, :] for i in range(3))
            v.wait_ge(S("scT"), 1)
            step(v.tensor_copy(X[:, 0, :], bank(0)[0:Q, :]))
            running_max(1, M, lambda h: X[:, 0, :])
            step(v.tensor_scalar(M[:, 0, :], M[:, 0, :], -1e9, None, ALU.max))
            from_ends(1, Z, lambda h: M[:, 0, :])
            v.tensor_tensor(X[:, 0, :], X[:, 0, :], Z[:, 0, :], ALU.subtract).then_inc(S("xm"), 1)
            v.wait_ge(S("exp"), 1)
            running_sum(1, M, lambda h: X[:, 0, :])
            from_ends(1, Z, lambda h: M[:, 0, :])
            step(v.tensor_scalar(Z[:, 0, :], Z[:, 0, :], 1e-10, None, ALU.add))
            step(v.reciprocal(Z[:, 0, :], Z[:, 0, :]))
            v.tensor_tensor(X[:, 0, :], X[:, 0, :], Z[:, 0, :], ALU.mult).then_inc(S("attn"), 1)
            v.wait_ge(S("wb"), 1)
            v.tensor_copy(sc[:, :].rearrange("p (q k) -> p k q", k=TPR), bank(0)[:, 0:T].rearrange("p (k q) -> p k q", k=TPR)).then_inc(S("sm0"), 1)

            v.wait_ge(S("sm0"), 1)
            v.tensor_scalar(nsc[:, :], sc[:, :], -1.0, None, ALU.mult).then_inc(S("nsc"), 1)
            v.memset(acc, 0.0).then_inc(S("cleared"), 1)

            def walk2(s, h):
                if not isinstance(s, int) or s >= 4:
                    v.wait_ge(S("sum"), s - 3)
                for j in OF_DVE:
                    t = s * SUP + j
                    o = v.tensor_scalar(onehots[h][:, j * P:(j + 1) * P], iota[:, 0:P], relbT[:, ds(t, 1)],
                                        sc[:, ds(t, 1)], ALU.is_equal, ALU.mult)
                o.then_inc(S("sel"), 1)

            for s in range(3):
                walk2(s, s)
            v.wait_ge(S("ae_in"), 16)
            scans(H2, scan_tile(2, 2), cont[:, :], lambda h: scan_tile(0, 2)[:, h, :], 0.0, SUM)
            walk2(3, 3)
            carry_over(H2, scan_tile(2, 2), pre[:, :], rowf[0:H2, 0, :], 0.0, SUM, False)
            walk2(4, 0)
            v.tensor_copy(scan_tile(0, 2).rearrange("p h c -> p (h c)").rearrange("p (c h) -> p h c", h=H2),
                          scan_tile(2, 2)).then_inc(S("mae1"), 1)
            walk2(5, 1)
            for b in range(0, NB - 1, 8):
                t = borders(b)
                for k in range(8):
                    o = v.tensor_scalar(over[:, b + k, :], iota[:, P:2 * P], relbT[:, ds(t[k], 1)], sc[:, ds(t[k], 1)], ALU.is_equal, ALU.mult)
            o.then_inc(S("over"), 1)
            with v.Fori(0, (NSUP - 6) // 4) as i:
                for u in range(4):
                    walk2(4 * i + (6 + u), (6 + u) % 4)

            v.wait_ge(S("x_in"), 64)
            v.wait_ge(S("sum"), NSUP + 1)
            v.tensor_tensor(fl(nodes[0]), fl(nodes[0]), acc[:, 0:NW], ALU.add).then_inc(S("x1"), 1)
            v.wait_ge(S("x1"), 1)

            v.wait_ge(S("sums_in"), 16 * NB)
            step(v.tensor_scalar(nb_[:, :], deg[:, :], 1.0, None, ALU.max))
            step(v.reciprocal(nb_[:, :], nb_[:, :]))
            step(v.tensor_tensor(mae[:, :, :], ncol[:, :, :], bc(nb_[:, :], 2, [P, NB, H2]), ALU.mult))

            norm_relu(nodes[0], nodes[1])
            v.wait_ge(S("ip_in"), 16 * 6)
            b1 = ipv[:, 0:KV]
            b2, pw, pb = (ipv[:, KV + i * P:KV + (i + 1) * P] for i in range(3))
            NZ = -(-NB // 2)
            for g in range(NZ + 2):
                if g < NZ:
                    n = min(2, NB - 2 * g)
                    v.wait_ge(S("z"), g + 1)
                    v.tensor_tensor(zt[:, 2 * g:2 * g + n, :], bank(2 + g % 2)[:, 0:n * KV].rearrange("p (b f) -> p b f", f=KV),
                                    bc(b1, 1, [P, n, KV]), ALU.add).then_inc(S("z_sb"), 1)
                if g >= 2:
                    v.wait_ge(S("z_relu"), g - 1)
                    for b in range(2 * g - 4, min(2 * g - 2, NB)):
                        c.did(v.bn_stats(stats[:, b, :], zt[:, b, :]))
            c.wait()
            scales()
            for g in range(NG):
                for b in group(g):
                    i = normed(zt, zt, b)
                    if b < group(g)[-1]:
                        c.did(i)
                i.then_inc(S("tsrc"), 1)
            for g in range(NG + 1):
                if g < NG:
                    n = min(4, NB - 4 * g)
                    v.wait_ge(S("y"), g + 1)
                    v.tensor_tensor(nodes[1][:, 4 * g:4 * g + n, :], bank(2 + g % 2)[:, 0:n * P].rearrange("p (b f) -> p b f", f=P),
                                    bc(b2, 1, [P, n, P]), ALU.add).then_inc(S("y_sb"), 1)
                if g > 0:
                    v.wait_ge(S("y_sb"), g)
                    for b in group(g - 1):
                        c.did(v.bn_stats(stats[:, b, :], nodes[1][:, b, :]))
            c.wait()
            scales()
            v.wait_ge(S("x1_out"), 16)
            attend(0)
            ats = [], []
            for g in range(NG + 2):
                norm_affine(nodes[1], nodes[0], pw, pb, g, ats)
                if g > 1:
                    y = nodes[0][:, 4 * g - 8:min(4 * g - 4, NB), :]
                    c.wait(ats[1][g - 2])
                    v.tensor_scalar(y, y, 0.0, 10.0, ALU.max, ALU.min).then_inc(S("tsrc"), 1)

            for l in range(2):
                for g in range(NGG):
                    n = min(3, NB - 3 * g)
                    v.wait_ge(S("hwp"), l * NGG + g + 1)
                    got = bank(2 + (l * NGG + g) % 2)[:, 0:n * (P + H2)].rearrange("p (b f) -> p b f", f=P + H2)
                    c.did(v.tensor_copy(ncol[:, 3 * g:3 * g + n, :], got[:, :, P:P + H2]))
                    v.tensor_copy(nodes[1][:, 3 * g:3 * g + n, :], got[:, :, 0:P]).then_inc(S("hw"), 1)
                c.wait()
                v.tensor_copy(nst[:, :, 0:H], ncol[:, :, H:H2]).then_inc(S("nst"), 1)
                a3 = a3r[:, :].rearrange("p (b h) -> p b h", h=H)
                step(v.tensor_tensor(a3, ncol[:, :, 0:H], ncol[:, :, H:H2], ALU.add))
                step(v.tensor_tensor(a3, a3, mae[:, :, l * H:(l + 1) * H], ALU.add))
                v.scalar_tensor_tensor(nst[:, :, H:H2], a3, 0.2, a3, ALU.mult, ALU.max).then_inc(S("nst"), 1)
                v.wait_ge(S("nst"), 2 * (l + 1))
                step(v.tensor_copy(a3, ncol[:, :, 0:H]))
                for m in range(2):
                    step(v.tensor_copy(A3[:, m, :], a3r[:, :]))
                    step(v.tensor_tensor(a3r[:, :], a3r[:, :], A3[:, m, :], ALU.subtract))
                v.tensor_copy(A3[:, 2, :], a3r[:, :]).then_inc(S("A3"), 1)

                def select(u, h):
                    v.wait_ge(S("prod"), u + (l * UNITS + 1))
                    prod = wk[:, 0:UNIT * NB * H].rearrange("p (j b h) -> p j h b", b=NB, h=H)
                    v.tensor_reduce(aT[:, ds(u * UNIT, UNIT), 0:H], prod, AX.X, ALU.add).then_inc(S("asel"), 1)

                def sources(i, first):
                    for h in range(2):
                        u = 2 * i + h
                        if not first:
                            v.wait_ge(S("prod"), u + (l * UNITS - 1))
                        v.tensor_tensor(ohh[h][:, :, :], bc(iota16[:, 0:NB], 1, [P, UNIT, NB]),
                                        bc(shiT[:, ds(u * UNIT, UNIT)], 2, [P, UNIT, NB]), ALU.is_equal).then_inc(S("hi_oh"), 1)
                        if not (first and h == 0):
                            select(u - 1, 1 - h)
                            v.wait_ge(S("asel"), u + l * UNITS)
                        v.wait_ge(S("hi_oh"), u + (l * UNITS + 1))
                        v.wait_ge(S("apre"), u + (l * UNITS + 1))
                        for a in range(2):
                            i_ = v.tensor_tensor(wk[:, a * TPR * NB * H:(a + 1) * TPR * NB * H].rearrange("p (j b h) -> p j b h", b=NB, h=H),
                                                 bank(2 * h + a)[:, 0:TPR * NB * H].rearrange("p (j b h) -> p j b h", b=NB, h=H),
                                                 bc(ohh[h][:, a * TPR:(a + 1) * TPR, :], 3, [P, TPR, NB, H]), ALU.mult)
                        i_.then_inc(S("prod"), 1)

                sources(0, True)
                with v.Fori(1, UNITS // 2) as i:
                    sources(i, False)
                select(UNITS - 1, 1)

                v.wait_ge(S("start_in"), 16 * (l + 1))
                V8 = scan_tile(2, 2).rearrange("p h c -> p (h c)").rearrange("p (c h) -> p c h", h=H2)
                AD, L, X, M = (scan_tile(i) for i in range(4))
                running_sum(H2, scan_tile(0, 2), lambda h: V8[:, :, h])
                for h in range(H):
                    v.wait_ge(S("xT"), l * H + h + 1)
                    i = v.tensor_tensor(X[:, h, :], bank(h)[0:Q, :], AD[:, h, :], ALU.add)
                    if h == H - 1:
                        i.then_inc(S("held"), 1)
                    else:
                        c.did(i)
                v.wait_ge(S("held"), l + 1)
                v.wait_ge(S("ael_in"), 16 * (l + 1))
                step(v.tensor_tensor(X, X, M, ALU.add))
                step(v.scalar_tensor_tensor(X, X, 0.2, X, ALU.mult, ALU.max))
                running_max(H, AD, lambda h: X[:, h, :])
                from_ends(H, M, lambda h: AD[:, h, :])
                step(v.tensor_tensor(M, M, L, ALU.max))
                v.tensor_tensor(X, X, M, ALU.subtract).then_inc(S("xm"), 1)
                v.tensor_tensor(L, L, M, ALU.subtract).then_inc(S("elm"), 1)
                v.wait_ge(S("exp"), 2 + 2 * l)
                running_sum(H, AD, lambda h: X[:, h, :])
                for h in range(H):
                    v.wait_ge(S("wb"), 1 + l * H + h + 1)
                    v.tensor_copy(aT[:, :, h].rearrange("p (q k) -> p k q", k=TPR),
                                  bank(h)[:, 0:T].rearrange("p (k q) -> p k q", k=TPR)).then_inc(S("wT"), 1)
                v.wait_ge(S("wT"), H * (l + 1))
                v.memset(acc, 0.0).then_inc(S("cleared"), 1)
                v.wait_ge(S("exp"), 3 + 2 * l)
                ends = scan_tile(2, 2).rearrange("p h c -> p (h c)").rearrange("p (c h) -> p h c", h=H2)
                c.did(v.tensor_copy(ends[:, 0:H, :], AD))
                v.tensor_copy(ends[:, H:H2, :], L).then_inc(S("el"), 1)

                with v.Fori(0, 2) as half:
                    for s in range(RS):
                        v.wait_ge(S(f"row{s}"), (half + 2 * l + 1) * 16 * SUP)
                        r = rows[:, s, :, :].rearrange("p j (h c) -> p j h c", c=C)
                        v.tensor_tensor(r, r, bc(aT[:, ds(half * (RS * SUP) + s * SUP, SUP), 0:H], 3, [P, SUP, H, C]), ALU.mult).then_inc(S("msg"), 1)
                        for pr in range(PPS):
                            v.wait_ge(S("sum"), (half * RS + s) * PPS + (NSUP + l * PAIRS + pr))
                            for j in range(2):
                                i = v.tensor_scalar(wk2[pr % 2][:, j * 2 * P:(j + 1) * 2 * P], iota[:, :],
                                                    relbT[:, ds(half * (RS * SUP) + (s * SUP + pr * 2 + j), 1)], None, ALU.is_equal)
                            i.then_inc(S("sel"), 1)

                bias, nw, nb = (vec6[:, 3 * l + i, :] for i in range(3))
                v.wait_ge(S("back_in"), 32 * (l + 1))
                c.did(v.tensor_tensor(nodes[0], nodes[0], bc(bias, 1, [P, NB, P]), ALU.add))
                v.wait_ge(S("al0"), l + 1)
                v.wait_ge(S("al_in"), 16 * NB * (l + 1))
                share, loop = al[:, :, 0:H], al[:, :, H:H2]
                r, m = fl(nodes[1]).rearrange("p (b h c) -> p b h c", h=H, c=C), fl(nodes[1])
                c.did(v.tensor_tensor(r, r, bc(loop, 3, [P, NB, H, C]), ALU.mult))
                step(v.tensor_tensor(share, share, loop, ALU.add))
                step(v.tensor_scalar(share, share, 1e-16, None, ALU.add))
                step(v.reciprocal(share, share))
                v.wait_ge(S("sum"), NSUP + 1 + (1 + l) * PAIRS)
                step(v.tensor_tensor(m, m, acc[:, 0:NW], ALU.add))
                step(v.tensor_tensor(r, r, bc(share, 3, [P, NB, H, C]), ALU.mult))
                v.tensor_tensor(nodes[0], nodes[0], nodes[1], ALU.add).then_inc(S("x1"), 1)
                v.wait_ge(S("x1"), 2 + l)
                step(v.tensor_scalar(fl(nodes[0]), fl(nodes[0]), -10.0, 10.0, ALU.max, ALU.min))
                moments(nodes[0])
                if l == 0:
                    attend(1)
                else:
                    v.wait_ge(S("x1_in"), 16)
                ats = [], [], []
                for g in range(NG + 3 + l):
                    norm_affine(nodes[0], nodes[0], nw, nb, g, ats)
                    if 2 <= g < NG + 2:
                        y, e = (nodes[i][:, 4 * g - 8:min(4 * g - 4, NB), :] for i in (0, 2))
                        c.wait(ats[1][g - 2])
                        v.tensor_scalar(e, y, 0.0, None, ALU.min).then_inc(S("elu"), 1)
                        v.wait_ge(S("elu"), l * NG + g - 1)
                        c.did(v.tensor_scalar(y, y, 0.0, None, ALU.max))
                        ats[2].append(c.n)
                    if 3 <= g < NG + 3:
                        y, e = (nodes[i][:, 4 * g - 12:min(4 * g - 8, NB), :] for i in (0, 2))
                        c.wait(ats[2][g - 3])
                        v.wait_ge(S("elu_e"), l * NG + g - 2)
                        v.scalar_tensor_tensor(y, e, -1.0, y, ALU.add, ALU.add).then_inc(S("elu_y" if l else "tsrc"), 1)
                    if g >= 4 and l == 1:
                        y, e = (nodes[i][:, 4 * g - 16:min(4 * g - 12, NB), :] for i in (0, 1))
                        v.wait_ge(S("elu_y"), g - 3)
                        v.tensor_tensor(y, y, e, ALU.add).then_inc(S("final"), 1)


def kernel(**inputs):
    import numpy as _np
    import concourse.bacc as _bacc
    from concourse import mybir as _mybir
    from concourse.bass_utils import run_bass_kernel_spmd as _run

    nc = _bacc.Bacc("TRN2", target_bir_lowering=False, num_devices=1)
    arrays, aps = {}, {}
    for name, value in inputs.items():
        a = _np.ascontiguousarray(value)
        arrays["in_" + name] = a
        aps[name] = nc.dram_tensor("in_" + name, a.shape, _mybir.dt.from_np(a.dtype), kind="ExternalInput").ap()
    out = nc.dram_tensor("out_x", inputs["x"].shape, _mybir.dt.float32, kind="ExternalOutput").ap()
    build(nc, aps, out)
    r = _run(nc, [arrays], core_ids=[0])
    return r.results[0]["out_x"]
```
